# Optimizing a Trainium2 kernel written in Bass

```python
import numpy as np
import jax
import jax.numpy as jnp

def _softmax(x, axis=-1):
    return jax.nn.softmax(x, axis=axis)

def _gelu(x):
    return jax.nn.gelu(x, approximate=True)

def _silu(x):
    return jax.nn.silu(x)

def _sigmoid(x):
    return jax.nn.sigmoid(x)

def _layernorm(x, axis=-1, eps=1e-05):
    m = jnp.mean(x, axis=axis, keepdims=True)
    v = jnp.var(x, axis=axis, keepdims=True)
    return (x - m) / jnp.sqrt(v + eps)

def _scatter_add(tgt, idx, src, axis=0):
    return tgt.at[idx].add(src)

def _segment_sum(src, seg, n):
    return jax.ops.segment_sum(src, seg, n)
kernel_name = 'mk_xattn_ffn_d2_seqx_r8_36dc61'

def setup_inputs(seed: int=0):
    np.random.seed(seed)
    _w = jnp.asarray

    def _rec_inputs():
        import jax
        import jax.numpy as jnp
        _rk = jax.random.key(seed)
        x = 0.5 + 0.2887 * jax.random.normal(jax.random.fold_in(_rk, 1), (4, 256, 256), jnp.float32)
        _lenS = 256 - jax.random.randint(jax.random.fold_in(_rk, 7), (4,), 0, max(1, 256 // 4) + 1, jnp.int32)
        _lenS2 = 256 - jax.random.randint(jax.random.fold_in(_rk, 8), (4,), 0, max(1, 256 // 4) + 1, jnp.int32)
        _ctx_512P = jax.random.normal(jax.random.fold_in(_rk, 11), (4, 16, 64), jnp.float32)
        _ctx_512c = jax.random.dirichlet(jax.random.fold_in(_rk, 511), 0.3 * jnp.ones((16,), jnp.float32), (4, 256))
        _ctx_512t = jnp.einsum('bsk,bkd->bsd', _ctx_512c, _ctx_512P)
        _ctx_512t = _ctx_512t * jax.lax.rsqrt(jnp.mean(jnp.square(_ctx_512t)) + 1e-12) * 0.953939
        ctx_512 = -0.000392918 + 0.999932 * (_ctx_512t + 0.3 * jax.random.normal(jax.random.fold_in(_rk, 611), (4, 256, 64), jnp.float32))
        return (x, ctx_512)
    x, ctx_512 = _rec_inputs()

    def _L0_xattn_setup():
        import jax, jax.numpy as jnp
        import numpy as np
        B, N, D = (16, 256, 64)
        H = 4
        TOP_K_RATIO = 0.3
        key = jax.random.key(seed)
        k1, k2, k3, k4 = jax.random.split(key, 4)
        h = jax.random.normal(k1, (B, N, D), dtype=jnp.float32)
        adj_raw = jax.random.uniform(k2, (B, N, N), dtype=jnp.float32)
        lim = 1.0 / np.sqrt(D)
        Wq = jax.random.uniform(k3, (D, D), minval=-lim, maxval=lim, dtype=jnp.float32)
        Wk = jax.random.uniform(k4, (D, D), minval=-lim, maxval=lim, dtype=jnp.float32)
        gamma_raw = jnp.float32(-0.85)
        return {'h': h, 'adj_raw': adj_raw, 'Wq': Wq, 'Wk': Wk, 'gamma_raw': gamma_raw}
    _L0_xattn_all = _L0_xattn_setup()
    _L0_xattn_in = {k: v for k, v in _L0_xattn_all.items() if k in ('Wq', 'Wk', 'gamma_raw')}
    del _L0_xattn_all

    def _L0_ffn_setup():
        import jax, jax.numpy as jnp
        import numpy as np
        B, S, D = (2, 256, 256)
        H, KV, HD = (16, 4, 128)
        E, F, TOPK = (8, 512, 2)
        THETA = 1000000.0
        EPS = 1e-05

        def rmsnorm(x, w):
            var = jnp.mean(jnp.square(x), axis=-1, keepdims=True)
            return x * jax.lax.rsqrt(var + EPS) * w

        def rope_cos_sin(seq_len):
            inv_freq = 1.0 / THETA ** (jnp.arange(0, HD, 2, dtype=jnp.float32) / HD)
            ang = jnp.arange(seq_len, dtype=jnp.float32)[:, None] * inv_freq[None, :]
            return (jnp.cos(ang)[None, :, None, :], jnp.sin(ang)[None, :, None, :])

        def apply_rope(x, cos, sin):
            x1, x2 = jnp.split(x, 2, axis=-1)
            return jnp.concatenate([x1 * cos - x2 * sin, x2 * cos + x1 * sin], axis=-1)

        def attention(x, wq, wk, wv, wo):
            b, s, _ = x.shape
            q = (x @ wq).reshape(b, s, H, HD)
            k = (x @ wk).reshape(b, s, KV, HD)
            v = (x @ wv).reshape(b, s, KV, HD)
            cos, sin = rope_cos_sin(s)
            q = apply_rope(q, cos, sin)
            k = apply_rope(k, cos, sin)
            rep = H // KV
            k = jnp.repeat(k, rep, axis=2)
            v = jnp.repeat(v, rep, axis=2)
            scores = jnp.einsum('bqhd,bkhd->bhqk', q, k) / np.sqrt(HD)
            causal = jnp.tril(jnp.ones((s, s), dtype=bool))
            scores = jnp.where(causal[None, None], scores, jnp.finfo(scores.dtype).min)
            probs = jax.nn.softmax(scores, axis=-1)
            out = jnp.einsum('bhqk,bkhd->bqhd', probs, v).reshape(b, s, H * HD)
            return out @ wo

        def moe(x, gate_w, w1, w3, w2):
            b, s, d = x.shape
            xt = x.reshape(b * s, d)
            logits = xt @ gate_w
            topv, topi = jax.lax.top_k(logits, TOPK)
            probs = jax.nn.softmax(topv, axis=-1)
            w = jnp.zeros_like(logits)
            for kk in range(TOPK):
                w = w + jax.nn.one_hot(topi[:, kk], E, dtype=logits.dtype) * probs[:, kk:kk + 1]
            out = jnp.zeros_like(xt)
            for e in range(E):
                h = jax.nn.silu(xt @ w1[e]) * (xt @ w3[e])
                out = out + w[:, e:e + 1] * (h @ w2[e])
            return out.reshape(b, s, d)
        key = jax.random.key(seed)
        ks = jax.random.split(key, 10)
        init = lambda k, shape: jax.random.normal(k, shape, jnp.float32) * 0.02
        return {'hidden_states': jax.random.normal(ks[0], (B, S, D), jnp.float32), 'norm1_w': jnp.ones((D,), jnp.float32), 'norm2_w': jnp.ones((D,), jnp.float32), 'wq': init(ks[1], (D, H * HD)), 'wk': init(ks[2], (D, KV * HD)), 'wv': init(ks[3], (D, KV * HD)), 'wo': init(ks[4], (H * HD, D)), 'gate_w': init(ks[5], (D, E)), 'w1': init(ks[6], (E, D, F)), 'w3': init(ks[7], (E, D, F)), 'w2': init(ks[8], (E, F, D))}
    _L0_ffn_all = _L0_ffn_setup()
    _L0_ffn_in = {k: v for k, v in _L0_ffn_all.items() if k in ('norm1_w', 'norm2_w', 'wq', 'wk', 'wv', 'wo', 'gate_w', 'w1', 'w3', 'w2')}
    del _L0_ffn_all

    def _L1_xattn_setup():
        import jax, jax.numpy as jnp
        import numpy as np
        import math
        NUM_Q_HEADS = 32
        NUM_KV_HEADS = 8
        key = jax.random.key(seed)
        k1, k2, k3 = jax.random.split(key, 3)
        B, S, E = (2, 256, 256)
        kv_E = NUM_KV_HEADS * (E // NUM_Q_HEADS)
        q = jax.random.normal(k1, (B, S, E), dtype=jnp.float32)
        k = jax.random.normal(k2, (B, S, kv_E), dtype=jnp.float32)
        v = jax.random.normal(k3, (B, S, kv_E), dtype=jnp.float32)
        return {'q': q, 'k': k, 'v': v}
    _L1_xattn_all = _L1_xattn_setup()
    _L1_xattn_in = {k: v for k, v in _L1_xattn_all.items() if k in ()}
    del _L1_xattn_all

    def _L1_ffn_setup():
        import jax, jax.numpy as jnp
        import numpy as np
        B, S, H = (1, 128, 256)
        NH, NKV, D = (32, 8, 64)
        GROUPS = NH // NKV
        E, F, TOPK = (8, 1024, 2)
        EPS = 1e-05

        def rmsnorm(x, w):
            return x * jax.lax.rsqrt(jnp.mean(x * x, axis=-1, keepdims=True) + EPS) * w

        def attention(h, wq, wk, wv, wo):
            b, s, _ = h.shape
            q = (h @ wq).reshape(b, s, NH, D).transpose(0, 2, 1, 3)
            k = (h @ wk).reshape(b, s, NKV, D).transpose(0, 2, 1, 3)
            v = (h @ wv).reshape(b, s, NKV, D).transpose(0, 2, 1, 3)
            k = jnp.repeat(k, GROUPS, axis=1)
            v = jnp.repeat(v, GROUPS, axis=1)
            scores = jnp.einsum('bhqd,bhkd->bhqk', q, k) / jnp.sqrt(jnp.float32(D))
            causal = jnp.tril(jnp.ones((s, s), bool))
            scores = jnp.where(causal, scores, jnp.finfo(scores.dtype).min)
            attn = jax.nn.softmax(scores, axis=-1)
            out = jnp.einsum('bhqk,bhkd->bhqd', attn, v)
            out = out.transpose(0, 2, 1, 3).reshape(b, s, NH * D)
            return out @ wo

        def moe(h, gate_w, w1, w2, w3):
            b, s, hd = h.shape
            t = h.reshape(-1, hd)
            T = t.shape[0]
            probs = jax.nn.softmax(t @ gate_w, axis=-1)
            topw, topi = jax.lax.top_k(probs, TOPK)
            topw = topw / jnp.sum(topw, axis=-1, keepdims=True)
            combine = jnp.zeros((T, E), t.dtype).at[jnp.arange(T)[:, None], topi].add(topw)
            up = jnp.einsum('th,ehf->etf', t, w1)
            gated = jax.nn.relu(up) * jnp.einsum('th,ehf->etf', t, w3)
            down = jnp.einsum('etf,efh->eth', gated, w2)
            out = jnp.einsum('eth,te->th', down, combine)
            return out.reshape(b, s, hd)
        key = jax.random.key(seed)
        ks = jax.random.split(key, 12)
        sc = 0.02
        return {'x': jax.random.normal(ks[0], (B, S, H), dtype=jnp.float32), 'ln1_w': jnp.ones((H,), jnp.float32), 'wq': jax.random.normal(ks[1], (H, NH * D), jnp.float32) * sc, 'wk': jax.random.normal(ks[2], (H, NKV * D), jnp.float32) * sc, 'wv': jax.random.normal(ks[3], (H, NKV * D), jnp.float32) * sc, 'wo': jax.random.normal(ks[4], (NH * D, H), jnp.float32) * sc, 'ln2_w': jnp.ones((H,), jnp.float32), 'gate_w': jax.random.normal(ks[5], (H, E), jnp.float32) * sc, 'w1': jax.random.normal(ks[6], (E, H, F), jnp.float32) * sc, 'w2': jax.random.normal(ks[7], (E, F, H), jnp.float32) * sc, 'w3': jax.random.normal(ks[8], (E, H, F), jnp.float32) * sc}
    _L1_ffn_all = _L1_ffn_setup()
    _L1_ffn_in = {k: v for k, v in _L1_ffn_all.items() if k in ('ln1_w', 'wq', 'wk', 'wv', 'wo', 'ln2_w', 'gate_w', 'w1', 'w2', 'w3')}
    del _L1_ffn_all
    return {'x': x, 'ctx_512': ctx_512, 'L0_xattn_Wq': _L0_xattn_in['Wq'], 'L0_xattn_Wk': _L0_xattn_in['Wk'], 'L0_xattn_gamma_raw': _L0_xattn_in['gamma_raw'], 'L0_ffn_norm1_w': _L0_ffn_in['norm1_w'], 'L0_ffn_norm2_w': _L0_ffn_in['norm2_w'], 'L0_ffn_wq': _L0_ffn_in['wq'], 'L0_ffn_wk': _L0_ffn_in['wk'], 'L0_ffn_wv': _L0_ffn_in['wv'], 'L0_ffn_wo': _L0_ffn_in['wo'], 'L0_ffn_gate_w': _L0_ffn_in['gate_w'], 'L0_ffn_w1': _L0_ffn_in['w1'], 'L0_ffn_w3': _L0_ffn_in['w3'], 'L0_ffn_w2': _L0_ffn_in['w2'], 'L1_ffn_ln1_w': _L1_ffn_in['ln1_w'], 'L1_ffn_wq': _L1_ffn_in['wq'], 'L1_ffn_wk': _L1_ffn_in['wk'], 'L1_ffn_wv': _L1_ffn_in['wv'], 'L1_ffn_wo': _L1_ffn_in['wo'], 'L1_ffn_ln2_w': _L1_ffn_in['ln2_w'], 'L1_ffn_gate_w': _L1_ffn_in['gate_w'], 'L1_ffn_w1': _L1_ffn_in['w1'], 'L1_ffn_w2': _L1_ffn_in['w2'], 'L1_ffn_w3': _L1_ffn_in['w3']}

def reference(x, ctx_512, L0_xattn_Wq, L0_xattn_Wk, L0_xattn_gamma_raw, L0_ffn_norm1_w, L0_ffn_norm2_w, L0_ffn_wq, L0_ffn_wk, L0_ffn_wv, L0_ffn_wo, L0_ffn_gate_w, L0_ffn_w1, L0_ffn_w3, L0_ffn_w2, L1_ffn_ln1_w, L1_ffn_wq, L1_ffn_wk, L1_ffn_wv, L1_ffn_wo, L1_ffn_ln2_w, L1_ffn_gate_w, L1_ffn_w1, L1_ffn_w2, L1_ffn_w3):
    import jax
    import jax.numpy as jnp

    def _L0_xattn_ref(h, adj_raw, Wq, Wk, gamma_raw):
        import jax, jax.numpy as jnp
        import numpy as np
        B, N, D = (16, 256, 64)
        H = 4
        TOP_K_RATIO = 0.3
        b, n, dm = h.shape
        d = dm // H
        Q = (h @ Wq.T).reshape(b, n, H, d).transpose(0, 2, 1, 3)
        K = (h @ Wk.T).reshape(b, n, H, d).transpose(0, 2, 1, 3)
        sim = jnp.einsum('bhnd,bhmd->bnm', Q, K) / (jnp.sqrt(jnp.float32(d)) * H)
        k = max(1, int(n * TOP_K_RATIO))
        topk_vals = jax.lax.top_k(sim, k)[0]
        threshold = topk_vals[:, :, -1:]
        sparse_mask = (sim >= threshold).astype(sim.dtype)
        A_learned = jax.nn.sigmoid(sim) * sparse_mask
        A_learned = (A_learned + jnp.swapaxes(A_learned, -1, -2)) * 0.5
        gamma = jax.nn.sigmoid(gamma_raw)
        return (1.0 - gamma) * adj_raw + gamma * A_learned

    def _L0_ffn_ref(hidden_states, norm1_w, norm2_w, wq, wk, wv, wo, gate_w, w1, w3, w2):
        import jax, jax.numpy as jnp
        import numpy as np
        B, S, D = (2, 256, 256)
        H, KV, HD = (16, 4, 128)
        E, F, TOPK = (8, 512, 2)
        THETA = 1000000.0
        EPS = 1e-05

        def rmsnorm(x, w):
            var = jnp.mean(jnp.square(x), axis=-1, keepdims=True)
            return x * jax.lax.rsqrt(var + EPS) * w

        def rope_cos_sin(seq_len):
            inv_freq = 1.0 / THETA ** (jnp.arange(0, HD, 2, dtype=jnp.float32) / HD)
            ang = jnp.arange(seq_len, dtype=jnp.float32)[:, None] * inv_freq[None, :]
            return (jnp.cos(ang)[None, :, None, :], jnp.sin(ang)[None, :, None, :])

        def apply_rope(x, cos, sin):
            x1, x2 = jnp.split(x, 2, axis=-1)
            return jnp.concatenate([x1 * cos - x2 * sin, x2 * cos + x1 * sin], axis=-1)

        def attention(x, wq, wk, wv, wo):
            b, s, _ = x.shape
            q = (x @ wq).reshape(b, s, H, HD)
            k = (x @ wk).reshape(b, s, KV, HD)
            v = (x @ wv).reshape(b, s, KV, HD)
            cos, sin = rope_cos_sin(s)
            q = apply_rope(q, cos, sin)
            k = apply_rope(k, cos, sin)
            rep = H // KV
            k = jnp.repeat(k, rep, axis=2)
            v = jnp.repeat(v, rep, axis=2)
            scores = jnp.einsum('bqhd,bkhd->bhqk', q, k) / np.sqrt(HD)
            causal = jnp.tril(jnp.ones((s, s), dtype=bool))
            scores = jnp.where(causal[None, None], scores, jnp.finfo(scores.dtype).min)
            probs = jax.nn.softmax(scores, axis=-1)
            out = jnp.einsum('bhqk,bkhd->bqhd', probs, v).reshape(b, s, H * HD)
            return out @ wo

        def moe(x, gate_w, w1, w3, w2):
            b, s, d = x.shape
            xt = x.reshape(b * s, d)
            logits = xt @ gate_w
            topv, topi = jax.lax.top_k(logits, TOPK)
            probs = jax.nn.softmax(topv, axis=-1)
            w = jnp.zeros_like(logits)
            for kk in range(TOPK):
                w = w + jax.nn.one_hot(topi[:, kk], E, dtype=logits.dtype) * probs[:, kk:kk + 1]
            out = jnp.zeros_like(xt)
            for e in range(E):
                h = jax.nn.silu(xt @ w1[e]) * (xt @ w3[e])
                out = out + w[:, e:e + 1] * (h @ w2[e])
            return out.reshape(b, s, d)
        attn_out = attention(rmsnorm(hidden_states, norm1_w), wq, wk, wv, wo)
        h = hidden_states + attn_out
        out = h + moe(rmsnorm(h, norm2_w), gate_w, w1, w3, w2)
        return out

    def _L1_xattn_ref(q, k, v):
        import jax, jax.numpy as jnp
        import numpy as np
        import math
        NUM_Q_HEADS = 32
        NUM_KV_HEADS = 8
        B, S, E = q.shape
        H, KV = (NUM_Q_HEADS, NUM_KV_HEADS)
        D = E // H
        G = H // KV
        scale = math.sqrt(D)
        qh = q.reshape(B, S, KV, G, D).transpose(0, 2, 3, 1, 4)
        kh = k.reshape(B, S, KV, D).transpose(0, 2, 1, 3)
        vh = v.reshape(B, S, KV, D).transpose(0, 2, 1, 3)
        scores = jnp.einsum('bkgsd,bktd->bkgst', qh, kh) / scale
        weights = jax.nn.softmax(scores, axis=-1)
        out = jnp.einsum('bkgst,bktd->bkgsd', weights, vh)
        return out.transpose(0, 3, 1, 2, 4).reshape(B, S, E)

    def _L1_ffn_ref(x, ln1_w, wq, wk, wv, wo, ln2_w, gate_w, w1, w2, w3):
        import jax, jax.numpy as jnp
        import numpy as np
        B, S, H = (1, 128, 256)
        NH, NKV, D = (32, 8, 64)
        GROUPS = NH // NKV
        E, F, TOPK = (8, 1024, 2)
        EPS = 1e-05

        def rmsnorm(x, w):
            return x * jax.lax.rsqrt(jnp.mean(x * x, axis=-1, keepdims=True) + EPS) * w

        def attention(h, wq, wk, wv, wo):
            b, s, _ = h.shape
            q = (h @ wq).reshape(b, s, NH, D).transpose(0, 2, 1, 3)
            k = (h @ wk).reshape(b, s, NKV, D).transpose(0, 2, 1, 3)
            v = (h @ wv).reshape(b, s, NKV, D).transpose(0, 2, 1, 3)
            k = jnp.repeat(k, GROUPS, axis=1)
            v = jnp.repeat(v, GROUPS, axis=1)
            scores = jnp.einsum('bhqd,bhkd->bhqk', q, k) / jnp.sqrt(jnp.float32(D))
            causal = jnp.tril(jnp.ones((s, s), bool))
            scores = jnp.where(causal, scores, jnp.finfo(scores.dtype).min)
            attn = jax.nn.softmax(scores, axis=-1)
            out = jnp.einsum('bhqk,bhkd->bhqd', attn, v)
            out = out.transpose(0, 2, 1, 3).reshape(b, s, NH * D)
            return out @ wo

        def moe(h, gate_w, w1, w2, w3):
            b, s, hd = h.shape
            t = h.reshape(-1, hd)
            T = t.shape[0]
            probs = jax.nn.softmax(t @ gate_w, axis=-1)
            topw, topi = jax.lax.top_k(probs, TOPK)
            topw = topw / jnp.sum(topw, axis=-1, keepdims=True)
            combine = jnp.zeros((T, E), t.dtype).at[jnp.arange(T)[:, None], topi].add(topw)
            up = jnp.einsum('th,ehf->etf', t, w1)
            gated = jax.nn.relu(up) * jnp.einsum('th,ehf->etf', t, w3)
            down = jnp.einsum('etf,efh->eth', gated, w2)
            out = jnp.einsum('eth,te->th', down, combine)
            return out.reshape(b, s, hd)
        h = x + attention(rmsnorm(x, ln1_w), wq, wk, wv, wo)
        return h + moe(rmsnorm(h, ln2_w), gate_w, w1, w2, w3)
    x = x + _L0_xattn_ref(ctx_512, _layernorm(x, axis=-1), L0_xattn_Wq, L0_xattn_Wk, L0_xattn_gamma_raw)
    x = x + _L0_ffn_ref(_layernorm(x, axis=-1), L0_ffn_norm1_w, L0_ffn_norm2_w, L0_ffn_wq, L0_ffn_wk, L0_ffn_wv, L0_ffn_wo, L0_ffn_gate_w, L0_ffn_w1, L0_ffn_w3, L0_ffn_w2)
    x = x + _L1_xattn_ref(_layernorm(x, axis=-1), ctx_512, ctx_512)
    x = x + _L1_ffn_ref(_layernorm(x, axis=-1), L1_ffn_ln1_w, L1_ffn_wq, L1_ffn_wk, L1_ffn_wv, L1_ffn_wo, L1_ffn_ln2_w, L1_ffn_gate_w, L1_ffn_w1, L1_ffn_w2, L1_ffn_w3)
    return x

_drawn_inputs = setup_inputs


def setup_inputs(seed=0):
    import zlib

    import numpy as np

    out = dict(_drawn_inputs(seed))
    spreads = {'L0_ffn_norm1_w': (1.0, 0.6),
     'L0_ffn_norm2_w': (1.0, 0.6),
     'L1_ffn_ln1_w': (1.0, 0.6),
     'L1_ffn_ln2_w': (1.0, 0.6)}
    factors = {'L0_ffn_wq': 8.0,
     'L0_ffn_wk': 8.0,
     'L0_ffn_gate_w': 6.674,
     'L0_ffn_w1': 5.975,
     'L0_ffn_w3': 5.864,
     'L0_ffn_w2': 5.865,
     'L1_ffn_wq': 8.0,
     'L1_ffn_wk': 8.0,
     'L1_ffn_gate_w': 6.17,
     'L1_ffn_w1': 6.572,
     'L1_ffn_w2': 5.443,
     'L1_ffn_w3': 5.446}
    for name, (base, spread) in spreads.items():
        noise = np.random.default_rng([zlib.crc32(name.encode()), seed]).standard_normal(out[name].shape)
        drawn = base * np.exp(spread * noise) if base else spread * noise
        out[name] = jnp.asarray(drawn.astype(out[name].dtype))
    for name, factor in factors.items():
        out[name] = (out[name] * factor).astype(out[name].dtype)
    return out
```

```python
from contextlib import ExitStack

import numpy as np

import concourse.bass as bass
from concourse import mybir

F32 = mybir.dt.float32
I32 = mybir.dt.int32
U32 = mybir.dt.uint32
ALU = mybir.AluOpType
ACT = mybir.ActivationFunctionType
AX_X = mybir.AxisListType.X

P = 128
NB, S, D = 4, 256, 256
CD = 64
NT = NB * S // P
KB = D // P
TS = S // P
EPS = 1e-5

TOPK_SIM = int(S * 0.3)
ROUNDS = -(-TOPK_SIM // 8)
GH, GD = 4, 16

XKV, XG, XD = 8, 4, 8
XV = XD + 1

NE = 8
CF = 256
NSLOT = (2 * NB * S + NE * (P - 1)) // P
EW = KB * 2 * CF + CF // P * D
CHUNK_W = NE * EW
NEG = -1.0e30

QW, KW = 2048, 512
OB = QW // P
WK0, WV0, WO0 = KB * QW, KB * (QW + KW), KB * (QW + 2 * KW)
WA = WO0 + OB * D


class Layer:

    def __init__(self, n, heads, kv, f, rope, act):
        self.n, self.heads, self.kv, self.rope, self.act = n, heads, kv, rope, act
        self.hd = QW // heads
        self.units = heads // 2
        self.kunits = kv // 2
        self.scale = float(1.0 / np.sqrt(self.hd))
        self.chunks = f // CF
        self.steps = self.chunks * NSLOT


LAYERS = [Layer(0, 16, 4, 512, True, ACT.Silu), Layer(1, 32, 8, 1024, False, ACT.Relu)]

C_ID, C_TRI, C_ONE, C_MASK, C_COS, C_SIN = 0, 128, 256, 384, 640, 896
C_GM, C_IOTA, C_THR, C_TILE, C_HALF, C_END = 1152, 1156, 1164, 1172, 1196, 1204
W_N, W_G, W_GAM, W_END = 0, 8, 40, 41


def constants():
    c = np.zeros((P, C_END), np.float32)
    c[:, C_ID:C_ID + P] = np.eye(P)
    c[:, C_TRI:C_TRI + P] = np.triu(np.ones((P, P)), 1)
    c[:, C_ONE:C_ONE + P] = 1.0
    c[:, C_MASK + P:C_MASK + 2 * P] = np.triu(np.full((P, P), NEG), 1)
    half = P // 2
    freq = (np.float32(1.0) / np.float32(1000000.0) ** (np.arange(0, P, 2, dtype=np.float32) / np.float32(P)))
    ang = (np.arange(S, dtype=np.float32)[:, None] * freq.astype(np.float32)[None, :]).astype(np.float32).T
    c[:, C_COS:C_COS + S] = np.concatenate([np.cos(ang)] * 2)
    c[:half, C_SIN:C_SIN + S] = np.sin(ang)
    c[half:, C_SIN:C_SIN + S] = -np.sin(ang)
    for g in range(XG):
        c[:, C_GM + g] = np.where(np.arange(P) % (XG * XD) // XD == g, 1.0 / np.sqrt(np.float32(XD)), 0.0)
    c[:, C_IOTA:C_IOTA + NE] = np.arange(NE)
    c[:, C_THR:C_THR + NT] = P * np.arange(NT)
    c[:, C_TILE:C_TILE + 24] = np.arange(24)
    c[:, C_HALF:C_HALF + NT] = -0.5
    return c


def graph_phase(nc, g, sem, scratch):
    x, con, sm, mv, qd, bank = g["x"], g["con"], g["sm"], g["mv"], g["qd"], g["bank"]
    ident = con[:, C_ID:C_ID + P]
    qk = scratch("g_qk", [CD, 2 * S])
    sim = [scratch(f"g_sim{u}", [P, S]) for u in range(TS)]
    sig = [scratch(f"g_sig{u}", [P, S]) for u in range(TS)]
    left = [scratch(f"g_left{u}", [P, S]) for u in range(TS)]
    top = [scratch(f"g_top{u}", [P, ROUNDS, 8]) for u in range(TS)]
    stat = scratch("g_stat", [P, NT, 6])
    gam = scratch("g_gam", [P, 3])
    norm = scratch("g_norm", [P, TS, D])
    ctx_t = scratch("g_ctxT", [CD, NB * S])
    wqk = scratch("g_wqk", [CD, 2 * CD])
    loaded = sem("g_loaded")
    zeroed = sem("g_zeroed")
    stored = sem("g_stored")
    gate = sem("g_gate")
    stats = sem("g_stats")
    rstd = sem("g_rstd")
    q_mm = sem("g_q_mm")
    q_sb = sem("g_q_sb")
    s_mm = sem("g_s_mm")
    s_sb = sem("g_s_sb")
    pick = sem("g_pick")
    a_t = sem("g_a_t")
    mix = sem("g_mix")
    QK = TS * (2 * ROUNDS - 1) + TS
    MX = 2 * TS + 2

    with nc.Block() as block:
        @block.sync
        def _(sp):
            sp.dma_start(con[:], g["const_in"]).then_inc(loaded, 16)
            sp.dma_start(sm[:], g["small_in"]).then_inc(loaded, 16)
            sp.dma_start(ctx_t[:], g["ctx_t_in"]).then_inc(loaded, 16)
            sp.dma_start(wqk[:], g["wqk_in"]).then_inc(loaded, 16)
            sp.dma_start(x[:], g["x_in"]).then_inc(loaded, 16)
            sp.dma_start(g["wat"][:], g["wa_in"][0]).then_inc(g["wat_loaded"], 16)
            sp.wait_ge(zeroed, 1)
            for n in range(2):
                sp.dma_start(g["xs_dram"][n].rearrange("(t p) d -> p t d", p=P),
                             g["zero"][:].rearrange("p (o d) -> p o d", o=1).to_broadcast([P, NSLOT, D])
                             ).then_inc(stored, 16)
            sp.dma_start(g["ring"][:, 0:CHUNK_W], g["wm_in"][0][0]).then_inc(g["ring_loaded"][0], 16)
            sp.wait_ge(stored, 32)

        @block.gpsimd
        def _(pool):
            nc.gpsimd.memset(g["zero"][:], 0.0).then_inc(zeroed, 1)
            pool.wait_ge(loaded, 80)
            pool.wait_ge(stats, 2 * NT + 1)
            nc.gpsimd.tensor_tensor(qd[:, 1, :], qd[:, 0, :], con[:, C_HALF:C_HALF + NT], ALU.pow).then_inc(rstd, 1)

        @block.tensor
        def _(pe):
            pe.wait_ge(loaded, 80)
            with pe.Fori(0, NB) as b:
                pe.wait_ge(s_sb, b * (2 * TS))
                nc.tensor.matmul(bank[0][:, 0:S], wqk[:], ctx_t[:, bass.ds(b * S, S)],
                                 start=True, stop=True).then_inc(q_mm, 1)
                pe.wait_ge(q_sb, 2 * b + 2)
                for u in range(TS):
                    nc.tensor.matmul(bank[1 + u][:, 0:S], qk[:, u * P:(u + 1) * P], qk[:, S:2 * S],
                                     start=True, stop=True).then_inc(s_mm, 1)
                pe.wait_ge(pick, (b + 1) * QK)
                pe.wait_ge(mix, b * MX)
                for u in range(TS):
                    for v in range(TS):
                        mm = nc.tensor.transpose(bank[3][:, v * S + u * P:v * S + (u + 1) * P],
                                                 left[u][:, v * P:(v + 1) * P], ident)
                mm.then_inc(a_t, 1)

        @block.scalar
        def _(act):
            act.wait_ge(loaded, 80)
            nc.scalar.activation(gam[:, 0:1], sm[:, W_GAM:W_GAM + 1], ACT.Sigmoid).then_inc(gate, 1)
            with act.Fori(0, NB) as b:
                act.wait_ge(q_mm, b + 1)
                act.wait_ge(s_mm, b * TS)
                for i in range(2):
                    nc.scalar.activation(qk[:, i * S:(i + 1) * S], bank[0][i * CD:(i + 1) * CD, 0:S],
                                         ACT.Copy).then_inc(q_sb, 1)
                for u in range(TS):
                    act.wait_ge(s_mm, b * TS + u + 1)
                    act.wait_ge(pick, b * QK)
                    nc.scalar.activation(sim[u][:], bank[1 + u][:, 0:S], ACT.Copy,
                                         scale=float(1.0 / (np.sqrt(GD) * GH))).then_inc(s_sb, 1)
                    nc.scalar.activation(sig[u][:], bank[1 + u][:, 0:S], ACT.Sigmoid,
                                         scale=float(1.0 / (np.sqrt(GD) * GH))).then_inc(s_sb, 1)

        @block.vector
        def _(dve):
            dve.wait_ge(loaded, 80)
            for t in range(NT):
                nc.vector.bn_stats(stat[:, t, :], x[:, t, :]).then_inc(stats, 1)
            for t in range(NT):
                dve.wait_ge(stats, t + 1)
                nc.vector.bn_aggr(mv[:, t, :], stat[:, t, :]).then_inc(stats, 1)
            dve.wait_ge(stats, 2 * NT)
            nc.vector.tensor_scalar(qd[:, 0, :], mv[:, :, 1], EPS, None, ALU.add).then_inc(stats, 1)
            dve.wait_ge(gate, 1)
            nc.vector.tensor_scalar(gam[:, 1:2], gam[:, 0:1], -1.0, 1.0, ALU.mult, ALU.add).then_inc(stats, 1)
            nc.vector.tensor_scalar(gam[:, 2:3], gam[:, 0:1], 0.5, None, ALU.mult).then_inc(stats, 1)
            dve.wait_ge(rstd, 1)
            dve.wait_ge(stats, 2 * NT + 3)
            nc.vector.tensor_scalar(qd[:, 2, :], qd[:, 1, :], gam[:, 1:2], None, ALU.mult).then_inc(stats, 1)
            dve.wait_ge(stats, 2 * NT + 4)
            nc.vector.scalar_tensor_tensor(out=qd[:, 3, :], in0=mv[:, :, 0], scalar=-1.0, in1=qd[:, 2, :],
                                           op0=ALU.mult, op1=ALU.mult).then_inc(stats, 1)
            dve.wait_ge(stats, 2 * NT + 5)
            for b in range(NB):
                n = 0
                dve.wait_ge(s_sb, (b + 1) * (2 * TS))
                dve.wait_ge(a_t, b)
                for r in range(ROUNDS):
                    for u in range(TS):
                        dve.wait_ge(pick, b * QK + max(n - 1, 0))
                        nc.vector.max(top[u][:, r, :], (sim if r == 0 else left)[u][:]).then_inc(pick, 1)
                        n += 1
                    for u in range(TS):
                        if r < ROUNDS - 1:
                            dve.wait_ge(pick, b * QK + n - 1)
                            nc.vector.match_replace(left[u][:], top[u][:, r, :], (sim if r == 0 else left)[u][:],
                                                    NEG).then_inc(pick, 1)
                            n += 1
                last = (TOPK_SIM - 1) % 8
                for u in range(TS):
                    dve.wait_ge(pick, b * QK + n - 1)
                    nc.vector.scalar_tensor_tensor(out=left[u][:], in0=sim[u][:], scalar=top[u][:, ROUNDS - 1, last:last + 1],
                                                   in1=sig[u][:], op0=ALU.is_ge, op1=ALU.mult).then_inc(pick, 1)
                    n += 1
                assert n == QK
                for u in range(TS):
                    dve.wait_ge(mix, b * MX)
                    nc.vector.tensor_scalar(norm[:, u, :], x[:, b * TS + u, :],
                                            qd[:, 2, b * TS + u:b * TS + u + 1], qd[:, 3, b * TS + u:b * TS + u + 1],
                                            ALU.mult, ALU.add).then_inc(mix, 1)
                dve.wait_ge(a_t, b + 1)
                dve.wait_ge(mix, b * MX + TS)
                pair = norm[:].rearrange("p t d -> p (t d)")
                nc.vector.scalar_tensor_tensor(out=pair, in0=bank[3][:], scalar=gam[:, 2:3], in1=pair,
                                               op0=ALU.mult, op1=ALU.add).then_inc(mix, 1)
                dve.wait_ge(mix, b * MX + TS + 1)
                for u in range(TS):
                    nc.vector.scalar_tensor_tensor(out=norm[:, u, :], in0=left[u][:], scalar=gam[:, 2:3],
                                                   in1=norm[:, u, :], op0=ALU.mult, op1=ALU.add).then_inc(mix, 1)
                dve.wait_ge(mix, b * MX + 2 * TS + 1)
                xb = x[:, b * TS:(b + 1) * TS, :].rearrange("p t d -> p (t d)")
                nc.vector.tensor_tensor(xb, xb, pair, ALU.add).then_inc(mix, 1)


def norm_phase(nc, g, sem, scratch, tag, source, mode, weight):
    con, sm, mv, qd, bank, yT, y, xn = (g[k] for k in ("con", "sm", "mv", "qd", "bank", "yT", "y", "xn"))
    src = g[source]
    half = con[:, C_HALF:C_HALF + NT]
    stat = scratch(f"{tag}_stat", [P, NT, 6])
    stats = sem(f"{tag}_stats")
    powed = sem(f"{tag}_powed")
    normed = sem(f"{tag}_normed")
    kept = sem(f"{tag}_kept")
    turned = sem(f"{tag}_turned")
    in_yt = sem(f"{tag}_in_yt")
    base = 2 * NT
    first = base + (3 if mode == "rms" else 1)
    second = first + 4
    groups = NT // 4
    with nc.Block() as block:
        @block.gpsimd
        def _(pool):
            pool.wait_ge(stats, first)
            nc.gpsimd.tensor_tensor(qd[:, 1, :], qd[:, 0, :], half, ALU.pow).then_inc(powed, 1)
            if mode == "ln+rms":
                pool.wait_ge(stats, second)
                nc.gpsimd.tensor_tensor(qd[:, 5, :], qd[:, 4, :], half, ALU.pow).then_inc(powed, 1)

        @block.vector
        def _(dve):
            for t in range(NT):
                nc.vector.bn_stats(stat[:, t, :], src[:, t, :]).then_inc(stats, 1)
            for t in range(NT):
                dve.wait_ge(stats, t + 1)
                nc.vector.bn_aggr(mv[:, t, :], stat[:, t, :]).then_inc(stats, 1)
            mean, var = mv[:, :, 0], mv[:, :, 1]
            dve.wait_ge(stats, base)
            if mode == "rms":
                nc.vector.tensor_tensor(qd[:, 2, :], mean, mean, ALU.mult).then_inc(stats, 1)
                dve.wait_ge(stats, base + 1)
                nc.vector.tensor_tensor(qd[:, 3, :], qd[:, 2, :], var, ALU.add).then_inc(stats, 1)
                dve.wait_ge(stats, base + 2)
                nc.vector.tensor_scalar(qd[:, 0, :], qd[:, 3, :], EPS, None, ALU.add).then_inc(stats, 1)
            else:
                nc.vector.tensor_scalar(qd[:, 0, :], var, EPS, None, ALU.add).then_inc(stats, 1)
            dve.wait_ge(powed, 1)
            if mode != "rms":
                nc.vector.scalar_tensor_tensor(out=qd[:, 3, :], in0=mean, scalar=-1.0, in1=qd[:, 1, :],
                                               op0=ALU.mult, op1=ALU.mult).then_inc(stats, 1)
            if mode == "ln+rms":
                nc.vector.tensor_tensor(qd[:, 2, :], qd[:, 1, :], qd[:, 1, :], ALU.mult).then_inc(stats, 1)
                dve.wait_ge(stats, first + 2)
                nc.vector.tensor_tensor(qd[:, 6, :], qd[:, 2, :], var, ALU.mult).then_inc(stats, 1)
                dve.wait_ge(stats, first + 3)
                nc.vector.tensor_scalar(qd[:, 4, :], qd[:, 6, :], EPS, None, ALU.add).then_inc(stats, 1)
                for t in range(NT):
                    nc.vector.tensor_scalar(y[:, t, :], src[:, t, :], qd[:, 1, t:t + 1], qd[:, 3, t:t + 1],
                                            ALU.mult, ALU.add).then_inc(kept, 1)
                dve.wait_ge(powed, 2)
                for t in range(NT):
                    dve.wait_ge(kept, t + 1)
                    nc.vector.tensor_scalar(xn[:, t, :], y[:, t, :], qd[:, 5, t:t + 1], None,
                                            ALU.mult).then_inc(normed, 1)
            elif mode == "ln":
                dve.wait_ge(stats, first + 1)
                for t in range(NT):
                    nc.vector.tensor_scalar(xn[:, t, :], src[:, t, :], qd[:, 1, t:t + 1], qd[:, 3, t:t + 1],
                                            ALU.mult, ALU.add).then_inc(normed, 1)
            else:
                for t in range(NT):
                    nc.vector.tensor_scalar(xn[:, t, :], src[:, t, :], qd[:, 1, t:t + 1], None,
                                            ALU.mult).then_inc(normed, 1)

        @block.tensor
        def _(pe):
            for q in range(groups):
                pe.wait_ge(normed, 4 * (q + 1))
                for k in range(KB):
                    for j in range(4):
                        mm = nc.tensor.transpose(bank[q * KB + k][:, j * P:(j + 1) * P],
                                                 xn[:, 4 * q + j, k * P:(k + 1) * P], con[:, C_ID:C_ID + P])
                    mm.then_inc(turned, 1)

        @block.scalar
        def _(act):
            for q in range(groups):
                for k in range(KB):
                    act.wait_ge(turned, q * KB + k + 1)
                    scale = 1.0 if weight is None else sm[:, W_N + weight * KB + k:W_N + weight * KB + k + 1]
                    nc.scalar.activation(yT[:, k, q * 4 * P:(q + 1) * 4 * P], bank[q * KB + k][:], ACT.Copy,
                                         scale=scale).then_inc(in_yt, 1)


def attention_phase(nc, g, sem, scratch, lay):
    con, bank, yT, y, wat = (g[k] for k in ("con", "bank", "yT", "y", "wat"))
    ident = con[:, C_ID:C_ID + P]
    tag, hd, U, KU = f"a{lay.n}", lay.hd, lay.units, lay.kunits
    NPR = KU + U
    group = lay.heads // lay.kv
    W = 3 * P
    yb = scratch(f"{tag}_yb", [P, KB, S])
    kT = scratch(f"{tag}_kT", [P, lay.kv, S])
    v = scratch(f"{tag}_v", [P, TS, KW])
    qT = [scratch(f"{tag}_qT{i}", [P, 2, S]) for i in range(3)]
    rot = [scratch(f"{tag}_rot{i}", [P, 2, S]) for i in range(2)]
    pr = [scratch(f"{tag}_p{i}", [P, 2, W]) for i in range(3)]
    prT = [scratch(f"{tag}_pT{i}", [P, 2, W]) for i in range(2)]
    oT = scratch(f"{tag}_oT", [P, OB, S])
    nmax = [scratch(f"{tag}_nmax{i}", [P, 4]) for i in range(3)]
    total = [scratch(f"{tag}_sum{i}", [P, 4]) for i in range(3)]
    rinv = [scratch(f"{tag}_rinv{i}", [P, 4]) for i in range(3)]
    idle = scratch(f"{tag}_idle", [P, 1])
    waited = sem(f"{tag}_waited")
    yb_ok = sem(f"{tag}_yb")
    proj = sem(f"{tag}_proj")
    v_mm = sem(f"{tag}_v_mm")
    v_sb = sem(f"{tag}_v_sb")
    taken = sem(f"{tag}_taken")
    ready = sem(f"{tag}_ready") if lay.rope else taken
    s_mm = sem(f"{tag}_s_mm")
    s_rd = sem(f"{tag}_s_rd")
    expd = sem(f"{tag}_exp")
    inv = sem(f"{tag}_inv")
    p_ok = sem(f"{tag}_p_ok")
    t_mm = sem(f"{tag}_t_mm")
    t_sb = sem(f"{tag}_t_sb")
    o_mm = sem(f"{tag}_o_mm")
    o_sb = sem(f"{tag}_o_sb")
    w_mm = sem(f"{tag}_w_mm")
    w_rd = sem(f"{tag}_w_rd")
    psQ, psS, psT, psO, psW = [bank[0], bank[7]], bank[1:3], bank[3:5], bank[5], bank[6]
    TK = 3 if lay.rope else 1
    parts = [(0, P, C_MASK + P), (P, 2 * P, C_MASK)]

    with nc.Block() as block:
        @block.tensor
        def _(pe):
            pe.wait_ge(g["wat_loaded"], 16 * (lay.n + 1))
            with pe.Fori(0, NB) as b:
                def project(n):
                    if n >= 2:
                        pe.wait_ge(taken, b * (NPR * TK) + (n - 1) * TK)
                    elif n == 0:
                        pe.wait_ge(taken, b * (NPR * TK))
                    for i in range(2):
                        if n >= KU:
                            cols = 2 * (n - KU) + i
                            w = lambda k: wat[:, k * QW + cols * P:k * QW + (cols + 1) * P]
                        else:
                            h = 2 * n + i
                            w = lambda k: wat[:, WK0 + k * KW + h * hd:WK0 + k * KW + (h + 1) * hd]
                        if n >= KU and hd < P:
                            if i == 1:
                                continue
                            w = lambda k: wat[:, k * QW + (n - KU) * P:k * QW + (n - KU + 1) * P]
                        for half in range(P // hd if n < KU else 1):
                            rows = slice(half * hd, (half + 1) * hd) if n < KU else slice(0, P)
                            for k in range(KB):
                                mm = nc.tensor.matmul(psQ[n % 2][rows, i * S:(i + 1) * S], w(k), yb[:, k, :],
                                                      start=(k == 0), stop=(k == KB - 1))
                    mm.then_inc(proj, 1)

                def scores(u):
                    pe.wait_ge(ready, b * NPR + KU + u + 1)
                    if u >= 1:
                        pe.wait_ge(s_rd, b * (4 * U) + 4 * u)
                    for i in range(2):
                        kv = (2 * u + i) // group
                        for r, (c0, n, _) in enumerate(parts):
                            if hd == P:
                                lhs, rhs = qT[u % 3][:, i, r * P:(r + 1) * P], kT[:, kv, 0:n]
                            else:
                                half = slice(i * hd, (i + 1) * hd)
                                lhs, rhs = qT[u % 3][half, 0, r * P:(r + 1) * P], kT[half, kv, 0:n]
                            mm = nc.tensor.matmul(psS[i][:, c0:c0 + n], lhs, rhs, start=True, stop=True)
                        mm.then_inc(s_mm, 1)

                def turn(u):
                    pe.wait_ge(p_ok, b * (4 * U) + 4 * u + 4)
                    for i in range(2):
                        if u >= 1:
                            pe.wait_ge(t_sb, b * (2 * U) + 2 * u - 1 + i)
                        else:
                            pe.wait_ge(v_sb, b * TS + 1 + i)
                        for j in range(3):
                            mm = nc.tensor.transpose(psT[i][:, j * P:(j + 1) * P], pr[u % 3][:, i, j * P:(j + 1) * P], ident)
                        mm.then_inc(t_mm, 1)

                def values(u):
                    pe.wait_ge(t_sb, b * (2 * U) + 2 * u + 2)
                    if u >= 1:
                        pe.wait_ge(o_sb, b * U + u)
                    for i in range(2):
                        kv = (2 * u + i) // group
                        o = psO[:, i * S:(i + 1) * S] if hd == P else psO[i * hd:(i + 1) * hd, 0:S]
                        nc.tensor.matmul(o, v[:, 0, kv * hd:(kv + 1) * hd], prT[u % 2][:, i, 0:2 * P],
                                         start=True, stop=False)
                        mm = nc.tensor.matmul(o[:, P:2 * P], v[:, 1, kv * hd:(kv + 1) * hd], prT[u % 2][:, i, 2 * P:3 * P],
                                              start=False, stop=True)
                    mm.then_inc(o_mm, 1)

                pe.wait_ge(yb_ok, b + 1)
                for n in range(KU):
                    project(n)
                for t in range(TS):
                    pe.wait_ge(t_sb, b * (2 * U))
                    for k in range(KB):
                        mm = nc.tensor.matmul(psT[t][:, 0:KW], yb[:, k, t * P:(t + 1) * P],
                                              wat[:, WV0 + k * KW:WV0 + (k + 1) * KW], start=(k == 0), stop=(k == KB - 1))
                    mm.then_inc(v_mm, 1)
                project(KU)
                project(KU + 1)
                for u in range(U + 2):
                    if u < U:
                        scores(u)
                    if u + 2 < U:
                        project(KU + u + 2)
                    if 1 <= u <= U:
                        turn(u - 1)
                    if u >= 2:
                        values(u - 2)
                pe.wait_ge(w_rd, b)
                for t in range(TS):
                    for c in range(OB):
                        if t == 0 and c == 0:
                            pe.wait_ge(o_sb, b * U + U - 1)
                        if t == 0 and c == OB - OB // U:
                            pe.wait_ge(o_sb, b * U + U)
                        mm = nc.tensor.matmul(psW[:, t * D:(t + 1) * D], oT[:, c, t * P:(t + 1) * P],
                                              wat[:, WO0 + c * D:WO0 + (c + 1) * D], start=(c == 0), stop=(c == OB - 1))
                mm.then_inc(w_mm, 1)

        @block.scalar
        def _(act):
            with act.Fori(0, NB) as b:
                for t in range(TS):
                    act.wait_ge(v_mm, b * TS + t + 1)
                    act.wait_ge(o_mm, b * U)
                    nc.scalar.activation(v[:, t, :], psT[t][:], ACT.Copy).then_inc(v_sb, 1)
                for u in range(U + 2):
                    if u < U:
                        for i in range(2):
                            for r, (c0, n, _) in enumerate(parts):
                                act.wait_ge(s_rd, b * (4 * U) + 4 * u + 2 * i + r + 1)
                                p = pr[u % 3][:, i, c0:c0 + n]
                                k = 2 * i + r
                                nc.scalar.activation(p, p, ACT.Exp, scale=-1.0, bias=nmax[u % 3][:, k:k + 1],
                                                     accum_out=total[u % 3][:, k:k + 1]).then_inc(expd, 1)
                    if 1 <= u <= U:
                        for i in range(2):
                            act.wait_ge(t_mm, b * (2 * U) + 2 * (u - 1) + i + 1)
                            if u >= 3:
                                act.wait_ge(o_mm, b * U + u - 2)
                            nc.scalar.activation(prT[(u - 1) % 2][:, i, :], psT[i][:, 0:W], ACT.Copy).then_inc(t_sb, 1)
                    if u >= 2:
                        act.wait_ge(o_mm, b * U + u - 1)
                        if u == 2:
                            act.wait_ge(w_mm, b)
                        if hd == P:
                            nc.scalar.activation(oT[:, 2 * (u - 2):2 * (u - 1), :].rearrange("p h s -> p (h s)"), psO[:],
                                                 ACT.Copy).then_inc(o_sb, 1)
                        else:
                            nc.scalar.activation(oT[:, u - 2, :], psO[:, 0:S], ACT.Copy).then_inc(o_sb, 1)

        def dest(n):
            if n >= KU:
                return qT[(n - KU) % 3][:]
            return kT[:, 2 * n:2 * n + 2, :]

        @block.gpsimd
        def _(pool):
            if lay.rope:
                with pool.Fori(0, NB) as b:
                    for n in range(NPR):
                        pool.wait_ge(taken, b * (NPR * TK) + n * TK + TK)
                        nc.gpsimd.tensor_tensor(dest(n), dest(n), rot[n % 2][:], ALU.add).then_inc(ready, 1)

        @block.vector
        def _(dve):
            cos = con[:, C_COS:C_COS + S].rearrange("p (o s) -> p o s", o=1)
            sin = con[:, C_SIN:C_SIN + S].rearrange("p (o s) -> p o s", o=1)
            with dve.Fori(0, NB) as b:
                def take(n):
                    dve.wait_ge(proj, b * NPR + n + 1)
                    ps = psQ[n % 2][:].rearrange("p (i s) -> p i s", i=2)
                    if n >= KU + 3:
                        dve.wait_ge(s_mm, b * (2 * U) + 2 * (n - KU - 2))
                    else:
                        dve.wait_ge(s_mm, b * (2 * U))
                    if not lay.rope:
                        if n >= KU:
                            nc.vector.tensor_copy(qT[(n - KU) % 3][:, 0, :], psQ[n % 2][:, 0:S]).then_inc(taken, 1)
                        else:
                            nc.vector.tensor_copy(dest(n), ps).then_inc(taken, 1)
                        return
                    if n >= 2:
                        dve.wait_ge(ready, b * NPR + n - 1)
                    h = P // 2
                    nc.vector.tensor_tensor(dest(n), ps, cos.to_broadcast([P, 2, S]), ALU.mult).then_inc(taken, 1)
                    nc.vector.tensor_tensor(rot[n % 2][0:h], ps[h:P], sin[h:P].to_broadcast([h, 2, S]),
                                            ALU.mult).then_inc(taken, 1)
                    nc.vector.tensor_tensor(rot[n % 2][h:P], ps[0:h], sin[0:h].to_broadcast([h, 2, S]),
                                            ALU.mult).then_inc(taken, 1)

                dve.wait_ge(v_mm, b * TS)
                nc.vector.tensor_copy(yb[:], yT[:, :, bass.ds(b * S, S)]).then_inc(yb_ok, 1)
                for n in range(KU + 2):
                    take(n)
                for u in range(U):
                    for i in range(2):
                        dve.wait_ge(s_mm, b * (2 * U) + 2 * u + i + 1)
                        if u >= 3:
                            dve.wait_ge(t_mm, b * (2 * U) + 2 * (u - 2))
                        dve.wait_ge(waited, b * (2 * U) + 2 * u + i)
                        nc.vector.memset(idle, 0.0).then_inc(waited, 1)
                        for r, (c0, n, m) in enumerate(parts):
                            k = 2 * i + r
                            nc.vector.tensor_tensor_reduce(pr[u % 3][:, i, c0:c0 + n], psS[i][:, c0:c0 + n],
                                                           con[:, m:m + n], -lay.scale, 3.0e38, ALU.add, ALU.min,
                                                           nmax[u % 3][:, k:k + 1]).then_inc(s_rd, 1)
                    if u + 2 < U:
                        take(KU + u + 2)
                    dve.wait_ge(expd, b * (4 * U) + 4 * u + 4)
                    nc.vector.reciprocal(rinv[u % 3][:], total[u % 3][:]).then_inc(inv, 1)
                    dve.wait_ge(inv, b * U + u + 1)
                    for i in range(2):
                        for r, (c0, n, _) in enumerate(parts):
                            k = 2 * i + r
                            p = pr[u % 3][:, i, c0:c0 + n]
                            nc.vector.tensor_scalar(p, p, rinv[u % 3][:, k:k + 1], None, ALU.mult).then_inc(p_ok, 1)
                dve.wait_ge(w_mm, b + 1)
                yt = y[:, bass.ds(b * TS, TS), :].rearrange("p t d -> p (t d)")
                nc.vector.tensor_tensor(yt, yt, psW[:], ALU.add).then_inc(w_rd, 1)


def route_phase(nc, g, sem, scratch, lay):
    con, sm, bank, yT, xn, slot, wgt, offs = (g[k] for k in ("con", "sm", "bank", "yT", "xn", "slot", "wgt", "offs"))
    tag = f"r{lay.n}"
    logit = scratch(f"{tag}_logit", [P, NT, NE])
    best = scratch(f"{tag}_best", [P, NT, 8])
    arg = scratch(f"{tag}_arg", [P, NT, 8], U32)
    argf = scratch(f"{tag}_argf", [P, NT, 2])
    hot = [scratch(f"{tag}_hot{k}", [P, NT, NE]) for k in range(2)]
    both = scratch(f"{tag}_both", [P, NT, NE])
    before = scratch(f"{tag}_before", [P, NT + 1, NE])
    count = scratch(f"{tag}_count", [P, NE])
    fills = scratch(f"{tag}_fills", [P, NE, NT])
    tiles = scratch(f"{tag}_tiles", [P, NE])
    end = scratch(f"{tag}_end", [P, NE])
    start = scratch(f"{tag}_start", [P, NE])
    pos = scratch(f"{tag}_pos", [P, NT, NE])
    mine = scratch(f"{tag}_mine", [P, NT, NE])
    slotf = scratch(f"{tag}_slotf", [P, NT])
    passed = scratch(f"{tag}_passed", [1, NSLOT, NE])
    expert = scratch(f"{tag}_expert", [1, NSLOT])
    expert2 = scratch(f"{tag}_expert2", [1, NSLOT])
    gap = scratch(f"{tag}_gap", [P, NT])
    log_mm = sem(f"{tag}_log_mm")
    step = sem(f"{tag}_step")
    rank_mm = sem(f"{tag}_rank_mm")
    exp_ok = sem(f"{tag}_exp")
    slot_ok = sem(f"{tag}_slot_ok")
    sent = sem(f"{tag}_sent")
    BEFORE = {}

    def bc(ap, shape):
        return ap.to_broadcast(shape)

    with nc.Block() as block:
        @block.vector
        def _(dve):
            n = 0

            def then(ins):
                nonlocal n
                n += 1
                ins.then_inc(step, 1)
                dve.wait_ge(step, n)

            dve.wait_ge(log_mm, 1)
            then(nc.vector.tensor_copy(logit.rearrange("p t e -> p (t e)"), bank[0][:, 0:NT * NE]))
            for t in range(NT):
                n += 1
                nc.vector.max(best[:, t, :], logit[:, t, :]).then_inc(step, 1)
            first = n - NT
            for t in range(NT):
                dve.wait_ge(step, first + t + 1)
                n += 1
                nc.vector.max_index(arg[:, t, :], best[:, t, :], logit[:, t, :]).then_inc(step, 1)
            dve.wait_ge(step, n)
            then(nc.vector.tensor_tensor(gap, best[:, :, 1], best[:, :, 0], ALU.subtract))
            BEFORE["gap"] = n
            then(nc.vector.tensor_copy(argf, arg[:, :, 0:2]))
            iota = con[:, C_IOTA:C_IOTA + NE].rearrange("p (o e) -> p o e", o=1)
            for k in range(2):
                n += 1
                nc.vector.tensor_tensor(hot[k], bc(iota, [P, NT, NE]), bc(argf[:, :, k:k + 1], [P, NT, NE]),
                                        ALU.is_equal).then_inc(step, 1)
            dve.wait_ge(step, n)
            then(nc.vector.tensor_tensor(both, hot[0], hot[1], ALU.add))
            then(nc.vector.memset(before[:, 0, :], 0.0))
            for t in range(NT):
                then(nc.vector.tensor_tensor(before[:, t + 1, :], before[:, t, :], both[:, t, :], ALU.add))
            BEFORE["before"] = n
            dve.wait_ge(rank_mm, 1)
            then(nc.vector.tensor_copy(count, bank[1][:, NT * NE:(NT + 1) * NE]))
            thr = con[:, C_THR:C_THR + NT].rearrange("p (o k) -> p o k", o=1)
            then(nc.vector.tensor_tensor(fills, bc(count.rearrange("p (e o) -> p e o", o=1), [P, NE, NT]),
                                         bc(thr, [P, NE, NT]), ALU.is_gt))
            then(nc.vector.tensor_reduce(tiles, fills, AX_X, ALU.add))
            then(nc.vector.tensor_tensor_scan(end, con[:, C_ONE:C_ONE + NE], tiles, 0.0, ALU.mult, ALU.add))
            then(nc.vector.tensor_tensor(start, end, tiles, ALU.subtract))
            then(nc.vector.scalar_tensor_tensor(
                out=pos, in0=bc(start.rearrange("p (o e) -> p o e", o=1), [P, NT, NE]), scalar=float(P),
                in1=bank[1][:, 0:NT * NE].rearrange("p (t e) -> p t e", t=NT), op0=ALU.mult, op1=ALU.add))
            for k in range(2):
                then(nc.vector.tensor_tensor(mine, hot[k], pos, ALU.mult))
                then(nc.vector.tensor_reduce(slotf, mine, AX_X, ALU.add))
                nc.vector.tensor_copy(slot[k][:], slotf).then_inc(slot_ok, 1)
                dve.wait_ge(slot_ok, k + 1)
            then(nc.vector.tensor_tensor(
                passed, bc(end[0:1].rearrange("p (o e) -> p o e", o=1), [1, NSLOT, NE]),
                bc(con[0:1, C_TILE:C_TILE + NSLOT].rearrange("p (t o) -> p t o", o=1), [1, NSLOT, NE]), ALU.is_le))
            then(nc.vector.tensor_reduce(expert, passed, AX_X, ALU.add))
            then(nc.vector.tensor_scalar(expert2, expert, float(NE - 1), None, ALU.min))
            for c in range(lay.chunks):
                nc.vector.tensor_scalar(offs[:, c * NSLOT:(c + 1) * NSLOT], expert2, float(EW), float(c % 2 * CHUNK_W),
                                        ALU.mult, ALU.add).then_inc(step, 1)
            dve.wait_ge(exp_ok, 1)
            n += lay.chunks
            then(nc.vector.tensor_scalar(gap, wgt[:, 2, :], 1.0, None, ALU.add))
            then(nc.vector.reciprocal(wgt[:, 0, :], gap))
            then(nc.vector.tensor_tensor(wgt[:, 1, :], wgt[:, 2, :], wgt[:, 0, :], ALU.mult))

        @block.scalar
        def _(act):
            act.wait_ge(step, BEFORE["gap"])
            nc.scalar.activation(wgt[:, 2, :], gap, ACT.Exp).then_inc(exp_ok, 1)

        @block.tensor
        def _(pe):
            for t in range(NT):
                for k in range(KB):
                    w = W_G + (lay.n * KB + k) * NE
                    mm = nc.tensor.matmul(bank[0][:, t * NE:(t + 1) * NE], yT[:, k, t * P:(t + 1) * P], sm[:, w:w + NE],
                                          start=(k == 0), stop=(k == KB - 1))
            mm.then_inc(log_mm, 1)
            pe.wait_ge(step, BEFORE["before"])
            tri, ones = con[:, C_TRI:C_TRI + P], con[:, C_ONE:C_ONE + P]
            nc.tensor.matmul(bank[1][:, 0:NT * NE], tri, both.rearrange("p t e -> p (t e)"), start=True, stop=False)
            nc.tensor.matmul(bank[1][:, 0:NT * NE], ones, before[:, 0:NT, :].rearrange("p t e -> p (t e)"),
                             start=False, stop=True)
            nc.tensor.matmul(bank[1][:, NT * NE:(NT + 1) * NE], ones, before[:, NT, :],
                             start=True, stop=True).then_inc(rank_mm, 1)

        @block.gpsimd
        def _(pool):
            for k in range(2):
                pool.wait_ge(slot_ok, k + 1)
                for t in range(NT):
                    nc.gpsimd.indirect_dma_start(
                        g["xs_dram"][lay.n], bass.IndirectOffsetOnAxis(ap=slot[k][:, t:t + 1], axis=0),
                        xn[:, t, :], None).then_inc(sent, 16)
            pool.wait_ge(sent, 2 * NT * 16)


def expert_phase(nc, g, sem, scratch, lay):
    con, sm, bank, ring, offs = (g[k] for k in ("con", "sm", "bank", "ring", "offs"))
    tag, NS, C = f"e{lay.n}", lay.steps, lay.chunks
    ident = con[:, C_ID:C_ID + P]
    acc = scratch(f"{tag}_acc", [P, NSLOT, D])
    xf = [scratch(f"{tag}_xf{i}", [P, KB, P]) for i in range(2)]
    up = [scratch(f"{tag}_up{i}", [P, CF]) for i in range(2)]
    hid = [scratch(f"{tag}_hid{i}", [P, CF]) for i in range(2)]
    hidT = [scratch(f"{tag}_hidT{i}", [P, CF // P, P]) for i in range(2)]
    xsT = scratch(f"{tag}_xsT", [P, NSLOT, KB, P])
    FB = CF // P
    PARTS = [(0, 6), (6, 12), (12, 18), (18, NSLOT)]
    fetched = [sem(f"{tag}_fetched{i}") for i in range(len(PARTS))]
    turned = sem(f"{tag}_turned")
    in_xs = sem(f"{tag}_in_xs")
    cleared = sem(f"{tag}_cleared")
    xf_ok = sem(f"{tag}_xf")
    up_mm = sem(f"{tag}_up_mm")
    up_sb = sem(f"{tag}_up_sb")
    hid_ok = sem(f"{tag}_hid")
    hidt_mm = sem(f"{tag}_hidt_mm")
    hidt_sb = sem(f"{tag}_hidt_sb")
    dn_mm = sem(f"{tag}_dn_mm")
    added = sem(f"{tag}_added")
    stored = sem(f"{tag}_stored")
    loaded = g["ring_loaded"][lay.n]
    psH, psT, psD, psX = bank[0:2], bank[2:4], bank[4:6], bank[6:8]

    with nc.Block() as block:
        @block.sync
        def _(sp):
            xs = g["xs_dram"][lay.n].rearrange("(t p) d -> p t d", p=P)
            for i, (a, z) in enumerate(PARTS):
                sp.dma_start(acc[:, a:z, :], xs[:, a:z, :]).then_inc(fetched[i], 16)
            for c in range(1, C):
                if c >= 2:
                    sp.wait_ge(dn_mm, (c - 1) * NSLOT)
                sp.dma_start(ring[:, c % 2 * CHUNK_W:(c % 2 + 1) * CHUNK_W], g["wm_in"][lay.n][c]).then_inc(loaded, 16)
            ys = g["ys_dram"][lay.n].rearrange("(t p) d -> p t d", p=P)
            for i, (a, z) in enumerate(PARTS):
                sp.wait_ge(added, (C - 1) * NSLOT + z)
                sp.dma_start(ys[:, a:z, :], acc[:, a:z, :]).then_inc(stored, 16)
            sp.wait_ge(stored, 16 * len(PARTS))

        @block.gpsimd
        def _(pool):
            pool.wait_ge(turned, NSLOT)
            nc.gpsimd.memset(acc, 0.0).then_inc(cleared, 1)

        @block.tensor
        def _(pe):
            for t in range(NSLOT):
                for i, (a, _) in enumerate(PARTS):
                    if t == a:
                        pe.wait_ge(fetched[i], 16)
                if t >= 2:
                    pe.wait_ge(in_xs, KB * (t - 1))
                for k in range(KB):
                    mm = nc.tensor.transpose(psX[t % 2][:, k * P:(k + 1) * P], acc[:, t, k * P:(k + 1) * P], ident)
                mm.then_inc(turned, 1)

            def offset(s):
                return nc.tensor.value_load(offs[0:1, bass.ds(s, 1)], min_val=0, max_val=CHUNK_W + (NE - 1) * EW)

            def hidden(s, par):
                w = offset(s)
                pe.wait_ge(loaded, (s // NSLOT + 1) * 16)
                pe.wait_ge(xf_ok, s + 1)
                if not isinstance(s, int) or s >= 2:
                    pe.wait_ge(hid_ok, s - 1)
                for k in range(KB):
                    mm = nc.tensor.matmul(psH[par][:], xf[par][:, k, :], ring[:, bass.ds(w + k * 2 * CF, 2 * CF)],
                                          start=(k == 0), stop=(k == KB - 1))
                mm.then_inc(up_mm, 1)

            def turn(s, par):
                pe.wait_ge(hid_ok, s + 1)
                if not isinstance(s, int) or s >= 2:
                    pe.wait_ge(hidt_sb, s - 1)
                for k in range(FB):
                    mm = nc.tensor.transpose(psT[par][:, k * P:(k + 1) * P], hid[par][:, k * P:(k + 1) * P], ident)
                mm.then_inc(hidt_mm, 1)

            def down(s, par):
                w = offset(s)
                pe.wait_ge(hidt_sb, s + 1)
                if not isinstance(s, int) or s >= 2:
                    pe.wait_ge(added, s - 1)
                for k in range(FB):
                    mm = nc.tensor.matmul(psD[par][:, 0:D], hidT[par][:, k, :], ring[:, bass.ds(w + KB * 2 * CF + k * D, D)],
                                          start=(k == 0), stop=(k == FB - 1))
                mm.then_inc(dn_mm, 1)

            for s in range(4):
                hidden(s, s % 2)
                if s >= 1:
                    turn(s - 1, (s - 1) % 2)
                if s >= 2:
                    down(s - 2, s % 2)
            with pe.Fori(2, NS // 2) as pair:
                s = pair * 2
                for i in range(2):
                    hidden(s + i, i)
                    turn(s + (i - 1), 1 - i)
                    down(s + (i - 2), i)
            turn(NS - 1, 1)
            down(NS - 2, 0)
            down(NS - 1, 1)

        @block.scalar
        def _(act):
            for t in range(NSLOT):
                act.wait_ge(turned, t + 1)
                for k in range(KB):
                    w = W_N + (2 * lay.n + 1) * KB + k
                    nc.scalar.activation(xsT[:, t, k, :], psX[t % 2][:, k * P:(k + 1) * P], ACT.Copy,
                                         scale=sm[:, w:w + 1]).then_inc(in_xs, 1)

            def activate(s, par):
                act.wait_ge(up_mm, s + 1)
                if not isinstance(s, int) or s >= 2:
                    act.wait_ge(hid_ok, s - 1)
                nc.scalar.activation(up[par], psH[par][:, 0:CF], lay.act).then_inc(up_sb, 1)

            def take(s, par):
                act.wait_ge(hidt_mm, s + 1)
                if not isinstance(s, int) or s >= 2:
                    act.wait_ge(dn_mm, s - 1)
                nc.scalar.activation(hidT[par].rearrange("p k t -> p (k t)"), psT[par][:, 0:CF], ACT.Copy).then_inc(hidt_sb, 1)

            for s in range(4):
                activate(s, s % 2)
                if s >= 1:
                    take(s - 1, (s - 1) % 2)
            with act.Fori(2, NS // 2) as pair:
                s = pair * 2
                for i in range(2):
                    activate(s + i, i)
                    take(s + (i - 1), 1 - i)
            take(NS - 1, 1)

        @block.vector
        def _(dve):
            dve.wait_ge(in_xs, KB * NSLOT)
            dve.wait_ge(cleared, 1)

            def fixed(s, par):
                if not isinstance(s, int) or s >= 2:
                    dve.wait_ge(up_mm, s - 1)
                t = s % NSLOT
                nc.vector.tensor_copy(xf[par], xsT[:, bass.ds(t, 1), :, :].rearrange("p o k t -> p (o k) t")).then_inc(xf_ok, 1)

            def hide(s, par):
                dve.wait_ge(up_sb, s + 1)
                if not isinstance(s, int) or s >= 2:
                    dve.wait_ge(hidt_mm, s - 1)
                nc.vector.tensor_tensor(hid[par], up[par], psH[par][:, CF:2 * CF], ALU.mult).then_inc(hid_ok, 1)

            def gather(s, par):
                dve.wait_ge(dn_mm, s + 1)
                if not isinstance(s, int) or s >= NSLOT:
                    dve.wait_ge(added, (s - NSLOT + 1) if isinstance(s, int) else s - 1)
                t = acc[:, bass.ds(s % NSLOT, 1), :].rearrange("p o d -> p (o d)")
                nc.vector.tensor_tensor(t, t, psD[par][:, 0:D], ALU.add).then_inc(added, 1)

            fixed(0, 0)
            for s in range(4):
                fixed(s + 1, (s + 1) % 2)
                hide(s, s % 2)
                if s >= 2:
                    gather(s - 2, s % 2)
            with dve.Fori(2, NS // 2) as pair:
                s = pair * 2
                for i in range(2):
                    if i == 0:
                        fixed(s + 1, 1)
                    else:
                        fixed(s + 2, 0)
                    hide(s + i, i)
                    gather(s + (i - 2), i)
            gather(NS - 2, 0)
            gather(NS - 1, 1)


def combine_phase(nc, g, sem, scratch, lay):
    x, y, slot, wgt = g["x"], g["y"], g["slot"], g["wgt"]
    tag = f"c{lay.n}"
    rows = [scratch(f"{tag}_rows{k}", [P, NT, D]) for k in range(2)]
    got = [[sem(f"{tag}_got{k}_{t}") for t in range(NT // 2)] for k in range(2)]
    add = sem(f"{tag}_add")
    stored = sem(f"{tag}_stored")
    with nc.Block() as block:
        @block.gpsimd
        def _(pool):
            for t in range(NT):
                for k in range(2):
                    nc.gpsimd.indirect_dma_start(
                        rows[k][:, t, :], None, g["ys_dram"][lay.n],
                        bass.IndirectOffsetOnAxis(ap=slot[k][:, t:t + 1], axis=0)).then_inc(got[k][t // 2], 16)

        @block.vector
        def _(dve):
            for t in range(NT):
                nc.vector.tensor_tensor(x[:, t, :], x[:, t, :], y[:, t, :], ALU.add).then_inc(add, 1)
            n = NT
            for q in range(NT // 2):
                for k in range(2):
                    dve.wait_ge(got[k][q], 32)
                    for t in (2 * q, 2 * q + 1):
                        dve.wait_ge(add, t + 1 if k == 0 else n - 1)
                        nc.vector.scalar_tensor_tensor(out=x[:, t, :], in0=rows[k][:, t, :], scalar=wgt[:, k, t:t + 1],
                                                       in1=x[:, t, :], op0=ALU.mult, op1=ALU.add).then_inc(add, 1)
                        n += 1

        if lay.n == 1:
            @block.sync
            def _(sp):
                for q in range(NT // 2):
                    sp.wait_ge(add, NT + 4 * (q + 1))
                    sp.dma_start(g["out"][:, 2 * q:2 * q + 2, :], x[:, 2 * q:2 * q + 2, :]).then_inc(stored, 16)
                sp.wait_ge(stored, 16 * (NT // 2))
        else:
            @block.sync
            def _(sp):
                sp.dma_start(g["wat"][:], g["wa_in"][1]).then_inc(g["wat_loaded"], 16)
                sp.dma_start(g["ring"][:, 0:CHUNK_W], g["wm_in"][1][0]).then_inc(g["ring_loaded"][1], 16)


def cross_phase(nc, g, sem, scratch):
    con, bank, yT, x = g["con"], g["bank"], g["yT"], g["x"]
    ident = con[:, C_ID:C_ID + P]
    rep = scratch("x_rep", [P, KB, NB * S])
    keys = [scratch(f"x_keys{i}", [P, KB, XG, S]) for i in range(2)]
    yb = [scratch(f"x_yb{i}", [P, KB, S]) for i in range(2)]
    pr = [scratch(f"x_p{i}", [P, XG, S]) for i in range(2)]
    prT = [scratch(f"x_pT{i}", [P, TS, XG, P]) for i in range(2)]
    tok = scratch("x_tok", [P, NT, CD])
    vals = scratch("x_vals", [P, NT, XKV, XV])
    nmax = [scratch(f"x_nmax{i}", [P, XG]) for i in range(2)]
    rinv = [scratch(f"x_rinv{i}", [P, XKV * XG]) for i in range(TS)]
    add = [scratch(f"x_add{i}", [P, XKV * XG, XD]) for i in range(TS)]
    loaded = sem("x_loaded")
    vals_ok = sem("x_vals")
    keys_ok = sem("x_keys")
    s_mm = sem("x_s_mm")
    m_ok = sem("x_m_ok")
    expd = sem("x_exp")
    t_mm = sem("x_t_mm")
    t_sb0 = sem("x_t_sb0")
    t_sb1 = sem("x_t_sb1")
    o_mm = sem("x_o_mm")
    o_rd = sem("x_o_rd")
    psS, psT, psO = [bank[0:2], bank[2:4]], bank[4:6], bank[6:8]
    U = TS * XKV
    KS = 1 + KB * XG

    with nc.Block() as block:
        @block.sync
        def _(sp):
            sp.dma_start(rep, g["ctx_rep_in"]).then_inc(loaded, 16)
            sp.dma_start(tok, g["ctx_tok_in"]).then_inc(loaded, 16)

        @block.vector
        def _(dve):
            nc.vector.memset(vals, 1.0).then_inc(vals_ok, 1)
            dve.wait_ge(loaded, 32)
            dve.wait_ge(vals_ok, 1)
            nc.vector.tensor_copy(vals.rearrange("p t h c -> p (t h) c")[:, :, 0:XD],
                                  tok.rearrange("p t (h c) -> p (t h) c", h=XKV)).then_inc(vals_ok, 1)

            def prepare(b, i):
                nc.vector.tensor_copy(yb[i], yT[:, :, bass.ds(b * S, S)]).then_inc(keys_ok, 1)
                for k in range(KB):
                    for q in range(XG):
                        nc.vector.tensor_scalar(keys[i][:, k, q, :], rep[:, k, bass.ds(b * S, S)],
                                                con[:, C_GM + q:C_GM + q + 1], None, ALU.mult).then_inc(keys_ok, 1)

            prepare(0, 0)
            with dve.Fori(0, NB // 2) as pair:
                for i in range(2):
                    b = pair * 2 + i
                    for u in range(U + 1):
                        if u < U:
                            dve.wait_ge(s_mm, b * U + u + 1)
                            if u >= 2:
                                dve.wait_ge(expd, b * (U * XG) + (u - 1) * XG)
                            for h in range(2):
                                nc.vector.tensor_reduce(nmax[u % 2][:, 2 * h:2 * h + 2],
                                                        psS[u % 2][h][:].rearrange("p (q s) -> p q s", q=2),
                                                        AX_X, ALU.max, negate=True).then_inc(m_ok, 1)
                        if u >= 1:
                            dve.wait_ge(t_mm, b * (U * TS) + (u - 1) * TS + 1)
                            if u >= 3:
                                dve.wait_ge(o_mm, b * U + u - 2)
                            nc.vector.tensor_copy(prT[(u - 1) % 2][:, 0, :, :].rearrange("p q s -> p (q s)"),
                                                  psT[0][:]).then_inc(t_sb0, 1)
                        if u == 5:
                            dve.wait_ge(o_mm, b * U)
                            prepare((b + 1) % NB, 1 - i)
                        if u in (XKV + 3, U):
                            t = 0 if u < U else 1
                            dve.wait_ge(o_mm, b * U + (t + 1) * XKV)
                            base = b * (3 * TS) + 3 * t
                            o = psO[t][:, 0:XKV * XG * XV].rearrange("p (h c) -> p h c", c=XV)
                            nc.vector.reciprocal(rinv[t].rearrange("p (h o) -> p h o", o=1), o[:, :, XD:XV]).then_inc(o_rd, 1)
                            dve.wait_ge(o_rd, base + 1)
                            nc.vector.tensor_tensor(add[t], o[:, :, 0:XD],
                                                    rinv[t].rearrange("p (h o) -> p h o", o=1).to_broadcast([P, XKV * XG, XD]),
                                                    ALU.mult).then_inc(o_rd, 1)
                            dve.wait_ge(o_rd, base + 2)
                            xt = x[:, bass.ds(b * TS + t, 1), :].rearrange("p o d -> p (o d)")
                            nc.vector.tensor_tensor(xt, xt, add[t].rearrange("p h c -> p (h c)"), ALU.add).then_inc(o_rd, 1)

        @block.scalar
        def _(act):
            with act.Fori(0, NB) as b:
                for u in range(U + 1):
                    if u < U:
                        for q in range(XG):
                            if q % 2 == 0:
                                act.wait_ge(m_ok, b * (2 * U) + 2 * u + q // 2 + 1)
                            if q == 0 and u >= 2:
                                act.wait_ge(t_mm, b * (U * TS) + (u - 1) * TS)
                            nc.scalar.activation(pr[u % 2][:, q, :], psS[u % 2][q // 2][:, q % 2 * S:(q % 2 + 1) * S],
                                                 ACT.Exp, bias=nmax[u % 2][:, q:q + 1]).then_inc(expd, 1)
                    if u >= 1:
                        act.wait_ge(t_mm, b * (U * TS) + u * TS)
                        if u >= 3:
                            act.wait_ge(o_mm, b * U + u - 2)
                        nc.scalar.activation(prT[(u - 1) % 2][:, 1, :, :].rearrange("p q s -> p (q s)"), psT[1][:],
                                             ACT.Copy).then_inc(t_sb1, 1)

        @block.tensor
        def _(pe):
            with pe.Fori(0, NB // 2) as pair:
                for i in range(2):
                    b = pair * 2 + i

                    def scores(u):
                        t, kv = divmod(u, XKV)
                        rows = slice(kv % 4 * 32, kv % 4 * 32 + 32)
                        if u >= 2:
                            pe.wait_ge(expd, b * (U * XG) + (u - 1) * XG)
                        for h in range(2):
                            mm = nc.tensor.matmul(psS[u % 2][h][:], yb[i][rows, kv // 4, t * P:(t + 1) * P],
                                                  keys[i][rows, kv // 4, 2 * h:2 * h + 2, :].rearrange("p q s -> p (q s)"),
                                                  start=True, stop=True)
                        mm.then_inc(s_mm, 1)

                    def turn(u):
                        pe.wait_ge(expd, b * (U * XG) + (u + 1) * XG)
                        for t in range(TS):
                            if u >= 1:
                                pe.wait_ge((t_sb0, t_sb1)[t], b * U + u)
                            for q in range(XG):
                                mm = nc.tensor.transpose(psT[t][:, q * P:(q + 1) * P], pr[u % 2][:, q, t * P:(t + 1) * P], ident)
                            mm.then_inc(t_mm, 1)

                    def values(u):
                        t, kv = divmod(u, XKV)
                        pe.wait_ge(t_sb0, b * U + u + 1)
                        pe.wait_ge(t_sb1, b * U + u + 1)
                        if kv == 0:
                            pe.wait_ge(o_rd, b * (3 * TS))
                        for q in range(XG):
                            o = (kv * XG + q) * XV
                            for m in range(TS):
                                mm = nc.tensor.matmul(psO[t][:, o:o + XV], prT[u % 2][:, m, q, :],
                                                      vals_of(b, m, kv), start=(m == 0), stop=(m == TS - 1))
                        mm.then_inc(o_mm, 1)

                    def vals_of(b, m, kv):
                        return vals[:, bass.ds(b * TS + m, 1), kv, :].rearrange("p o c -> p (o c)")

                    pe.wait_ge(vals_ok, 2)
                    pe.wait_ge(keys_ok, (b + 1) * KS)
                    for u in range(U + 2):
                        if u < U:
                            scores(u)
                        if 1 <= u <= U:
                            turn(u - 1)
                        if u >= 2:
                            values(u - 2)


def program(nc, x_in, ctx_t, ctx_tok, ctx_rep, wqk, small, const, wa0, wa1, wm0, wm1, out):
    ctx = ExitStack()
    with ctx:
        def sb(name, shape, dt=F32):
            return ctx.enter_context(nc.sbuf_tensor(name, shape, dt))

        def sem(name):
            return ctx.enter_context(nc.semaphore(name))

        g = {
            "bank": [ctx.enter_context(nc.psum_tensor(f"bank{i}", [P, 512], F32)) for i in range(8)],
            "x": sb("x", [P, NT, D]),
            "y": sb("y", [P, NT, D]),
            "yT": sb("yT", [P, KB, NT * P]),
            "con": sb("con", [P, C_END]),
            "sm": sb("sm", [P, W_END]),
            "wat": sb("wat", [P, WA]),
            "ring": sb("ring", [P, 2 * CHUNK_W]),
            "xn": sb("xn", [P, NT, D]),
            "zero": sb("zero", [P, D]),
            "mv": sb("mv", [P, NT, 2]),
            "qd": sb("qd", [P, 8, NT]),
            "slot": [sb(f"slot{k}", [P, NT], U32) for k in range(2)],
            "wgt": sb("wgt", [P, 3, NT]),
            "offs": sb("offs", [1, LAYERS[1].steps], I32),
            "x_in": x_in, "ctx_t_in": ctx_t, "ctx_tok_in": ctx_tok, "ctx_rep_in": ctx_rep, "wqk_in": wqk,
            "small_in": small, "const_in": const, "wa_in": [wa0, wa1], "wm_in": [wm0, wm1], "out": out,
            "xs_dram": [nc.dram_tensor(f"xs{n}", (NSLOT * P, D), F32, kind="Internal").ap() for n in range(2)],
            "ys_dram": [nc.dram_tensor(f"ys{n}", (NSLOT * P, D), F32, kind="Internal").ap() for n in range(2)],
            "wat_loaded": sem("wat_loaded"),
            "ring_loaded": [sem(f"ring_loaded{n}") for n in range(2)],
        }

        def phase(f, *args, home=None):
            with ExitStack() as own:
                at, stop = home[1:] if home else (0, 0)
                used = [at]

                def scratch(name, shape, dt=F32):
                    n = int(np.prod(shape[1:]))
                    if used[0] + n > stop or dt != F32:
                        return own.enter_context(nc.sbuf_tensor(name, shape, dt))[:]
                    flat = g[home[0]][0:shape[0], used[0]:used[0] + n]
                    used[0] += n
                    if len(shape) == 2:
                        return flat
                    axes = "abc"[:len(shape) - 1]
                    return flat.rearrange(f"p ({' '.join(axes)}) -> p {' '.join(axes)}", **dict(zip(axes, shape[1:])))

                f(nc, g, sem, scratch, *args)

        spare = ("ring", CHUNK_W, 2 * CHUNK_W)
        phase(graph_phase)
        plan = [(norm_phase, "n0", "x", "ln+rms", 0), (attention_phase, LAYERS[0]),
                (norm_phase, "m0", "y", "rms", 1), (route_phase, LAYERS[0]),
                (expert_phase, LAYERS[0]), (combine_phase, LAYERS[0]),
                (norm_phase, "nx", "x", "ln", None), (cross_phase,),
                (norm_phase, "n1", "x", "ln+rms", 2), (attention_phase, LAYERS[1]),
                (norm_phase, "m1", "y", "rms", 3), (route_phase, LAYERS[1]),
                (expert_phase, LAYERS[1]), (combine_phase, LAYERS[1])]
        for f, *args in plan:
            phase(f, *args, home=("wat", 0, WA) if f is expert_phase else spare)


def kernel(**inputs):
    import concourse.bacc as _bacc
    from concourse.bass_utils import run_bass_kernel_spmd as _run

    def tiles(a):
        return a.reshape(-1, P, a.shape[-1]).transpose(1, 0, 2)

    def blocks(w):
        return w.reshape(-1, P, w.shape[-1]).transpose(1, 0, 2).reshape(P, -1)

    def attention(n):
        return np.concatenate([blocks(inputs[f"L{n}_ffn_{k}"]) for k in ("wq", "wk", "wv", "wo")], axis=1)

    def experts(n):
        w1, w3, w2 = (inputs[f"L{n}_ffn_{k}"] for k in ("w1", "w3", "w2"))
        f = w1.shape[2]
        up = np.stack([w1, w3], axis=2).reshape(NE, KB, P, 2, f // CF, CF).transpose(4, 2, 0, 1, 3, 5)
        down = w2.reshape(NE, f // CF, CF // P, P, D).transpose(1, 3, 0, 2, 4)
        return np.concatenate([up.reshape(f // CF, P, NE, -1), down.reshape(f // CF, P, NE, -1)], axis=3).reshape(f // CF, P, CHUNK_W)

    inputs = {k: np.asarray(v) for k, v in inputs.items()}
    ctx2 = inputs["ctx_512"].reshape(NB * S, CD)
    ctx_t = ctx2.T
    rep = np.repeat(ctx_t.reshape(XKV, 1, XD, NB * S), XG, axis=1).reshape(KB, P, NB * S).transpose(1, 0, 2)
    small = np.concatenate(
        [inputs[k].reshape(KB, P).T for k in ("L0_ffn_norm1_w", "L0_ffn_norm2_w", "L1_ffn_ln1_w", "L1_ffn_ln2_w")]
        + [blocks(inputs[f"L{n}_ffn_gate_w"]) for n in range(2)]
        + [np.broadcast_to(inputs["L0_xattn_gamma_raw"].reshape(1, 1), (P, 1))], axis=1)
    data = {
        "x_in": tiles(inputs["x"].reshape(NB * S, D)), "ctx_t": ctx_t, "ctx_tok": tiles(ctx2), "ctx_rep": rep,
        "wqk": np.concatenate([inputs["L0_xattn_Wq"].T, inputs["L0_xattn_Wk"].T], axis=1), "small": small,
        "const": constants(), "wa0": attention(0), "wa1": attention(1), "wm0": experts(0), "wm1": experts(1),
    }
    nc = _bacc.Bacc("TRN2", target_bir_lowering=False, num_devices=1)
    arrays, args = {}, []
    for name, a in data.items():
        arrays[name] = np.ascontiguousarray(a)
        args.append(nc.dram_tensor(name, a.shape, F32, kind="ExternalInput").ap())
    res = nc.dram_tensor("result", (P, NT, D), F32, kind="ExternalOutput").ap()
    program(nc, *args, res)
    r = _run(nc, [arrays], core_ids=[0])
    return r.results[0]["result"].transpose(1, 0, 2).reshape(NB, S, D)
```

```python
from contextlib import ExitStack

import numpy as np

import concourse.bass as bass
from concourse import mybir

F32 = mybir.dt.float32
I32 = mybir.dt.int32
U32 = mybir.dt.uint32
BF16 = mybir.dt.bfloat16
ALU = mybir.AluOpType
ACT = mybir.ActivationFunctionType
AX_X = mybir.AxisListType.X

P = 128
NB, S, D = 4, 256, 256
CD = 64
NT = NB * S // P
KB = D // P
TS = S // P
EPS = 1e-5

TOPK_SIM = int(S * 0.3)
ROUNDS = -(-TOPK_SIM // 8)
GH, GD = 4, 16

XKV, XG, XD = 8, 4, 8
XV = XD + 1
XR = 64
PARTS_K = (0, 1, 2, 0, 1, 0)

NE = 8
CF = 256
NSLOT = (2 * NB * S + NE * (P - 1)) // P
EW = KB * 2 * CF + CF // P * D
CHUNK_W = NE * EW
NEG = -1.0e30

QW, KW = 2048, 512
OB = QW // P
WK0, WV0, WO0 = KB * QW, KB * (QW + KW), KB * (QW + 2 * KW)
WA = WO0 + OB * D


class Layer:

    def __init__(self, n, heads, kv, f, rope, act):
        self.n, self.heads, self.kv, self.rope, self.act = n, heads, kv, rope, act
        self.hd = QW // heads
        self.units = heads // 2
        self.kunits = kv // 2
        self.scale = float(1.0 / np.sqrt(self.hd))
        self.chunks = f // CF
        self.steps = self.chunks * NSLOT


LAYERS = [Layer(0, 16, 4, 512, True, ACT.Silu), Layer(1, 32, 8, 1024, False, ACT.Relu)]

C_ID, C_TRI, C_ONE, C_MASK, C_COS, C_SIN = 0, 128, 256, 384, 640, 896
C_GM, C_IOTA, C_THR, C_TILE, C_HALF, C_M1, C_M2, C_END = 1152, 1156, 1164, 1172, 1196, 1212, 1213, 1214
W_N, W_G, W_GAM, W_END = 0, 8, 40, 41


def constants():
    c = np.zeros((P, C_END), np.float32)
    c[:, C_ID:C_ID + P] = np.eye(P)
    c[:, C_TRI:C_TRI + P] = np.triu(np.ones((P, P)), 1)
    c[:, C_ONE:C_ONE + P] = 1.0
    c[:, C_MASK + P:C_MASK + 2 * P] = np.triu(np.full((P, P), NEG), 1)
    half = P // 2
    freq = (np.float32(1.0) / np.float32(1000000.0) ** (np.arange(0, P, 2, dtype=np.float32) / np.float32(P)))
    ang = (np.arange(S, dtype=np.float32)[:, None] * freq.astype(np.float32)[None, :]).astype(np.float32).T
    c[:, C_COS:C_COS + S] = np.concatenate([np.cos(ang)] * 2)
    c[:half, C_SIN:C_SIN + S] = np.sin(ang)
    c[half:, C_SIN:C_SIN + S] = -np.sin(ang)
    part = np.zeros(XR, np.int64)
    part[:len(PARTS_K) * XD] = np.repeat(PARTS_K, XD)
    c[:, C_M1] = np.tile(np.where(part >= 1, -1.0, 0.0), P // XR)
    c[:, C_M2] = np.tile(np.where(part == 2, -1.0, 0.0), P // XR)
    c[:, C_IOTA:C_IOTA + NE] = np.arange(NE)
    c[:, C_THR:C_THR + NT] = P * np.arange(NT)
    c[:, C_TILE:C_TILE + 24] = np.arange(24)
    c[:, C_HALF:C_HALF + 2 * NT] = -0.5
    return c


def graph_phase(nc, g, sem, scratch):
    x, con, sm, mv, qd, bank = g["x"], g["con"], g["sm"], g["mv"], g["qd"], g["bank"]
    ident = con[:, C_ID:C_ID + P]
    qk = scratch("g_qk", [CD, 2 * S])
    sim = [[scratch(f"g_sim{i}_{u}", [P, S]) for u in range(TS)] for i in range(2)]
    sig = [[scratch(f"g_sig{i}_{u}", [P, S]) for u in range(TS)] for i in range(2)]
    left = [scratch(f"g_left{u}", [P, S]) for u in range(TS)]
    top = [scratch(f"g_top{u}", [P, ROUNDS, 8]) for u in range(TS)]
    stat = scratch("g_stat", [P, NT, 6])
    gam = scratch("g_gam", [P, 3])
    norm = scratch("g_norm", [P, TS, D])
    ctx_t = scratch("g_ctxT", [CD, NB * S])
    wqk = scratch("g_wqk", [CD, 2 * CD])
    loaded = sem("g_loaded")
    x_in = sem("g_x_in")
    zeroed = sem("g_zeroed")
    stored = sem("g_stored")
    gate = sem("g_gate")
    stats = sem("g_stats")
    rstd = sem("g_rstd")
    q_mm = sem("g_q_mm")
    q_sb = sem("g_q_sb")
    s_mm = sem("g_s_mm")
    s_sb = sem("g_s_sb")
    pick = sem("g_pick")
    a_t = sem("g_a_t")
    mix = sem("g_mix")
    psS = [bank[1:3], bank[4:6]]
    QK = TS * (2 * ROUNDS - 1) + TS
    MX = 2 * TS + 2

    with nc.Block() as block:
        @block.sync
        def _(sp):
            sp.dma_start(wqk[:], g["wqk_in"]).then_inc(loaded, 16)
            sp.dma_start(ctx_t[:], g["ctx_t_in"]).then_inc(loaded, 16)
            sp.dma_start(con[:], g["const_in"]).then_inc(loaded, 16)
            sp.dma_start(sm[:], g["small_in"]).then_inc(x_in, 16)
            sp.dma_start(x[:], g["x_in"]).then_inc(x_in, 16)
            sp.dma_start(g["wat"][:], g["wa_in"][0]).then_inc(g["wat_loaded"], 16)
            sp.wait_ge(zeroed, 1)
            for n in range(2):
                sp.dma_start(g["xs_dram"][n].rearrange("(t p) d -> p t d", p=P),
                             g["zero"][:].rearrange("p (o d) -> p o d", o=1).to_broadcast([P, NSLOT, D])
                             ).then_inc(stored, 16)
            sp.dma_start(g["ring"][:, 0:CHUNK_W], g["wm_in"][0][0]).then_inc(g["ring_loaded"][0], 16)
            sp.wait_ge(stored, 32)

        @block.gpsimd
        def _(pool):
            nc.gpsimd.memset(g["zero"][:], 0.0).then_inc(zeroed, 1)
            pool.wait_ge(loaded, 48)
            pool.wait_ge(stats, 2 * NT + 1)
            nc.gpsimd.tensor_tensor(qd[:, 1, :], qd[:, 0, :], con[:, C_HALF:C_HALF + NT], ALU.pow).then_inc(rstd, 1)

        @block.tensor
        def _(pe):
            pe.wait_ge(loaded, 48)

            def similarities(b):
                pe.wait_ge(q_sb, 2 * b)
                nc.tensor.matmul(bank[0][:, 0:S], wqk[:], ctx_t[:, b * S:(b + 1) * S],
                                 start=True, stop=True).then_inc(q_mm, 1)
                pe.wait_ge(q_sb, 2 * b + 2)
                if b >= 2:
                    pe.wait_ge(s_sb, (b - 1) * 2 * TS)
                for u in range(TS):
                    nc.tensor.matmul(psS[b % 2][u][:, 0:S], qk[:, u * P:(u + 1) * P], qk[:, S:2 * S],
                                     start=True, stop=True).then_inc(s_mm, 1)

            similarities(0)
            for b in range(NB):
                if b + 1 < NB:
                    similarities(b + 1)
                pe.wait_ge(pick, (b + 1) * QK)
                pe.wait_ge(mix, b * MX)
                for u in range(TS):
                    for v in range(TS):
                        mm = nc.tensor.transpose(bank[3][:, v * S + u * P:v * S + (u + 1) * P],
                                                 left[u][:, v * P:(v + 1) * P], ident)
                mm.then_inc(a_t, 1)

        @block.scalar
        def _(act):
            scale = float(1.0 / (np.sqrt(GD) * GH))
            for b in range(NB):
                act.wait_ge(q_mm, b + 1)
                act.wait_ge(s_mm, b * TS)
                for i in range(2):
                    nc.scalar.activation(qk[:, i * S:(i + 1) * S], bank[0][i * CD:(i + 1) * CD, 0:S],
                                         ACT.Copy).then_inc(q_sb, 1)
                for u in range(TS):
                    act.wait_ge(s_mm, b * TS + u + 1)
                    if b >= 2:
                        act.wait_ge(pick, (b - 1) * QK)
                    nc.scalar.activation(sim[b % 2][u][:], psS[b % 2][u][:, 0:S], ACT.Copy, scale=scale).then_inc(s_sb, 1)
                    nc.scalar.activation(sig[b % 2][u][:], psS[b % 2][u][:, 0:S], ACT.Sigmoid, scale=scale).then_inc(s_sb, 1)
                if b == 0:
                    act.wait_ge(x_in, 32)
                    nc.scalar.activation(gam[:, 0:1], sm[:, W_GAM:W_GAM + 1], ACT.Sigmoid).then_inc(gate, 1)

        @block.vector
        def _(dve):
            def normalizers():
                dve.wait_ge(x_in, 32)
                for t in range(NT):
                    nc.vector.bn_stats(stat[:, t, :], x[:, t, :]).then_inc(stats, 1)
                for t in range(NT):
                    dve.wait_ge(stats, t + 1)
                    nc.vector.bn_aggr(mv[:, t, :], stat[:, t, :]).then_inc(stats, 1)
                dve.wait_ge(stats, 2 * NT)
                nc.vector.tensor_scalar(qd[:, 0, :], mv[:, :, 1], EPS, None, ALU.add).then_inc(stats, 1)
                dve.wait_ge(gate, 1)
                nc.vector.tensor_scalar(gam[:, 1:2], gam[:, 0:1], -1.0, 1.0, ALU.mult, ALU.add).then_inc(stats, 1)
                nc.vector.tensor_scalar(gam[:, 2:3], gam[:, 0:1], 0.5, None, ALU.mult).then_inc(stats, 1)
                dve.wait_ge(rstd, 1)
                dve.wait_ge(stats, 2 * NT + 3)
                nc.vector.tensor_scalar(qd[:, 2, :], qd[:, 1, :], gam[:, 1:2], None, ALU.mult).then_inc(stats, 1)
                dve.wait_ge(stats, 2 * NT + 4)
                nc.vector.scalar_tensor_tensor(out=qd[:, 3, :], in0=mv[:, :, 0], scalar=-1.0, in1=qd[:, 2, :],
                                               op0=ALU.mult, op1=ALU.mult).then_inc(stats, 1)
                dve.wait_ge(stats, 2 * NT + 5)

            for b in range(NB):
                n = 0
                dve.wait_ge(s_sb, (b + 1) * (2 * TS))
                dve.wait_ge(a_t, b)
                for r in range(ROUNDS):
                    for u in range(TS):
                        dve.wait_ge(pick, b * QK + max(n - 1, 0))
                        nc.vector.max(top[u][:, r, :], (sim[b % 2] if r == 0 else left)[u][:]).then_inc(pick, 1)
                        n += 1
                    for u in range(TS):
                        if r < ROUNDS - 1:
                            dve.wait_ge(pick, b * QK + n - 1)
                            nc.vector.match_replace(left[u][:], top[u][:, r, :], (sim[b % 2] if r == 0 else left)[u][:],
                                                    NEG).then_inc(pick, 1)
                            n += 1
                last = (TOPK_SIM - 1) % 8
                for u in range(TS):
                    dve.wait_ge(pick, b * QK + n - 1)
                    nc.vector.scalar_tensor_tensor(out=left[u][:], in0=sim[b % 2][u][:], scalar=top[u][:, ROUNDS - 1, last:last + 1],
                                                   in1=sig[b % 2][u][:], op0=ALU.is_ge, op1=ALU.mult).then_inc(pick, 1)
                    n += 1
                assert n == QK
                if b == 0:
                    normalizers()
                for u in range(TS):
                    dve.wait_ge(mix, b * MX)
                    nc.vector.tensor_scalar(norm[:, u, :], x[:, b * TS + u, :],
                                            qd[:, 2, b * TS + u:b * TS + u + 1], qd[:, 3, b * TS + u:b * TS + u + 1],
                                            ALU.mult, ALU.add).then_inc(mix, 1)
                dve.wait_ge(a_t, b + 1)
                dve.wait_ge(mix, b * MX + TS)
                pair = norm[:].rearrange("p t d -> p (t d)")
                nc.vector.scalar_tensor_tensor(out=pair, in0=bank[3][:], scalar=gam[:, 2:3], in1=pair,
                                               op0=ALU.mult, op1=ALU.add).then_inc(mix, 1)
                dve.wait_ge(mix, b * MX + TS + 1)
                for u in range(TS):
                    nc.vector.scalar_tensor_tensor(out=norm[:, u, :], in0=left[u][:], scalar=gam[:, 2:3],
                                                   in1=norm[:, u, :], op0=ALU.mult, op1=ALU.add).then_inc(mix, 1)
                dve.wait_ge(mix, b * MX + 2 * TS + 1)
                xb = x[:, b * TS:(b + 1) * TS, :].rearrange("p t d -> p (t d)")
                nc.vector.tensor_tensor(xb, xb, pair, ALU.add).then_inc(mix, 1)
                dve.wait_ge(mix, (b + 1) * MX)
                for u in range(TS):
                    tile_stats(nc, g, "x", b * TS + u)


def tile_stats(nc, g, source, tile):
    at = slice(tile, tile + 1) if isinstance(tile, int) else bass.ds(tile, 1)
    return nc.vector.bn_stats(g["stat"][:, at, :].rearrange("p o s -> p (o s)"),
                              g[source][:, at, :].rearrange("p o d -> p (o d)"))


class Norm:

    def __init__(self, nc, g, sem, tag, source, mode, weight=None, banks=()):
        self.nc, self.g, self.source, self.mode, self.weight, self.banks = nc, g, source, mode, weight, banks
        self.steps = sem(f"{tag}_steps")
        self.powed = sem(f"{tag}_powed")
        if mode != "ln":
            self.turned = sem(f"{tag}_turned")
            self.in_yt = sem(f"{tag}_in_yt")
        self.first = NT + {"ln": 1, "rms": 3, "ln+rms": 4}[mode]
        self.scaled = self.first + {"ln": 1, "rms": 0, "ln+rms": 3}[mode]
        self.end = self.scaled + NT
        if mode == "ln+rms":
            self.kept = sem(f"{tag}_kept")

    def rows(self, tile):
        return self.scaled + tile + 1

    def pool(self, pool):
        qd, con, nc = self.g["qd"], self.g["con"], self.nc
        n = 2 if self.mode == "ln+rms" else 1
        pool.wait_ge(self.steps, self.first)
        nc.gpsimd.tensor_tensor(qd[:, 2:2 + n, :], qd[:, 0:n, :],
                                con[:, C_HALF:C_HALF + n * NT].rearrange("p (n t) -> p n t", n=n),
                                ALU.pow).then_inc(self.powed, 1)

    def vector(self, dve):
        nc, g, mode, steps = self.nc, self.g, self.mode, self.steps
        mv, qd, xn, src = (g[k] for k in ("mv", "qd", "xn", self.source))
        mean, var, n = mv[:, :, 0], mv[:, :, 1], NT
        for t in range(NT):
            nc.vector.bn_aggr(mv[:, t, :], g["stat"][:, t, :]).then_inc(steps, 1)
        dve.wait_ge(steps, n)
        if mode == "rms":
            nc.vector.tensor_tensor(qd[:, 6, :], mean, mean, ALU.mult).then_inc(steps, 1)
            dve.wait_ge(steps, n + 1)
            nc.vector.tensor_tensor(qd[:, 7, :], qd[:, 6, :], var, ALU.add).then_inc(steps, 1)
            dve.wait_ge(steps, n + 2)
            nc.vector.tensor_scalar(qd[:, 0, :], qd[:, 7, :], EPS, None, ALU.add).then_inc(steps, 1)
        else:
            nc.vector.tensor_scalar(qd[:, 0, :], var, EPS, None, ALU.add).then_inc(steps, 1)
        if mode == "ln+rms":
            dve.wait_ge(steps, n + 1)
            nc.vector.reciprocal(qd[:, 6, :], qd[:, 0, :]).then_inc(steps, 1)
            dve.wait_ge(steps, n + 2)
            nc.vector.tensor_tensor(qd[:, 7, :], qd[:, 6, :], var, ALU.mult).then_inc(steps, 1)
            dve.wait_ge(steps, n + 3)
            nc.vector.tensor_scalar(qd[:, 1, :], qd[:, 7, :], EPS, None, ALU.add).then_inc(steps, 1)
        dve.wait_ge(self.powed, 1)
        n = self.first
        if mode == "ln":
            nc.vector.scalar_tensor_tensor(out=qd[:, 5, :], in0=mean, scalar=-1.0, in1=qd[:, 2, :],
                                           op0=ALU.mult, op1=ALU.mult).then_inc(steps, 1)
            scale, shift = 2, 5
        elif mode == "ln+rms":
            nc.vector.tensor_tensor(qd[:, 4, :], qd[:, 2, :], qd[:, 3, :], ALU.mult).then_inc(steps, 1)
            nc.vector.scalar_tensor_tensor(out=qd[:, 6, :], in0=mean, scalar=-1.0, in1=qd[:, 2, :],
                                           op0=ALU.mult, op1=ALU.mult).then_inc(steps, 1)
            dve.wait_ge(steps, n + 1)
            nc.vector.scalar_tensor_tensor(out=qd[:, 5, :], in0=mean, scalar=-1.0, in1=qd[:, 4, :],
                                           op0=ALU.mult, op1=ALU.mult).then_inc(steps, 1)
            scale, shift = 4, 5
        else:
            scale, shift = 2, None
        dve.wait_ge(steps, self.scaled)
        for t in range(NT):
            if shift is None:
                nc.vector.tensor_scalar(xn[:, t, :], src[:, t, :], qd[:, scale, t:t + 1], None, ALU.mult).then_inc(steps, 1)
            else:
                nc.vector.tensor_scalar(xn[:, t, :], src[:, t, :], qd[:, scale, t:t + 1], qd[:, shift, t:t + 1],
                                        ALU.mult, ALU.add).then_inc(steps, 1)

    def tensor(self, pe):
        for q in range(NT // 4):
            pe.wait_ge(self.steps, self.rows(4 * q + 3))
            for k in range(KB):
                for j in range(4):
                    mm = self.nc.tensor.transpose(self.g["bank"][self.banks[q * KB + k]][:, j * P:(j + 1) * P],
                                                  self.g["xn"][:, 4 * q + j, k * P:(k + 1) * P],
                                                  self.g["con"][:, C_ID:C_ID + P])
                mm.then_inc(self.turned, 1)

    def scalar(self, act):
        for q in range(NT // 4):
            for k in range(KB):
                w = W_N + self.weight * KB + k
                act.wait_ge(self.turned, q * KB + k + 1)
                self.nc.scalar.activation(self.g["yT"][:, k, q * 4 * P:(q + 1) * 4 * P],
                                          self.g["bank"][self.banks[q * KB + k]][:], ACT.Copy,
                                          scale=self.g["sm"][:, w:w + 1]).then_inc(self.in_yt, 1)
        if self.mode == "ln+rms":
            qd = self.g["qd"]
            for t in range(NT):
                self.nc.scalar.activation(self.g["y"][:, t, :], self.g[self.source][:, t, :], ACT.Identity,
                                          scale=qd[:, 2, t:t + 1], bias=qd[:, 6, t:t + 1]).then_inc(self.kept, 1)


def attention_phase(nc, g, sem, scratch, lay):
    con, bank, yT, y, wat = (g[k] for k in ("con", "bank", "yT", "y", "wat"))
    ident = con[:, C_ID:C_ID + P]
    tag, hd, U, KU = f"a{lay.n}", lay.hd, lay.units, lay.kunits
    NPR = KU + U
    group = lay.heads // lay.kv
    W = 3 * P
    yb = scratch(f"{tag}_yb", [P, KB, S])
    kT = scratch(f"{tag}_kT", [P, lay.kv, S])
    v = scratch(f"{tag}_v", [P, TS, KW])
    qT = [scratch(f"{tag}_qT{i}", [P, 2, S]) for i in range(3)]
    rot = [scratch(f"{tag}_rot{i}", [P, 2, S]) for i in range(2)]
    pr = [scratch(f"{tag}_p{i}", [P, 2, W]) for i in range(3)]
    prT = [scratch(f"{tag}_pT{i}", [P, 2, W]) for i in range(2)]
    oT = scratch(f"{tag}_oT", [P, OB, S])
    nmax = [scratch(f"{tag}_nmax{i}", [P, 4]) for i in range(3)]
    total = [scratch(f"{tag}_sum{i}", [P, 4]) for i in range(3)]
    rinv = [scratch(f"{tag}_rinv{i}", [P, 4]) for i in range(3)]
    idle = scratch(f"{tag}_idle", [P, 1])
    waited = sem(f"{tag}_waited")
    yb_ok = sem(f"{tag}_yb")
    proj = sem(f"{tag}_proj")
    v_mm = sem(f"{tag}_v_mm")
    v_sb = sem(f"{tag}_v_sb")
    taken = sem(f"{tag}_taken")
    ready = sem(f"{tag}_ready") if lay.rope else taken
    s_mm = sem(f"{tag}_s_mm")
    s_rd = sem(f"{tag}_s_rd")
    expd = sem(f"{tag}_exp")
    inv = sem(f"{tag}_inv")
    p_ok = sem(f"{tag}_p_ok")
    t_mm = sem(f"{tag}_t_mm")
    t_sb = sem(f"{tag}_t_sb")
    o_mm = sem(f"{tag}_o_mm")
    o_sb = sem(f"{tag}_o_sb")
    w_mm = sem(f"{tag}_w_mm")
    w_rd = sem(f"{tag}_w_rd")
    psQ, psS, psT, psO, psW = [bank[0], bank[7]], bank[1:3], bank[3:5], bank[5], bank[6]
    norm = Norm(nc, g, sem, f"n{lay.n}", "x", "ln+rms", 2 * lay.n, banks=(1, 2, 5, 6))
    TK = 3 if lay.rope else 1
    parts = [(0, P, C_MASK + P), (P, 2 * P, C_MASK)]

    with nc.Block() as block:
        if lay.n == 1:
            @block.sync
            def _(sp):
                sp.dma_start(g["ring"][:, 0:CHUNK_W], g["wm_in"][1][0]).then_inc(g["ring_loaded"][1], 16)

        @block.tensor
        def _(pe):
            norm.tensor(pe)
            pe.wait_ge(g["wat_loaded"], 16 * (lay.n + 1))

            def batch(b, first):
                def project(n):
                    if n >= 2:
                        pe.wait_ge(taken, b * (NPR * TK) + (n - 1) * TK)
                    elif n == 0:
                        pe.wait_ge(taken, b * (NPR * TK))
                    for i in range(2):
                        if n >= KU:
                            cols = 2 * (n - KU) + i
                            w = lambda k: wat[:, k * QW + cols * P:k * QW + (cols + 1) * P]
                        else:
                            h = 2 * n + i
                            w = lambda k: wat[:, WK0 + k * KW + h * hd:WK0 + k * KW + (h + 1) * hd]
                        if n >= KU and hd < P:
                            if i == 1:
                                continue
                            w = lambda k: wat[:, k * QW + (n - KU) * P:k * QW + (n - KU + 1) * P]
                        for half in range(P // hd if n < KU else 1):
                            rows = slice(half * hd, (half + 1) * hd) if n < KU else slice(0, P)
                            for k in range(KB):
                                mm = nc.tensor.matmul(psQ[n % 2][rows, i * S:(i + 1) * S], w(k), yb[:, k, :],
                                                      start=(k == 0), stop=(k == KB - 1))
                    mm.then_inc(proj, 1)

                def scores(u):
                    pe.wait_ge(ready, b * NPR + KU + u + 1)
                    if u >= 1:
                        pe.wait_ge(s_rd, b * (4 * U) + 4 * u)
                    for i in range(2):
                        kv = (2 * u + i) // group
                        for r, (c0, n, _) in enumerate(parts):
                            if hd == P:
                                lhs, rhs = qT[u % 3][:, i, r * P:(r + 1) * P], kT[:, kv, 0:n]
                            else:
                                half = slice(i * hd, (i + 1) * hd)
                                lhs, rhs = qT[u % 3][half, 0, r * P:(r + 1) * P], kT[half, kv, 0:n]
                            mm = nc.tensor.matmul(psS[i][:, c0:c0 + n], lhs, rhs, start=True, stop=True)
                        mm.then_inc(s_mm, 1)

                def turn(u):
                    pe.wait_ge(p_ok, b * (4 * U) + 4 * u + 4)
                    for i in range(2):
                        if u >= 1:
                            pe.wait_ge(t_sb, b * (2 * U) + 2 * u - 1 + i)
                        else:
                            pe.wait_ge(v_sb, b * TS + 1 + i)
                        for j in range(3):
                            mm = nc.tensor.transpose(psT[i][:, j * P:(j + 1) * P], pr[u % 3][:, i, j * P:(j + 1) * P], ident)
                        mm.then_inc(t_mm, 1)

                def values(u):
                    pe.wait_ge(t_sb, b * (2 * U) + 2 * u + 2)
                    if u >= 1:
                        pe.wait_ge(o_sb, b * U + u)
                    for i in range(2):
                        kv = (2 * u + i) // group
                        o = psO[:, i * S:(i + 1) * S] if hd == P else psO[i * hd:(i + 1) * hd, 0:S]
                        nc.tensor.matmul(o, v[:, 0, kv * hd:(kv + 1) * hd], prT[u % 2][:, i, 0:2 * P],
                                         start=True, stop=False)
                        mm = nc.tensor.matmul(o[:, P:2 * P], v[:, 1, kv * hd:(kv + 1) * hd], prT[u % 2][:, i, 2 * P:3 * P],
                                              start=False, stop=True)
                    mm.then_inc(o_mm, 1)

                pe.wait_ge(yb_ok, b + 1)
                for n in range(KU):
                    project(n)
                for t in range(TS):
                    pe.wait_ge(t_sb, b * (2 * U))
                    for k in range(KB):
                        mm = nc.tensor.matmul(psT[t][:, 0:KW], yb[:, k, t * P:(t + 1) * P],
                                              wat[:, WV0 + k * KW:WV0 + (k + 1) * KW], start=(k == 0), stop=(k == KB - 1))
                    mm.then_inc(v_mm, 1)
                project(KU)
                project(KU + 1)
                pe.wait_ge(norm.in_yt, 2 * KB)
                for u in range(U + 2):
                    if u < U:
                        scores(u)
                    if u + 2 < U:
                        project(KU + u + 2)
                    if u < TS and not first:
                        output(b - 1, u)
                    if 1 <= u <= U:
                        turn(u - 1)
                    if u >= 2:
                        values(u - 2)

            def output(b, t):
                if t == 0:
                    pe.wait_ge(w_rd, b)
                    pe.wait_ge(o_sb, b * U + U)
                for c in range(OB):
                    mm = nc.tensor.matmul(psW[:, t * D:(t + 1) * D], oT[:, c, t * P:(t + 1) * P],
                                          wat[:, WO0 + c * D:WO0 + (c + 1) * D], start=(c == 0), stop=(c == OB - 1))
                if t == TS - 1:
                    mm.then_inc(w_mm, 1)

            batch(0, True)
            with pe.Fori(1, NB) as b:
                batch(b, False)
            for t in range(TS):
                output(NB - 1, t)

        @block.scalar
        def _(act):
            norm.scalar(act)
            with act.Fori(0, NB) as b:
                for t in range(TS):
                    act.wait_ge(v_mm, b * TS + t + 1)
                    act.wait_ge(o_mm, b * U)
                    nc.scalar.activation(v[:, t, :], psT[t][:], ACT.Copy).then_inc(v_sb, 1)
                for u in range(U + 2):
                    if u < U:
                        for i in range(2):
                            for r, (c0, n, _) in enumerate(parts):
                                act.wait_ge(s_rd, b * (4 * U) + 4 * u + 2 * i + r + 1)
                                p = pr[u % 3][:, i, c0:c0 + n]
                                k = 2 * i + r
                                nc.scalar.activation(p, p, ACT.Exp, scale=-1.0, bias=nmax[u % 3][:, k:k + 1],
                                                     accum_out=total[u % 3][:, k:k + 1]).then_inc(expd, 1)
                    if 1 <= u <= U:
                        for i in range(2):
                            act.wait_ge(t_mm, b * (2 * U) + 2 * (u - 1) + i + 1)
                            if u >= 3:
                                act.wait_ge(o_mm, b * U + u - 2)
                            nc.scalar.activation(prT[(u - 1) % 2][:, i, :], psT[i][:, 0:W], ACT.Copy).then_inc(t_sb, 1)
                    if u >= 2:
                        act.wait_ge(o_mm, b * U + u - 1)
                        if u == 2:
                            act.wait_ge(w_mm, b)
                        if hd == P:
                            nc.scalar.activation(oT[:, 2 * (u - 2):2 * (u - 1), :].rearrange("p h s -> p (h s)"), psO[:],
                                                 ACT.Copy).then_inc(o_sb, 1)
                        else:
                            nc.scalar.activation(oT[:, u - 2, :], psO[:, 0:S], ACT.Copy).then_inc(o_sb, 1)

        def dest(n):
            if n >= KU:
                return qT[(n - KU) % 3][:]
            return kT[:, 2 * n:2 * n + 2, :]

        @block.gpsimd
        def _(pool):
            norm.pool(pool)
            if lay.rope:
                with pool.Fori(0, NB) as b:
                    for n in range(NPR):
                        pool.wait_ge(taken, b * (NPR * TK) + n * TK + TK)
                        nc.gpsimd.tensor_tensor(dest(n), dest(n), rot[n % 2][:], ALU.add).then_inc(ready, 1)

        @block.vector
        def _(dve):
            cos = con[:, C_COS:C_COS + S].rearrange("p (o s) -> p o s", o=1)
            sin = con[:, C_SIN:C_SIN + S].rearrange("p (o s) -> p o s", o=1)
            norm.vector(dve)

            def batch(b, first):
                def take(n):
                    dve.wait_ge(proj, b * NPR + n + 1)
                    ps = psQ[n % 2][:].rearrange("p (i s) -> p i s", i=2)
                    if n >= KU + 3:
                        dve.wait_ge(s_mm, b * (2 * U) + 2 * (n - KU - 2))
                    else:
                        dve.wait_ge(s_mm, b * (2 * U))
                    if not lay.rope:
                        if n >= KU:
                            nc.vector.tensor_copy(qT[(n - KU) % 3][:, 0, :], psQ[n % 2][:, 0:S]).then_inc(taken, 1)
                        else:
                            nc.vector.tensor_copy(dest(n), ps).then_inc(taken, 1)
                        return
                    if n >= 2:
                        dve.wait_ge(ready, b * NPR + n - 1)
                    h = P // 2
                    nc.vector.tensor_tensor(dest(n), ps, cos.to_broadcast([P, 2, S]), ALU.mult).then_inc(taken, 1)
                    nc.vector.tensor_tensor(rot[n % 2][0:h], ps[h:P], sin[h:P].to_broadcast([h, 2, S]),
                                            ALU.mult).then_inc(taken, 1)
                    nc.vector.tensor_tensor(rot[n % 2][h:P], ps[0:h], sin[0:h].to_broadcast([h, 2, S]),
                                            ALU.mult).then_inc(taken, 1)

                dve.wait_ge(norm.in_yt, (b // 2 + 1) * KB)
                dve.wait_ge(v_mm, b * TS)
                nc.vector.tensor_copy(yb[:], yT[:, :, bass.ds(b * S, S)]).then_inc(yb_ok, 1)
                for n in range(KU + 2):
                    take(n)
                for u in range(U):
                    if u == TS and not first:
                        add_output(b - 1)
                    for i in range(2):
                        dve.wait_ge(s_mm, b * (2 * U) + 2 * u + i + 1)
                        if u >= 3:
                            dve.wait_ge(t_mm, b * (2 * U) + 2 * (u - 2))
                        dve.wait_ge(waited, b * (2 * U) + 2 * u + i)
                        nc.vector.memset(idle, 0.0).then_inc(waited, 1)
                        for r, (c0, n, m) in enumerate(parts):
                            k = 2 * i + r
                            nc.vector.tensor_tensor_reduce(pr[u % 3][:, i, c0:c0 + n], psS[i][:, c0:c0 + n],
                                                           con[:, m:m + n], -lay.scale, 3.0e38, ALU.add, ALU.min,
                                                           nmax[u % 3][:, k:k + 1]).then_inc(s_rd, 1)
                    if u + 2 < U:
                        take(KU + u + 2)
                    dve.wait_ge(expd, b * (4 * U) + 4 * u + 4)
                    nc.vector.reciprocal(rinv[u % 3][:], total[u % 3][:]).then_inc(inv, 1)
                    dve.wait_ge(inv, b * U + u + 1)
                    for i in range(2):
                        for r, (c0, n, _) in enumerate(parts):
                            k = 2 * i + r
                            p = pr[u % 3][:, i, c0:c0 + n]
                            nc.vector.tensor_scalar(p, p, rinv[u % 3][:, k:k + 1], None, ALU.mult).then_inc(p_ok, 1)

            def add_output(b):
                dve.wait_ge(norm.kept, NT)
                dve.wait_ge(w_mm, b + 1)
                tiles = slice(b * TS, (b + 1) * TS) if isinstance(b, int) else bass.ds(b * TS, TS)
                yt = y[:, tiles, :].rearrange("p t d -> p (t d)")
                nc.vector.tensor_tensor(yt, yt, psW[:], ALU.add).then_inc(w_rd, 1)
                dve.wait_ge(w_rd, b + 1)
                for t in range(TS):
                    tile_stats(nc, g, "y", b * TS + t)

            batch(0, True)
            with dve.Fori(1, NB) as b:
                batch(b, False)
            add_output(NB - 1)


def key_rows(nc, g, sem, scratch):
    con = g["con"]
    rep = [g["wat"][:, b * XKV * S:(b + 1) * XKV * S] for b in range(NB)]
    part = [scratch(f"k_part{b}", [P, XKV * S // 2]).bitcast(BF16) for b in range(NB)]
    loaded = [sem(f"k_loaded{b}") for b in range(NB)]
    rounded = sem("k_rounded")
    left = sem("k_left")
    stored = sem("k_stored")

    def transfer(sp):
        for b in range(NB):
            sp.dma_start(rep[b], g["ctx_rep_in"][b]).then_inc(loaded[b], 16)
        for b in range(NB):
            sp.wait_ge(left, NB + b + 1)
            sp.dma_start(g["keys_dram"][b].rearrange("p h t -> p (h t)"), part[b]).then_inc(stored, 16)
        sp.wait_ge(stored, NB * 16)

    def scalar(act):
        for n in range(2 * NB):
            b = n % NB
            act.wait_ge(loaded[b], 16)
            if n >= NB:
                act.wait_ge(left, b + 1)
            nc.scalar.activation(part[b], rep[b], ACT.Copy).then_inc(rounded, 1)

    def vector(dve):
        for n in range(2 * NB):
            b = n % NB
            mask = con[:, C_M1:C_M1 + 1] if n < NB else con[:, C_M2:C_M2 + 1]
            dve.wait_ge(loaded[b], 16)
            dve.wait_ge(rounded, n + 1)
            if n >= NB:
                dve.wait_ge(left, b + 1)
            nc.vector.scalar_tensor_tensor(out=rep[b] if n < NB else part[b], in0=part[b], scalar=mask, in1=rep[b],
                                           op0=ALU.mult, op1=ALU.add).then_inc(left, 1)

    return transfer, scalar, vector


def route_phase(nc, g, sem, scratch, lay):
    con, sm, bank, yT, xn, slot, wgt, offs = (g[k] for k in ("con", "sm", "bank", "yT", "xn", "slot", "wgt", "offs"))
    tag = f"r{lay.n}"
    logit = scratch(f"{tag}_logit", [P, NT, NE])
    best = scratch(f"{tag}_best", [P, NT, 8])
    arg = scratch(f"{tag}_arg", [P, NT, 8], U32)
    argf = scratch(f"{tag}_argf", [P, NT, 2])
    hot = [scratch(f"{tag}_hot{k}", [P, NT, NE]) for k in range(2)]
    both = scratch(f"{tag}_both", [P, NT, NE])
    before = scratch(f"{tag}_before", [P, NT + 1, NE])
    count = scratch(f"{tag}_count", [P, NE])
    fills = scratch(f"{tag}_fills", [P, NE, NT])
    tiles = scratch(f"{tag}_tiles", [P, NE])
    end = scratch(f"{tag}_end", [P, NE])
    start = scratch(f"{tag}_start", [P, NE])
    pos = scratch(f"{tag}_pos", [P, NT, NE])
    mine = scratch(f"{tag}_mine", [P, NT, NE])
    slotf = scratch(f"{tag}_slotf", [P, NT])
    passed = scratch(f"{tag}_passed", [1, NSLOT, NE])
    expert = scratch(f"{tag}_expert", [1, NSLOT])
    expert2 = scratch(f"{tag}_expert2", [1, NSLOT])
    gap = scratch(f"{tag}_gap", [P, NT])
    log_mm = sem(f"{tag}_log_mm")
    step = sem(f"{tag}_step")
    rank_mm = sem(f"{tag}_rank_mm")
    exp_ok = sem(f"{tag}_exp")
    slot_ok = sem(f"{tag}_slot_ok")
    sent = sem(f"{tag}_sent")
    BEFORE = {}

    def bc(ap, shape):
        return ap.to_broadcast(shape)

    norm = Norm(nc, g, sem, f"m{lay.n}", "y", "rms", 2 * lay.n + 1, banks=(2, 3, 4, 5))
    if lay.n == 0:
        move_keys, round_keys, split_keys = key_rows(nc, g, sem, scratch)
    with nc.Block() as block:
        if lay.n == 0:
            @block.sync
            def _(sp):
                move_keys(sp)

        @block.vector
        def _(dve):
            norm.vector(dve)
            n = 0

            def then(ins):
                nonlocal n
                n += 1
                ins.then_inc(step, 1)
                dve.wait_ge(step, n)

            dve.wait_ge(log_mm, 1)
            then(nc.vector.tensor_copy(logit.rearrange("p t e -> p (t e)"), bank[0][:, 0:NT * NE]))
            for t in range(NT):
                n += 1
                nc.vector.max(best[:, t, :], logit[:, t, :]).then_inc(step, 1)
            first = n - NT
            for t in range(NT):
                dve.wait_ge(step, first + t + 1)
                n += 1
                nc.vector.max_index(arg[:, t, :], best[:, t, :], logit[:, t, :]).then_inc(step, 1)
            dve.wait_ge(step, n)
            then(nc.vector.tensor_tensor(gap, best[:, :, 1], best[:, :, 0], ALU.subtract))
            BEFORE["gap"] = n
            then(nc.vector.tensor_copy(argf, arg[:, :, 0:2]))
            iota = con[:, C_IOTA:C_IOTA + NE].rearrange("p (o e) -> p o e", o=1)
            for k in range(2):
                n += 1
                nc.vector.tensor_tensor(hot[k], bc(iota, [P, NT, NE]), bc(argf[:, :, k:k + 1], [P, NT, NE]),
                                        ALU.is_equal).then_inc(step, 1)
            dve.wait_ge(step, n)
            then(nc.vector.tensor_tensor(both, hot[0], hot[1], ALU.add))
            then(nc.vector.memset(before[:, 0, :], 0.0))
            for t in range(NT):
                then(nc.vector.tensor_tensor(before[:, t + 1, :], before[:, t, :], both[:, t, :], ALU.add))
            BEFORE["before"] = n
            dve.wait_ge(rank_mm, 1)
            then(nc.vector.tensor_copy(count, bank[1][:, NT * NE:(NT + 1) * NE]))
            thr = con[:, C_THR:C_THR + NT].rearrange("p (o k) -> p o k", o=1)
            then(nc.vector.tensor_tensor(fills, bc(count.rearrange("p (e o) -> p e o", o=1), [P, NE, NT]),
                                         bc(thr, [P, NE, NT]), ALU.is_gt))
            then(nc.vector.tensor_reduce(tiles, fills, AX_X, ALU.add))
            then(nc.vector.tensor_tensor_scan(end, con[:, C_ONE:C_ONE + NE], tiles, 0.0, ALU.mult, ALU.add))
            then(nc.vector.tensor_tensor(start, end, tiles, ALU.subtract))
            then(nc.vector.scalar_tensor_tensor(
                out=pos, in0=bc(start.rearrange("p (o e) -> p o e", o=1), [P, NT, NE]), scalar=float(P),
                in1=bank[1][:, 0:NT * NE].rearrange("p (t e) -> p t e", t=NT), op0=ALU.mult, op1=ALU.add))
            for k in range(2):
                then(nc.vector.tensor_tensor(mine, hot[k], pos, ALU.mult))
                then(nc.vector.tensor_reduce(slotf, mine, AX_X, ALU.add))
                nc.vector.tensor_copy(slot[k][:], slotf).then_inc(slot_ok, 1)
                dve.wait_ge(slot_ok, k + 1)
            then(nc.vector.tensor_tensor(
                passed, bc(end[0:1].rearrange("p (o e) -> p o e", o=1), [1, NSLOT, NE]),
                bc(con[0:1, C_TILE:C_TILE + NSLOT].rearrange("p (t o) -> p t o", o=1), [1, NSLOT, NE]), ALU.is_le))
            then(nc.vector.tensor_reduce(expert, passed, AX_X, ALU.add))
            then(nc.vector.tensor_scalar(expert2, expert, float(NE - 1), None, ALU.min))
            for c in range(lay.chunks):
                nc.vector.tensor_scalar(offs[:, c * NSLOT:(c + 1) * NSLOT], expert2, float(EW), float(c % 2 * CHUNK_W),
                                        ALU.mult, ALU.add).then_inc(step, 1)
            dve.wait_ge(exp_ok, 1)
            n += lay.chunks
            then(nc.vector.tensor_scalar(gap, wgt[:, 2, :], 1.0, None, ALU.add))
            then(nc.vector.reciprocal(wgt[:, 0, :], gap))
            then(nc.vector.tensor_tensor(wgt[:, 1, :], wgt[:, 2, :], wgt[:, 0, :], ALU.mult))
            if lay.n == 0:
                split_keys(dve)

        @block.scalar
        def _(act):
            norm.scalar(act)
            act.wait_ge(step, BEFORE["gap"])
            nc.scalar.activation(wgt[:, 2, :], gap, ACT.Exp).then_inc(exp_ok, 1)
            if lay.n == 0:
                round_keys(act)

        @block.tensor
        def _(pe):
            norm.tensor(pe)
            for t in range(NT):
                if t % 4 == 0:
                    pe.wait_ge(norm.in_yt, (t // 4 + 1) * KB)
                for k in range(KB):
                    w = W_G + (lay.n * KB + k) * NE
                    mm = nc.tensor.matmul(bank[0][:, t * NE:(t + 1) * NE], yT[:, k, t * P:(t + 1) * P], sm[:, w:w + NE],
                                          start=(k == 0), stop=(k == KB - 1))
            mm.then_inc(log_mm, 1)
            pe.wait_ge(step, BEFORE["before"])
            tri, ones = con[:, C_TRI:C_TRI + P], con[:, C_ONE:C_ONE + P]
            nc.tensor.matmul(bank[1][:, 0:NT * NE], tri, both.rearrange("p t e -> p (t e)"), start=True, stop=False)
            nc.tensor.matmul(bank[1][:, 0:NT * NE], ones, before[:, 0:NT, :].rearrange("p t e -> p (t e)"),
                             start=False, stop=True)
            nc.tensor.matmul(bank[1][:, NT * NE:(NT + 1) * NE], ones, before[:, NT, :],
                             start=True, stop=True).then_inc(rank_mm, 1)

        @block.gpsimd
        def _(pool):
            norm.pool(pool)
            pool.wait_ge(norm.steps, norm.end)
            for k in range(2):
                pool.wait_ge(slot_ok, k + 1)
                for t in range(NT):
                    nc.gpsimd.indirect_dma_start(
                        g["xs_dram"][lay.n], bass.IndirectOffsetOnAxis(ap=slot[k][:, t:t + 1], axis=0),
                        xn[:, t, :], None).then_inc(sent, 16)
            pool.wait_ge(sent, 2 * NT * 16)


def expert_phase(nc, g, sem, scratch, lay):
    con, sm, bank, ring, offs = (g[k] for k in ("con", "sm", "bank", "ring", "offs"))
    tag, NS, C = f"e{lay.n}", lay.steps, lay.chunks
    ident = con[:, C_ID:C_ID + P]
    acc = scratch(f"{tag}_acc", [P, NSLOT, D])
    xf = [scratch(f"{tag}_xf{i}", [P, KB, P]) for i in range(2)]
    up = [scratch(f"{tag}_up{i}", [P, CF]) for i in range(2)]
    hid = [scratch(f"{tag}_hid{i}", [P, CF]) for i in range(2)]
    hidT = [scratch(f"{tag}_hidT{i}", [P, CF // P, P]) for i in range(2)]
    xsT = scratch(f"{tag}_xsT", [P, NSLOT, KB, P])
    FB = CF // P
    PARTS = [(0, 4), (4, 12), (12, NSLOT)]
    STORES = [(0, 12), (12, 20), (20, NSLOT)]
    GROUPS = [(a, min(a + 4, NSLOT)) for a in range(0, NSLOT, 4)]
    fetched = [sem(f"{tag}_fetched{i}") for i in range(len(PARTS))]
    turned = sem(f"{tag}_turned")
    in_xs0 = sem(f"{tag}_in_xs0")
    in_xs1 = sem(f"{tag}_in_xs1")
    cleared = sem(f"{tag}_cleared")
    xf_ok = sem(f"{tag}_xf")
    up_mm = sem(f"{tag}_up_mm")
    up_sb = sem(f"{tag}_up_sb")
    hid_ok = sem(f"{tag}_hid")
    hidt_mm = sem(f"{tag}_hidt_mm")
    hidt_sb = sem(f"{tag}_hidt_sb")
    dn_mm = sem(f"{tag}_dn_mm")
    added = sem(f"{tag}_added")
    stored = sem(f"{tag}_stored")
    loaded = g["ring_loaded"][lay.n]
    psH, psT, psD = bank[0:2], bank[2:4], bank[4:6]

    with nc.Block() as block:
        @block.sync
        def _(sp):
            xs = g["xs_dram"][lay.n].rearrange("(t p) d -> p t d", p=P)
            for i, (a, z) in enumerate(PARTS):
                sp.dma_start(acc[:, a:z, :], xs[:, a:z, :]).then_inc(fetched[i], 16)
            for c in range(1, C):
                if c == 1:
                    sp.wait_ge(fetched[-1], 16)
                if c >= 2:
                    sp.wait_ge(dn_mm, (c - 1) * NSLOT)
                sp.dma_start(ring[:, c % 2 * CHUNK_W:(c % 2 + 1) * CHUNK_W], g["wm_in"][lay.n][c]).then_inc(loaded, 16)
            ys = g["ys_dram"][lay.n].rearrange("(t p) d -> p t d", p=P)
            for a, z in STORES:
                sp.wait_ge(added, (C - 1) * NSLOT + z)
                sp.dma_start(ys[:, a:z, :], acc[:, a:z, :]).then_inc(stored, 16)
            sp.wait_ge(stored, 16 * len(STORES))

        @block.gpsimd
        def _(pool):
            pool.wait_ge(turned, KB * len(GROUPS))
            nc.gpsimd.memset(acc, 0.0).then_inc(cleared, 1)

        @block.tensor
        def _(pe):
            for q, (a, z) in enumerate(GROUPS):
                for i, (first, _) in enumerate(PARTS):
                    if a == first:
                        pe.wait_ge(fetched[i], 16)
                for k in range(KB):
                    if q >= 4:
                        pe.wait_ge((in_xs0, in_xs1)[k], q - 3)
                    for t in range(a, z):
                        mm = nc.tensor.transpose(bank[q % 4 * KB + k][:, (t - a) * P:(t - a + 1) * P],
                                                 acc[:, t, k * P:(k + 1) * P], ident)
                    mm.then_inc(turned, 1)

            def offset(s):
                return nc.tensor.value_load(offs[0:1, bass.ds(s, 1)], min_val=0, max_val=CHUNK_W + (NE - 1) * EW)

            def hidden(s, par):
                w = offset(s)
                pe.wait_ge(loaded, (s // NSLOT + 1) * 16)
                pe.wait_ge(xf_ok, s + 1)
                if not isinstance(s, int) or s >= 2:
                    pe.wait_ge(hid_ok, s - 1)
                for k in range(KB):
                    mm = nc.tensor.matmul(psH[par][:], xf[par][:, k, :], ring[:, bass.ds(w + k * 2 * CF, 2 * CF)],
                                          start=(k == 0), stop=(k == KB - 1))
                mm.then_inc(up_mm, 1)

            def turn(s, par):
                pe.wait_ge(hid_ok, s + 1)
                if not isinstance(s, int) or s >= 2:
                    pe.wait_ge(hidt_sb, s - 1)
                for k in range(FB):
                    mm = nc.tensor.transpose(psT[par][:, k * P:(k + 1) * P], hid[par][:, k * P:(k + 1) * P], ident)
                mm.then_inc(hidt_mm, 1)

            def down(s, par):
                w = offset(s)
                pe.wait_ge(hidt_sb, s + 1)
                if not isinstance(s, int) or s >= 2:
                    pe.wait_ge(added, s - 1)
                for k in range(FB):
                    mm = nc.tensor.matmul(psD[par][:, 0:D], hidT[par][:, k, :], ring[:, bass.ds(w + KB * 2 * CF + k * D, D)],
                                          start=(k == 0), stop=(k == FB - 1))
                mm.then_inc(dn_mm, 1)

            for s in range(4):
                hidden(s, s % 2)
                if s >= 1:
                    turn(s - 1, (s - 1) % 2)
                if s >= 2:
                    down(s - 2, s % 2)
            with pe.Fori(2, NS // 2) as pair:
                s = pair * 2
                for i in range(2):
                    hidden(s + i, i)
                    turn(s + (i - 1), 1 - i)
                    down(s + (i - 2), i)
            turn(NS - 1, 1)
            down(NS - 2, 0)
            down(NS - 1, 1)

        @block.scalar
        def _(act):
            for q, (a, z) in enumerate(GROUPS):
                act.wait_ge(turned, KB * q + 1)
                w = W_N + (2 * lay.n + 1) * KB
                nc.scalar.activation(xsT[:, a:z, 0, :],
                                     bank[q % 4 * KB][:, 0:(z - a) * P].rearrange("p (t r) -> p t r", r=P),
                                     ACT.Copy, scale=sm[:, w:w + 1]).then_inc(in_xs0, 1)

            def activate(s, par):
                act.wait_ge(up_mm, s + 1)
                if not isinstance(s, int) or s >= 2:
                    act.wait_ge(hid_ok, s - 1)
                nc.scalar.activation(up[par], psH[par][:, 0:CF], lay.act).then_inc(up_sb, 1)

            def take(s, par):
                act.wait_ge(hidt_mm, s + 1)
                if not isinstance(s, int) or s >= 2:
                    act.wait_ge(dn_mm, s - 1)
                nc.scalar.activation(hidT[par].rearrange("p k t -> p (k t)"), psT[par][:, 0:CF], ACT.Copy).then_inc(hidt_sb, 1)

            for s in range(4):
                activate(s, s % 2)
                if s >= 1:
                    take(s - 1, (s - 1) % 2)
            with act.Fori(2, NS // 2) as pair:
                s = pair * 2
                for i in range(2):
                    activate(s + i, i)
                    take(s + (i - 1), 1 - i)
            take(NS - 1, 1)

        @block.vector
        def _(dve):
            for q, (a, z) in enumerate(GROUPS):
                dve.wait_ge(turned, KB * q + 2)
                w = W_N + (2 * lay.n + 1) * KB + 1
                nc.vector.tensor_scalar(xsT[:, a:z, 1, :],
                                        bank[q % 4 * KB + 1][:, 0:(z - a) * P].rearrange("p (t r) -> p t r", r=P),
                                        sm[:, w:w + 1], None, ALU.mult).then_inc(in_xs1, 1)
            dve.wait_ge(in_xs0, len(GROUPS))
            dve.wait_ge(in_xs1, len(GROUPS))

            def fixed(s, par):
                if not isinstance(s, int) or s >= 2:
                    dve.wait_ge(up_mm, s - 1)
                t = s % NSLOT
                nc.vector.tensor_copy(xf[par], xsT[:, bass.ds(t, 1), :, :].rearrange("p o k t -> p (o k) t")).then_inc(xf_ok, 1)

            def hide(s, par):
                dve.wait_ge(up_sb, s + 1)
                if not isinstance(s, int) or s >= 2:
                    dve.wait_ge(hidt_mm, s - 1)
                nc.vector.tensor_tensor(hid[par], up[par], psH[par][:, CF:2 * CF], ALU.mult).then_inc(hid_ok, 1)

            def gather(s, par):
                dve.wait_ge(dn_mm, s + 1)
                if not isinstance(s, int) or s >= NSLOT:
                    dve.wait_ge(added, (s - NSLOT + 1) if isinstance(s, int) else s - 1)
                t = acc[:, bass.ds(s % NSLOT, 1), :].rearrange("p o d -> p (o d)")
                nc.vector.tensor_tensor(t, t, psD[par][:, 0:D], ALU.add).then_inc(added, 1)

            fixed(0, 0)
            for s in range(4):
                fixed(s + 1, (s + 1) % 2)
                hide(s, s % 2)
                if s == 2:
                    dve.wait_ge(cleared, 1)
                if s >= 2:
                    gather(s - 2, s % 2)
            with dve.Fori(2, NS // 2) as pair:
                s = pair * 2
                for i in range(2):
                    if i == 0:
                        fixed(s + 1, 1)
                    else:
                        fixed(s + 2, 0)
                    hide(s + i, i)
                    gather(s + (i - 2), i)
            gather(NS - 2, 0)
            gather(NS - 1, 1)


def combine_phase(nc, g, sem, scratch, lay):
    x, y, slot, wgt = g["x"], g["y"], g["slot"], g["wgt"]
    tag = f"c{lay.n}"
    rows = [scratch(f"{tag}_rows{k}", [P, NT, D]) for k in range(2)]
    got = g["got"]
    add = sem(f"{tag}_add")
    stored = sem(f"{tag}_stored")
    with nc.Block() as block:
        @block.gpsimd
        def _(pool):
            for t in range(NT):
                for k in range(2):
                    nc.gpsimd.indirect_dma_start(
                        rows[k][:, t, :], None, g["ys_dram"][lay.n],
                        bass.IndirectOffsetOnAxis(ap=slot[k][:, t:t + 1], axis=0)).then_inc(got[k][t // 2], 16)

        @block.vector
        def _(dve):
            for t in range(NT):
                nc.vector.tensor_tensor(x[:, t, :], x[:, t, :], y[:, t, :], ALU.add).then_inc(add, 1)
            n = NT
            for q in range(NT // 2):
                for k in range(2):
                    dve.wait_ge(got[k][q], 32 * (lay.n + 1))
                    for t in (2 * q, 2 * q + 1):
                        dve.wait_ge(add, t + 1 if k == 0 else n - 1)
                        nc.vector.scalar_tensor_tensor(out=x[:, t, :], in0=rows[k][:, t, :], scalar=wgt[:, k, t:t + 1],
                                                       in1=x[:, t, :], op0=ALU.mult, op1=ALU.add).then_inc(add, 1)
                        n += 1
                if lay.n == 0:
                    for t in (2 * q, 2 * q + 1):
                        dve.wait_ge(add, n - 1 + t % 2)
                        tile_stats(nc, g, "x", t)

        if lay.n == 1:
            @block.sync
            def _(sp):
                for q in range(NT // 2):
                    sp.wait_ge(add, NT + 4 * (q + 1))
                    sp.dma_start(g["out"][:, 2 * q:2 * q + 2, :], x[:, 2 * q:2 * q + 2, :]).then_inc(stored, 16)
                sp.wait_ge(stored, 16 * (NT // 2))


def cross_phase(nc, g, sem, scratch):
    con, bank, x, xn, keys = (g[k] for k in ("con", "bank", "x", "xn", "keys_dram"))
    PAIRS = XKV // 2
    W2 = XG * XR
    pT = [scratch(f"x_pT{i}", [P, TS, 2, 2 * S]) for i in range(4)]
    xq = scratch("x_xq", [P, NT * XKV * W2 // 2]).bitcast(BF16).rearrange("p (t h c) -> p t h c", t=NT, c=XR)
    high = scratch("x_high", [P, NT * D // 2]).bitcast(BF16).rearrange("p (t d) -> p t d", t=NT)
    mid = scratch("x_mid", [P, NT * D // 2]).bitcast(BF16).rearrange("p (t d) -> p t d", t=NT)
    tok = scratch("x_tok", [P, NT, CD])
    vals = scratch("x_vals", [P, PAIRS, TS, 2, 32])
    osb = [scratch(f"x_osb{i}", [P, 2 * S]) for i in range(2)]
    add = [scratch(f"x_add{i}", [P, 8 * TS, XD]) for i in range(2)]
    rinv = [scratch(f"x_rinv{i}", [P, 8 * TS]) for i in range(2)]
    nmax = [scratch(f"x_nmax{i}", [P, TS, XG]) for i in range(2)]
    rest = [scratch(f"x_rest{i}", [P, 2, TS * XG]) for i in range(2)]
    ident = scratch("x_ident", [P, P], BF16)
    xslot = scratch("x_xslot", [P, PAIRS, TS, 2 * W2], BF16)
    kslot = scratch("x_kslot", [P, XKV, S], BF16)
    qt = [scratch(f"x_qt{i}", [P, 4 * S], BF16) for i in range(2)]

    loaded = sem("x_loaded")
    split = sem("x_split")
    spread = sem("x_spread")
    blank = sem("x_blank")
    vals_ok = sem("x_vals")
    slot_in = [sem(f"x_slot_in{w}") for w in range(PAIRS)]
    t_mm = sem("x_t_mm")
    t_sb = sem("x_t_sb")
    s_mm = sem("x_s_mm")
    m_ok = sem("x_m_ok")
    n_ok = sem("x_n_ok")
    p_mm = sem("x_p_mm")
    expd = sem("x_exp")
    o_mm = sem("x_o_mm")
    o_sb = sem("x_o_sb")
    u_mm = sem("x_u_mm")
    fin = sem("x_fin")
    psS, psP, psT, psO, psU = bank[0:2], bank[2:4], bank[4], bank[5], bank[6]
    psT = psT[:].bitcast(BF16)
    UNITS = NB * XKV
    norm = Norm(nc, g, sem, "nx", "x", "ln")
    FIN = 2 + TS

    def sweep(engine, step):
        for j in range(XKV):
            step(0, j)
        with engine.Fori(1, NB) as b:
            for j in range(XKV):
                step(b, j)
        for j in range(XKV):
            step(NB, j)

    def unit(b, j, lag):
        d = j - 1 - lag
        n = b * XKV + d
        if isinstance(b, int) and not 0 <= n < UNITS:
            return None
        return n, d % XKV, b + d // XKV

    def since(n, least):
        return not isinstance(n, int) or n >= least

    with nc.Block() as block:
        @block.sync
        def _(sp):
            sp.dma_start(tok, g["ctx_tok_in"]).then_inc(loaded, 16)

            def fill(w, tiles, keys):
                sp.dma_start(xslot[:, w], xq[:, tiles, 2 * XG * w:2 * XG * (w + 1), :].rearrange("p t h c -> p t (h c)")
                             ).then_inc(slot_in[w], 16)
                sp.dma_start(kslot[:, 2 * w:2 * w + 2, :], keys).then_inc(slot_in[w], 16)

            sp.wait_ge(blank, 1)
            for b in range(2):
                sp.wait_ge(split, 4 if b == 0 else 4 * NB)
                sp.wait_ge(spread, 2 if b == 0 else 2 * NB)
                if b == 0:
                    for w in range(PAIRS):
                        fill(w, slice(0, TS), keys[0, :, 2 * w:2 * w + 2, :])
                    sp.dma_start(g["wat"][:], g["wa_in"][1]).then_inc(g["wat_loaded"], 16)
            with sp.Fori(1, NB) as b:
                for w in range(PAIRS):
                    sp.wait_ge(p_mm, b * (4 * XKV) + 4 * (2 * w + 2 - XKV))
                    fill(w, bass.ds(b * TS, TS), keys[bass.ds(b, 1), :, 2 * w:2 * w + 2, :].rearrange("o p h t -> (o p) h t"))

        @block.gpsimd
        def _(pool):
            norm.pool(pool)
            nc.gpsimd.memset(xq[:, :, :, 6 * XD:XR].rearrange("p t h c -> p (t h) c"), 0.0).then_inc(blank, 1)
            nc.gpsimd.memset(vals, 0.0).then_inc(blank, 1)
            pool.wait_ge(blank, 2)
            nc.gpsimd.memset(vals.rearrange("p w t h c -> p (w t h) c")[:, :, XD:XD + 1], 1.0).then_inc(blank, 1)
            one = con[:, C_ONE:C_ONE + TS * XG].rearrange("p (t g) -> p t g", t=TS)

            def step(b, j):
                at = unit(b, j, 0)
                if at:
                    n, u, _ = at
                    rows = xslot[:, u // 2].rearrange("p t (h g c) -> p t h g c", h=2, g=XG)[:, :, u % 2]
                    part = [rows[:, :, :, 6 * XD + i] for i in range(3)]
                    nm, r = nmax[u % 2], [rest[u % 2][:, i].rearrange("p (t g) -> p t g", t=TS) for i in range(2)]
                    pool.wait_ge(m_ok, n * 4 + 4)
                    nc.gpsimd.tensor_tensor(part[0], nm, one, ALU.mult).then_inc(n_ok, 1)
                    pool.wait_ge(n_ok, n * 5 + 1)
                    nc.gpsimd.tensor_tensor(r[0], nm, part[0], ALU.subtract).then_inc(n_ok, 1)
                    pool.wait_ge(n_ok, n * 5 + 2)
                    nc.gpsimd.tensor_tensor(part[1], r[0], one, ALU.mult).then_inc(n_ok, 1)
                    pool.wait_ge(n_ok, n * 5 + 3)
                    nc.gpsimd.tensor_tensor(r[1], r[0], part[1], ALU.subtract).then_inc(n_ok, 1)
                    pool.wait_ge(n_ok, n * 5 + 4)
                    nc.gpsimd.tensor_tensor(part[2], r[1], one, ALU.mult).then_inc(n_ok, 1)

            sweep(pool, step)

        @block.vector
        def _(dve):
            nc.vector.tensor_copy(ident, con[:, C_ID:C_ID + P]).then_inc(vals_ok, 1)
            norm.vector(dve)
            def split_queries(b):
                tiles = slice(b * TS, (b + 1) * TS)
                xb = xn[:, tiles, :]
                dve.wait_ge(norm.steps, norm.rows(b * TS + TS - 1))
                nc.vector.tensor_copy(high[:, tiles], xb).then_inc(split, 1)
                dve.wait_ge(split, 4 * b + 1)
                nc.vector.tensor_tensor(xb, xb, high[:, tiles], ALU.subtract).then_inc(split, 1)
                dve.wait_ge(split, 4 * b + 2)
                nc.vector.tensor_copy(mid[:, tiles], xb).then_inc(split, 1)
                dve.wait_ge(split, 4 * b + 3)
                nc.vector.tensor_tensor(xq[:, tiles, :, 5 * XD:6 * XD].rearrange("p t h c -> p (t h) c"),
                                        xb.rearrange("p t (h c) -> p (t h) c", c=XD),
                                        mid[:, tiles].rearrange("p t (h c) -> p (t h) c", c=XD),
                                        ALU.subtract).then_inc(split, 1)

            split_queries(0)
            dve.wait_ge(loaded, 16)
            dve.wait_ge(blank, 3)

            def step(b, j):
                at = unit(b, j, 0)
                if at:
                    n, u, c = at
                    for q in range(4):
                        t, e = divmod(q, 2)
                        if q == 0 and since(n, 2):
                            dve.wait_ge(n_ok, n * 5 - 5)
                        dve.wait_ge(s_mm, n * 4 + q + 1)
                        nc.vector.tensor_reduce(nmax[u % 2][:, t].rearrange("p (h e) -> p h e", e=2)[:, :, e],
                                                psS[e][:].rearrange("p (h s) -> p h s", h=2),
                                                AX_X, ALU.max, negate=True).then_inc(m_ok, 1)
                    if isinstance(b, int) and b == 0 and 2 <= j < 1 + NB:
                        split_queries(j - 1)
                    if u % 2 == 0:
                        w = u // 2
                        if since(n, XKV):
                            dve.wait_ge(o_mm, c * XKV + 2 * w + 2 - XKV)
                        tiles = slice(c * TS, (c + 1) * TS) if isinstance(c, int) else bass.ds(c * TS, TS)
                        nc.vector.tensor_copy(vals[:, w, :, :, 0:XD],
                                              tok[:, tiles, 2 * XD * w:2 * XD * (w + 1)].rearrange("p t (h c) -> p t h c", h=2)
                                              ).then_inc(vals_ok, 1)
                at = unit(b, j, 8)
                if at and at[1] % 2 == 0:
                    _, u, c = at
                    w = u // 2
                    p, o = c * PAIRS + w, psU[:].rearrange("p (q c) -> p q c", c=32)
                    r = rinv[w % 2].rearrange("p (q o) -> p q o", o=1)
                    dve.wait_ge(u_mm, p + 1)
                    nc.vector.reciprocal(r, o[:, :, XD:XV]).then_inc(fin, 1)
                    dve.wait_ge(fin, p * FIN + 1)
                    nc.vector.tensor_tensor(add[w % 2], o[:, :, 0:XD], r.to_broadcast([P, 8 * TS, XD]),
                                            ALU.mult).then_inc(fin, 1)
                    dve.wait_ge(fin, p * FIN + 2)
                    for t in range(TS):
                        tile = slice(c * TS + t, c * TS + t + 1) if isinstance(c, int) else bass.ds(c * TS + t, 1)
                        xt = x[:, tile, 8 * XD * w:8 * XD * (w + 1)].rearrange("p o (k h c) -> p (o h) k c", k=2, h=2)
                        nc.vector.tensor_tensor(xt, xt, add[w % 2][:, 8 * t:8 * t + 8].rearrange("p (h k e) d -> p h k (e d)", h=2, k=2),
                                                ALU.add).then_inc(fin, 1)
                    if w == PAIRS - 1:
                        dve.wait_ge(fin, p * FIN + FIN)
                        for t in range(TS):
                            tile_stats(nc, g, "x", c * TS + t)

            sweep(dve, step)

        @block.scalar
        def _(act):
            def spread_queries(b):
                tiles = slice(b * TS, (b + 1) * TS)
                for i, (part, lo, hi) in enumerate([(high, 0, 3), (mid, 3, 5)]):
                    act.wait_ge(split, 4 * b + 1 + 2 * i)
                    src = part[:, tiles].rearrange("p t (h o c) -> p (t h) o c", o=1, c=XD)
                    nc.scalar.activation(xq[:, tiles, :, lo * XD:hi * XD].rearrange("p t h (r c) -> p (t h) r c", c=XD),
                                         src.to_broadcast([P, TS * XKV * XG, hi - lo, XD]), ACT.Copy).then_inc(spread, 1)

            spread_queries(0)

            def step(b, j):
                k = b * XKV + j - 1
                plain, shifted = unit(b, j, -1), unit(b, j, 2)
                if plain or shifted:
                    act.wait_ge(t_mm, k + 2)
                    if unit(b, j, 1):
                        act.wait_ge(s_mm, k * 4)
                    if since(k, 4):
                        act.wait_ge(p_mm, k * 4 - 12)
                    cols = slice(0 if plain else 2 * S, 4 * S if shifted else 2 * S)
                    nc.scalar.activation(qt[(j - 1) % 2][:, cols], psT[:, cols], ACT.Copy).then_inc(t_sb, 1)
                at, out = unit(b, j, 3), unit(b, j, 7)
                for q in range(4):
                    if at:
                        n, u, c = at
                        if since(n, 4) and q % 2 == 0:
                            act.wait_ge(o_mm, (c * PAIRS + u // 2) * 2 - 3 + q // 2)
                        act.wait_ge(p_mm, n * 4 + q + 1)
                        nc.scalar.activation(pT[u % 4][:, q // 2, q % 2], psP[q % 2][:], ACT.Exp,
                                             scale=float(1.0 / np.sqrt(np.float32(XD)))).then_inc(expd, 1)
                    if q == 1 and out and out[1] % 2 == 0:
                        p = out[2] * PAIRS + out[1] // 2
                        act.wait_ge(o_mm, p * 2 + 2)
                        if since(p, 1):
                            act.wait_ge(u_mm, p)
                        nc.scalar.activation(osb[out[1] // 2 % 2], psO[:], ACT.Copy).then_inc(o_sb, 1)
                if isinstance(b, int) and b == 0 and 2 <= j < 1 + NB:
                    spread_queries(j - 1)

            sweep(act, step)

        @block.tensor
        def _(pe):
            def step(b, j):
                k, par = b * XKV + j - 1, (j - 1) % 2
                plain, shifted = unit(b, j, -1), unit(b, j, 2)
                if (plain or shifted) and since(k, 0):
                    pe.wait_ge(t_sb, k + 1)
                for at, base in ((plain, 0), (shifted, 2 * S)):
                    if not at:
                        continue
                    n, u, c = at
                    if at is plain and u % 2 == 0:
                        pe.wait_ge(slot_in[u // 2], c * 32 + 32)
                    if at is shifted:
                        pe.wait_ge(n_ok, n * 5 + 5)
                    for h in range(2):
                        for t in range(TS):
                            mm = nc.tensor.transpose(psT[:, base + h * S + t * P:base + h * S + (t + 1) * P],
                                                     xslot[:, u // 2, t, u % 2 * W2 + h * P:u % 2 * W2 + (h + 1) * P], ident)
                if plain or shifted:
                    mm.then_inc(t_mm, 1)
                seen, lessmax, back = unit(b, j, 0), unit(b, j, 3), unit(b, j, 8)
                for q in range(4):
                    t, e = divmod(q, 2)
                    half = slice(64 * e, 64 * e + 64)
                    if seen:
                        n, u, _ = seen
                        if q == 0:
                            pe.wait_ge(t_sb, k + 1)
                        if q >= 2 or since(n, 1):
                            pe.wait_ge(m_ok, n * 4 + q - 1)
                        for h in range(2):
                            mm = nc.tensor.matmul(psS[e][:, h * S:(h + 1) * S],
                                                  qt[1 - par][half, h * S + t * P:h * S + (t + 1) * P],
                                                  kslot[half, u, :], start=True, stop=True)
                        mm.then_inc(s_mm, 1)
                    if lessmax:
                        n, u, _ = lessmax
                        if q == 0:
                            pe.wait_ge(t_sb, k + 1)
                        if q >= 2 or since(n, 1):
                            pe.wait_ge(expd, n * 4 + q - 1)
                        nc.tensor.matmul(psP[e][:], kslot[half, u, t * P:(t + 1) * P], qt[1 - par][half, 2 * S:4 * S],
                                         start=True, stop=True).then_inc(p_mm, 1)
                    if q == 1:
                        output(b, j)
                if back and back[1] % 2 == 0:
                    w = back[1] // 2
                    p = back[2] * PAIRS + w
                    pe.wait_ge(o_sb, p + 1)
                    if since(p, 1):
                        pe.wait_ge(fin, p * FIN)
                    for t in range(TS):
                        for h in range(2):
                            mm = nc.tensor.transpose(psU[:, (2 * t + h) * P:(2 * t + h + 1) * P],
                                                     osb[w % 2][:, h * S + t * P:h * S + (t + 1) * P], con[:, C_ID:C_ID + P])
                    mm.then_inc(u_mm, 1)

            def output(b, j):
                for m, lag in ((0, 6), (1, 7)):
                    at = unit(b, j, lag)
                    if at and at[1] % 2 == 0:
                        w = at[1] // 2
                        p = at[2] * PAIRS + w
                        pe.wait_ge(expd, p * 8 + (6, 8)[m])
                        if m == 0:
                            pe.wait_ge(vals_ok, p + 2)
                            if since(p, 1):
                                pe.wait_ge(o_sb, p)
                        for i in range(4):
                            mm = nc.tensor.matmul(psO[32 * i:32 * i + 32, :], vals[:, w, m, i // 2, :],
                                                  pT[(2 * w + i // 2) % 4][:, m, i % 2], start=(m == 0), stop=(m == TS - 1))
                        mm.then_inc(o_mm, 1)

            pe.wait_ge(vals_ok, 1)
            sweep(pe, step)


def program(nc, x_in, ctx_t, ctx_tok, ctx_rep, wqk, small, const, wa0, wa1, wm0, wm1, out):
    ctx = ExitStack()
    with ctx:
        def sb(name, shape, dt=F32):
            return ctx.enter_context(nc.sbuf_tensor(name, shape, dt))

        def sem(name):
            return ctx.enter_context(nc.semaphore(name))

        g = {
            "bank": [ctx.enter_context(nc.psum_tensor(f"bank{i}", [P, 512], F32)) for i in range(8)],
            "x": sb("x", [P, NT, D]),
            "y": sb("y", [P, NT, D]),
            "yT": sb("yT", [P, KB, NT * P]),
            "con": sb("con", [P, C_END]),
            "sm": sb("sm", [P, W_END]),
            "wat": sb("wat", [P, WA]),
            "ring": sb("ring", [P, 2 * CHUNK_W]),
            "xn": sb("xn", [P, NT, D]),
            "zero": sb("zero", [P, D]),
            "stat": sb("stat", [P, NT, 6]),
            "mv": sb("mv", [P, NT, 2]),
            "qd": sb("qd", [P, 8, NT]),
            "slot": [sb(f"slot{k}", [P, NT], U32) for k in range(2)],
            "wgt": sb("wgt", [P, 3, NT]),
            "offs": sb("offs", [1, LAYERS[1].steps], I32),
            "x_in": x_in, "ctx_t_in": ctx_t, "ctx_tok_in": ctx_tok, "ctx_rep_in": ctx_rep, "wqk_in": wqk,
            "small_in": small, "const_in": const, "wa_in": [wa0, wa1], "wm_in": [wm0, wm1], "out": out,
            "xs_dram": [nc.dram_tensor(f"xs{n}", (NSLOT * P, D), F32, kind="Internal").ap() for n in range(2)],
            "ys_dram": [nc.dram_tensor(f"ys{n}", (NSLOT * P, D), F32, kind="Internal").ap() for n in range(2)],
            "keys_dram": nc.dram_tensor("keys", (NB, P, XKV, S), BF16, kind="Internal").ap(),
            "wat_loaded": sem("wat_loaded"),
            "got": [[sem(f"got{k}_{t}") for t in range(NT // 2)] for k in range(2)],
            "ring_loaded": [sem(f"ring_loaded{n}") for n in range(2)],
        }

        def phase(f, *args, home=None):
            with ExitStack() as own:
                at, stop = home[1:] if home else (0, 0)
                used = [at]

                def scratch(name, shape, dt=F32):
                    n = int(np.prod(shape[1:]))
                    if used[0] + n > stop or dt != F32:
                        return own.enter_context(nc.sbuf_tensor(name, shape, dt))[:]
                    flat = g[home[0]][0:shape[0], used[0]:used[0] + n]
                    used[0] += n
                    if len(shape) == 2:
                        return flat
                    axes = "abcd"[:len(shape) - 1]
                    return flat.rearrange(f"p ({' '.join(axes)}) -> p {' '.join(axes)}", **dict(zip(axes, shape[1:])))

                f(nc, g, sem, scratch, *args)

        spare = ("ring", CHUNK_W, 2 * CHUNK_W)
        phase(graph_phase)
        plan = [(attention_phase, LAYERS[0]), (route_phase, LAYERS[0]), (expert_phase, LAYERS[0]),
                (combine_phase, LAYERS[0]), (cross_phase,), (attention_phase, LAYERS[1]),
                (route_phase, LAYERS[1]), (expert_phase, LAYERS[1]), (combine_phase, LAYERS[1])]
        for f, *args in plan:
            home = {expert_phase: ("wat", 0, WA), cross_phase: ("ring", 0, 2 * CHUNK_W)}.get(f, spare)
            phase(f, *args, home=home)


def kernel(**inputs):
    import concourse.bacc as _bacc
    from concourse.bass_utils import run_bass_kernel_spmd as _run

    def tiles(a):
        return a.reshape(-1, P, a.shape[-1]).transpose(1, 0, 2)

    def blocks(w):
        return w.reshape(-1, P, w.shape[-1]).transpose(1, 0, 2).reshape(P, -1)

    def attention(n):
        return np.concatenate([blocks(inputs[f"L{n}_ffn_{k}"]) for k in ("wq", "wk", "wv", "wo")], axis=1)

    def experts(n):
        w1, w3, w2 = (inputs[f"L{n}_ffn_{k}"] for k in ("w1", "w3", "w2"))
        f = w1.shape[2]
        up = np.stack([w1, w3], axis=2).reshape(NE, KB, P, 2, f // CF, CF).transpose(4, 2, 0, 1, 3, 5)
        down = w2.reshape(NE, f // CF, CF // P, P, D).transpose(1, 3, 0, 2, 4)
        return np.concatenate([up.reshape(f // CF, P, NE, -1), down.reshape(f // CF, P, NE, -1)], axis=3).reshape(f // CF, P, CHUNK_W)

    inputs = {k: np.asarray(v) for k, v in inputs.items()}
    ctx2 = inputs["ctx_512"].reshape(NB * S, CD)
    ctx_t = ctx2.T
    rep = np.zeros((NB, P // XR, XR, XKV, S), np.float32)
    by_head = ctx_t.reshape(XKV, XD, NB, S).transpose(2, 1, 0, 3)
    rep[:, :, :len(PARTS_K) * XD] = np.tile(by_head, (1, len(PARTS_K), 1, 1))[:, None]
    rep[:, :, len(PARTS_K) * XD:len(PARTS_K) * XD + 3] = 1.0
    rep = rep.reshape(NB, P, XKV * S)
    small = np.concatenate(
        [inputs[k].reshape(KB, P).T for k in ("L0_ffn_norm1_w", "L0_ffn_norm2_w", "L1_ffn_ln1_w", "L1_ffn_ln2_w")]
        + [blocks(inputs[f"L{n}_ffn_gate_w"]) for n in range(2)]
        + [np.broadcast_to(inputs["L0_xattn_gamma_raw"].reshape(1, 1), (P, 1))], axis=1)
    data = {
        "x_in": tiles(inputs["x"].reshape(NB * S, D)), "ctx_t": ctx_t, "ctx_tok": tiles(ctx2), "ctx_rep": rep,
        "wqk": np.concatenate([inputs["L0_xattn_Wq"].T, inputs["L0_xattn_Wk"].T], axis=1), "small": small,
        "const": constants(), "wa0": attention(0), "wa1": attention(1), "wm0": experts(0), "wm1": experts(1),
    }
    nc = _bacc.Bacc("TRN2", target_bir_lowering=False, num_devices=1)
    arrays, args = {}, []
    for name, a in data.items():
        arrays[name] = np.ascontiguousarray(a)
        args.append(nc.dram_tensor(name, a.shape, F32, kind="ExternalInput").ap())
    res = nc.dram_tensor("result", (P, NT, D), F32, kind="ExternalOutput").ap()
    program(nc, *args, res)
    r = _run(nc, [arrays], core_ids=[0])
    return r.results[0]["result"].transpose(1, 0, 2).reshape(NB, S, D)
```

```python
from contextlib import ExitStack

import numpy as np

import concourse.bass as bass
from concourse import mybir

F32 = mybir.dt.float32
I32 = mybir.dt.int32
U32 = mybir.dt.uint32
BF16 = mybir.dt.bfloat16
F32R = mybir.dt.float32r
ALU = mybir.AluOpType
ACT = mybir.ActivationFunctionType
AX_X = mybir.AxisListType.X

P = 128
NB, S, D = 4, 256, 256
CD = 64
NT = NB * S // P
KB = D // P
TS = S // P
EPS = 1e-5

TOPK_SIM = int(S * 0.3)
ROUNDS = -(-TOPK_SIM // 8)
GH, GD = 4, 16

XKV, XG, XD = 8, 4, 8
XV = XD + 1
XR = 64
PARTS_K = (0, 1, 2, 0, 1, 0)

NE = 8
CF = 256
NSLOT = (2 * NB * S + NE * (P - 1)) // P
EW = KB * 2 * CF + CF // P * D
CHUNK_W = NE * EW
NEG = -1.0e30

QW, KW = 2048, 512
OB = QW // P
WK0, WV0, WO0 = KB * QW, KB * (QW + KW), KB * (QW + 2 * KW)
WA = WO0 + OB * D
PIECE = KB * 2 * KW
PIECES = (WK0, 0, PIECE, WO0, WO0 + PIECE)


class Layer:

    def __init__(self, n, heads, kv, f, rope, act):
        self.n, self.heads, self.kv, self.rope, self.act = n, heads, kv, rope, act
        self.hd = QW // heads
        self.units = heads // 2
        self.kunits = kv // 2
        self.scale = float(1.0 / np.sqrt(self.hd))
        self.chunks = f // CF
        self.steps = self.chunks * NSLOT


LAYERS = [Layer(0, 16, 4, 512, True, ACT.Silu), Layer(1, 32, 8, 1024, False, ACT.Relu)]

C_ID, C_TRI, C_ONE, C_MASK, C_COS, C_SIN = 0, 128, 256, 384, 640, 896
C_GM, C_IOTA, C_THR, C_TILE, C_HALF, C_M1, C_M2, C_END = 1152, 1156, 1164, 1172, 1196, 1212, 1213, 1214
W_N, W_G, W_GAM, W_END = 0, 8, 40, 41


def constants():
    c = np.zeros((P, C_END), np.float32)
    c[:, C_ID:C_ID + P] = np.eye(P)
    c[:, C_TRI:C_TRI + P] = np.triu(np.ones((P, P)), 1)
    c[:, C_ONE:C_ONE + P] = 1.0
    c[:, C_MASK + P:C_MASK + 2 * P] = np.triu(np.full((P, P), NEG), 1)
    half = P // 2
    freq = (np.float32(1.0) / np.float32(1000000.0) ** (np.arange(0, P, 2, dtype=np.float32) / np.float32(P)))
    ang = (np.arange(S, dtype=np.float32)[:, None] * freq.astype(np.float32)[None, :]).astype(np.float32).T
    c[:, C_COS:C_COS + S] = np.concatenate([np.cos(ang)] * 2)
    c[:half, C_SIN:C_SIN + S] = np.sin(ang)
    c[half:, C_SIN:C_SIN + S] = -np.sin(ang)
    part = np.zeros(XR, np.int64)
    part[:len(PARTS_K) * XD] = np.repeat(PARTS_K, XD)
    c[:, C_M1] = np.tile(np.where(part >= 1, -1.0, 0.0), P // XR)
    c[:, C_M2] = np.tile(np.where(part == 2, -1.0, 0.0), P // XR)
    c[:, C_IOTA:C_IOTA + NE] = np.arange(NE)
    c[:, C_THR:C_THR + NT] = P * np.arange(NT)
    c[:, C_TILE:C_TILE + 24] = np.arange(24)
    c[:, C_HALF:C_HALF + 2 * NT] = -0.5
    return c


def load_pieces(sp, g, layer):
    for p, dest in enumerate((g["stage"][0][:], g["stage"][1][:], g["y"][:].rearrange("p t d -> p (t d)"))):
        sp.dma_start(dest, g["wa_in"][layer][:, PIECES[p]:PIECES[p] + PIECE]).then_inc(g["piece_loaded"][p], 16)


def graph_phase(nc, g, sem, scratch):
    x, con, sm, mv, qd, bank = g["x"], g["con"], g["sm"], g["mv"], g["qd"], g["bank"]
    ident = con[:, C_ID:C_ID + P]
    qk = scratch("g_qk", [CD, 2 * S])
    sim = [[scratch(f"g_sim{i}_{u}", [P, S]) for u in range(TS)] for i in range(2)]
    sig = [[scratch(f"g_sig{i}_{u}", [P, S]) for u in range(TS)] for i in range(2)]
    left = [scratch(f"g_left{u}", [P, S]) for u in range(TS)]
    top = [scratch(f"g_top{u}", [P, ROUNDS, 8]) for u in range(TS)]
    stat = scratch("g_stat", [P, NT, 6])
    gam = scratch("g_gam", [P, 3])
    norm = scratch("g_norm", [P, TS, D])
    ctx_t = scratch("g_ctxT", [CD, NB * S])
    wqk = scratch("g_wqk", [CD, 2 * CD])
    loaded = sem("g_loaded")
    x_in = sem("g_x_in")
    zeroed = sem("g_zeroed")
    stored = sem("g_stored")
    gate = sem("g_gate")
    stats = sem("g_stats")
    rstd = sem("g_rstd")
    q_mm = sem("g_q_mm")
    q_sb = sem("g_q_sb")
    s_mm = sem("g_s_mm")
    s_sb = sem("g_s_sb")
    pick = sem("g_pick")
    a_t = sem("g_a_t")
    mix = sem("g_mix")
    psS = [bank[1:3], bank[4:6]]
    QK = TS * (2 * ROUNDS - 1) + TS
    MX = 2 * TS + 2

    with nc.Block() as block:
        @block.sync
        def _(sp):
            sp.dma_start(wqk[:], g["wqk_in"]).then_inc(loaded, 16)
            sp.dma_start(ctx_t[:], g["ctx_t_in"]).then_inc(loaded, 16)
            sp.dma_start(con[:], g["const_in"]).then_inc(loaded, 16)
            sp.dma_start(sm[:], g["small_in"]).then_inc(x_in, 16)
            sp.dma_start(x[:], g["x_in"]).then_inc(x_in, 16)
            load_pieces(sp, g, 0)
            sp.wait_ge(zeroed, 1)
            for n in range(2):
                sp.dma_start(g["xs_dram"][n].rearrange("(t p) d -> p t d", p=P),
                             g["zero"][:].rearrange("p (o d) -> p o d", o=1).to_broadcast([P, NSLOT, D])
                             ).then_inc(stored, 16)
            sp.wait_ge(stored, 32)

        @block.gpsimd
        def _(pool):
            nc.gpsimd.memset(g["zero"][:], 0.0).then_inc(zeroed, 1)
            pool.wait_ge(loaded, 48)
            pool.wait_ge(stats, 2 * NT + 1)
            nc.gpsimd.tensor_tensor(qd[:, 1, :], qd[:, 0, :], con[:, C_HALF:C_HALF + NT], ALU.pow).then_inc(rstd, 1)

        @block.tensor
        def _(pe):
            pe.wait_ge(loaded, 48)

            def similarities(b):
                pe.wait_ge(q_sb, 2 * b)
                nc.tensor.matmul(bank[0][:, 0:S], wqk[:], ctx_t[:, b * S:(b + 1) * S],
                                 start=True, stop=True).then_inc(q_mm, 1)
                pe.wait_ge(q_sb, 2 * b + 2)
                if b >= 2:
                    pe.wait_ge(s_sb, (b - 1) * 2 * TS)
                for u in range(TS):
                    nc.tensor.matmul(psS[b % 2][u][:, 0:S], qk[:, u * P:(u + 1) * P], qk[:, S:2 * S],
                                     start=True, stop=True).then_inc(s_mm, 1)

            similarities(0)
            for b in range(NB):
                if b + 1 < NB:
                    similarities(b + 1)
                pe.wait_ge(pick, (b + 1) * QK)
                pe.wait_ge(mix, b * MX)
                for u in range(TS):
                    for v in range(TS):
                        mm = nc.tensor.transpose(bank[3][:, v * S + u * P:v * S + (u + 1) * P],
                                                 left[u][:, v * P:(v + 1) * P], ident)
                mm.then_inc(a_t, 1)

        @block.scalar
        def _(act):
            scale = float(1.0 / (np.sqrt(GD) * GH))
            for b in range(NB):
                act.wait_ge(q_mm, b + 1)
                act.wait_ge(s_mm, b * TS)
                for i in range(2):
                    nc.scalar.activation(qk[:, i * S:(i + 1) * S], bank[0][i * CD:(i + 1) * CD, 0:S],
                                         ACT.Copy).then_inc(q_sb, 1)
                for u in range(TS):
                    act.wait_ge(s_mm, b * TS + u + 1)
                    if b >= 2:
                        act.wait_ge(pick, (b - 1) * QK)
                    nc.scalar.activation(sim[b % 2][u][:], psS[b % 2][u][:, 0:S], ACT.Copy, scale=scale).then_inc(s_sb, 1)
                    nc.scalar.activation(sig[b % 2][u][:], psS[b % 2][u][:, 0:S], ACT.Sigmoid, scale=scale).then_inc(s_sb, 1)
                if b == 0:
                    act.wait_ge(x_in, 32)
                    nc.scalar.activation(gam[:, 0:1], sm[:, W_GAM:W_GAM + 1], ACT.Sigmoid).then_inc(gate, 1)

        @block.vector
        def _(dve):
            def normalizers():
                dve.wait_ge(x_in, 32)
                for t in range(NT):
                    nc.vector.bn_stats(stat[:, t, :], x[:, t, :]).then_inc(stats, 1)
                for t in range(NT):
                    dve.wait_ge(stats, t + 1)
                    nc.vector.bn_aggr(mv[:, t, :], stat[:, t, :]).then_inc(stats, 1)
                dve.wait_ge(stats, 2 * NT)
                nc.vector.tensor_scalar(qd[:, 0, :], mv[:, :, 1], EPS, None, ALU.add).then_inc(stats, 1)
                dve.wait_ge(gate, 1)
                nc.vector.tensor_scalar(gam[:, 1:2], gam[:, 0:1], -1.0, 1.0, ALU.mult, ALU.add).then_inc(stats, 1)
                nc.vector.tensor_scalar(gam[:, 2:3], gam[:, 0:1], 0.5, None, ALU.mult).then_inc(stats, 1)
                dve.wait_ge(rstd, 1)
                dve.wait_ge(stats, 2 * NT + 3)
                nc.vector.tensor_scalar(qd[:, 2, :], qd[:, 1, :], gam[:, 1:2], None, ALU.mult).then_inc(stats, 1)
                dve.wait_ge(stats, 2 * NT + 4)
                nc.vector.scalar_tensor_tensor(out=qd[:, 3, :], in0=mv[:, :, 0], scalar=-1.0, in1=qd[:, 2, :],
                                               op0=ALU.mult, op1=ALU.mult).then_inc(stats, 1)
                dve.wait_ge(stats, 2 * NT + 5)

            for b in range(NB):
                n = 0
                dve.wait_ge(s_sb, (b + 1) * (2 * TS))
                dve.wait_ge(a_t, b)
                for r in range(ROUNDS):
                    for u in range(TS):
                        dve.wait_ge(pick, b * QK + max(n - 1, 0))
                        nc.vector.max(top[u][:, r, :], (sim[b % 2] if r == 0 else left)[u][:]).then_inc(pick, 1)
                        n += 1
                    for u in range(TS):
                        if r < ROUNDS - 1:
                            dve.wait_ge(pick, b * QK + n - 1)
                            nc.vector.match_replace(left[u][:], top[u][:, r, :], (sim[b % 2] if r == 0 else left)[u][:],
                                                    NEG).then_inc(pick, 1)
                            n += 1
                last = (TOPK_SIM - 1) % 8
                for u in range(TS):
                    dve.wait_ge(pick, b * QK + n - 1)
                    nc.vector.scalar_tensor_tensor(out=left[u][:], in0=sim[b % 2][u][:], scalar=top[u][:, ROUNDS - 1, last:last + 1],
                                                   in1=sig[b % 2][u][:], op0=ALU.is_ge, op1=ALU.mult).then_inc(pick, 1)
                    n += 1
                assert n == QK
                if b == 0:
                    normalizers()
                for u in range(TS):
                    dve.wait_ge(mix, b * MX)
                    nc.vector.tensor_scalar(norm[:, u, :], x[:, b * TS + u, :],
                                            qd[:, 2, b * TS + u:b * TS + u + 1], qd[:, 3, b * TS + u:b * TS + u + 1],
                                            ALU.mult, ALU.add).then_inc(mix, 1)
                dve.wait_ge(a_t, b + 1)
                dve.wait_ge(mix, b * MX + TS)
                pair = norm[:].rearrange("p t d -> p (t d)")
                nc.vector.scalar_tensor_tensor(out=pair, in0=bank[3][:], scalar=gam[:, 2:3], in1=pair,
                                               op0=ALU.mult, op1=ALU.add).then_inc(mix, 1)
                dve.wait_ge(mix, b * MX + TS + 1)
                for u in range(TS):
                    nc.vector.scalar_tensor_tensor(out=norm[:, u, :], in0=left[u][:], scalar=gam[:, 2:3],
                                                   in1=norm[:, u, :], op0=ALU.mult, op1=ALU.add).then_inc(mix, 1)
                dve.wait_ge(mix, b * MX + 2 * TS + 1)
                xb = x[:, b * TS:(b + 1) * TS, :].rearrange("p t d -> p (t d)")
                nc.vector.tensor_tensor(xb, xb, pair, ALU.add).then_inc(mix, 1)
                dve.wait_ge(mix, (b + 1) * MX)
                for u in range(TS):
                    tile_stats(nc, g, "x", b * TS + u)


def tile_stats(nc, g, source, tile):
    at = slice(tile, tile + 1) if isinstance(tile, int) else bass.ds(tile, 1)
    return nc.vector.bn_stats(g["stat"][:, at, :].rearrange("p o s -> p (o s)"),
                              g[source][:, at, :].rearrange("p o d -> p (o d)"))


class Norm:

    def __init__(self, nc, g, sem, tag, source, mode, weight=None, banks=()):
        self.nc, self.g, self.source, self.mode, self.weight, self.banks = nc, g, source, mode, weight, banks
        self.steps = sem(f"{tag}_steps")
        self.powed = sem(f"{tag}_powed")
        if mode != "ln":
            self.turned = sem(f"{tag}_turned")
            self.in_yt = sem(f"{tag}_in_yt")
        self.first = NT + {"ln": 1, "rms": 3, "ln+rms": 4}[mode]
        self.scaled = self.first + {"ln": 1, "rms": 0, "ln+rms": 3}[mode]
        self.end = self.scaled + NT
        if mode == "ln+rms":
            self.kept = sem(f"{tag}_kept")

    def rows(self, tile):
        return self.scaled + tile + 1

    def pool(self, pool):
        qd, con, nc = self.g["qd"], self.g["con"], self.nc
        n = 2 if self.mode == "ln+rms" else 1
        pool.wait_ge(self.steps, self.first)
        nc.gpsimd.tensor_tensor(qd[:, 2:2 + n, :], qd[:, 0:n, :],
                                con[:, C_HALF:C_HALF + n * NT].rearrange("p (n t) -> p n t", n=n),
                                ALU.pow).then_inc(self.powed, 1)

    def vector(self, dve):
        nc, g, mode, steps = self.nc, self.g, self.mode, self.steps
        mv, qd, xn, src = (g[k] for k in ("mv", "qd", "xn", self.source))
        mean, var, n = mv[:, :, 0], mv[:, :, 1], NT
        for t in range(NT):
            nc.vector.bn_aggr(mv[:, t, :], g["stat"][:, t, :]).then_inc(steps, 1)
        dve.wait_ge(steps, n)
        if mode == "rms":
            nc.vector.tensor_tensor(qd[:, 6, :], mean, mean, ALU.mult).then_inc(steps, 1)
            dve.wait_ge(steps, n + 1)
            nc.vector.tensor_tensor(qd[:, 7, :], qd[:, 6, :], var, ALU.add).then_inc(steps, 1)
            dve.wait_ge(steps, n + 2)
            nc.vector.tensor_scalar(qd[:, 0, :], qd[:, 7, :], EPS, None, ALU.add).then_inc(steps, 1)
        else:
            nc.vector.tensor_scalar(qd[:, 0, :], var, EPS, None, ALU.add).then_inc(steps, 1)
        if mode == "ln+rms":
            dve.wait_ge(steps, n + 1)
            nc.vector.reciprocal(qd[:, 6, :], qd[:, 0, :]).then_inc(steps, 1)
            dve.wait_ge(steps, n + 2)
            nc.vector.tensor_tensor(qd[:, 7, :], qd[:, 6, :], var, ALU.mult).then_inc(steps, 1)
            dve.wait_ge(steps, n + 3)
            nc.vector.tensor_scalar(qd[:, 1, :], qd[:, 7, :], EPS, None, ALU.add).then_inc(steps, 1)
        dve.wait_ge(self.powed, 1)
        n = self.first
        if mode == "ln":
            nc.vector.scalar_tensor_tensor(out=qd[:, 5, :], in0=mean, scalar=-1.0, in1=qd[:, 2, :],
                                           op0=ALU.mult, op1=ALU.mult).then_inc(steps, 1)
            scale, shift = 2, 5
        elif mode == "ln+rms":
            nc.vector.tensor_tensor(qd[:, 4, :], qd[:, 2, :], qd[:, 3, :], ALU.mult).then_inc(steps, 1)
            nc.vector.scalar_tensor_tensor(out=qd[:, 6, :], in0=mean, scalar=-1.0, in1=qd[:, 2, :],
                                           op0=ALU.mult, op1=ALU.mult).then_inc(steps, 1)
            dve.wait_ge(steps, n + 1)
            nc.vector.scalar_tensor_tensor(out=qd[:, 5, :], in0=mean, scalar=-1.0, in1=qd[:, 4, :],
                                           op0=ALU.mult, op1=ALU.mult).then_inc(steps, 1)
            scale, shift = 4, 5
        else:
            scale, shift = 2, None
        dve.wait_ge(steps, self.scaled)
        for t in range(NT):
            if shift is None:
                nc.vector.tensor_scalar(xn[:, t, :], src[:, t, :], qd[:, scale, t:t + 1], None, ALU.mult).then_inc(steps, 1)
            else:
                nc.vector.tensor_scalar(xn[:, t, :], src[:, t, :], qd[:, scale, t:t + 1], qd[:, shift, t:t + 1],
                                        ALU.mult, ALU.add).then_inc(steps, 1)

    def tensor(self, pe):
        for q in range(NT // 4):
            pe.wait_ge(self.steps, self.rows(4 * q + 3))
            for k in range(KB):
                for j in range(4):
                    mm = self.nc.tensor.transpose(self.g["bank"][self.banks[q * KB + k]][:, j * P:(j + 1) * P],
                                                  self.g["xn"][:, 4 * q + j, k * P:(k + 1) * P],
                                                  self.g["con"][:, C_ID:C_ID + P])
                mm.then_inc(self.turned, 1)

    def scalar(self, act):
        for q in range(NT // 4):
            for k in range(KB):
                w = W_N + self.weight * KB + k
                act.wait_ge(self.turned, q * KB + k + 1)
                self.nc.scalar.activation(self.g["yT"][:, k, q * 4 * P:(q + 1) * 4 * P],
                                          self.g["bank"][self.banks[q * KB + k]][:], ACT.Copy,
                                          scale=self.g["sm"][:, w:w + 1]).then_inc(self.in_yt, 1)

    def keep(self, act, free, value):
        if self.mode == "ln+rms":
            qd = self.g["qd"]
            act.wait_ge(self.steps, self.end)
            act.wait_ge(free, value)
            for t in range(NT):
                self.nc.scalar.activation(self.g["y"][:, t, :], self.g[self.source][:, t, :], ACT.Identity,
                                          scale=qd[:, 2, t:t + 1], bias=qd[:, 6, t:t + 1]).then_inc(self.kept, 1)


def attention_phase(nc, g, sem, scratch, lay):
    con, bank, yT, y = (g[k] for k in ("con", "bank", "yT", "y"))
    ident = con[:, C_ID:C_ID + P]
    tag, hd, U, KU = f"a{lay.n}", lay.hd, lay.units, lay.kunits
    NPR = KU + U
    group = lay.heads // lay.kv
    W = 3 * P
    wat = [scratch(f"{tag}_w{i}", [P, WA], F32R) for i in range(2)]
    yb = [scratch(f"{tag}_yb{i}", [P, KB, S], F32R) for i in range(2)]
    oT = [scratch(f"{tag}_oT{i}", [P, OB, S], F32R) for i in range(2)]
    TERMS = ((0, 0), (0, 1), (1, 0))
    kT = scratch(f"{tag}_kT", [P, lay.kv, S])
    v = scratch(f"{tag}_v", [P, TS, KW])
    qT = [scratch(f"{tag}_qT{i}", [P, 2 * hd // P, S]) for i in range(3)]
    rot = [scratch(f"{tag}_rot{i}", [P, 2, S]) for i in range(2)] if lay.rope else None
    pr = [scratch(f"{tag}_p{i}", [P, 2, W]) for i in range(3)]
    prT = [scratch(f"{tag}_pT{i}", [P, 2, W]) for i in range(2)]
    nmax = [scratch(f"{tag}_nmax{i}", [P, 4]) for i in range(3)]
    total = [scratch(f"{tag}_sum{i}", [P, 4]) for i in range(3)]
    rinv = [scratch(f"{tag}_rinv{i}", [P, 4]) for i in range(3)]
    idle = scratch(f"{tag}_idle", [P, 1])
    waited = sem(f"{tag}_waited")
    yb_ok = sem(f"{tag}_yb")
    proj = sem(f"{tag}_proj")
    v_mm = sem(f"{tag}_v_mm")
    v_sb = sem(f"{tag}_v_sb")
    taken = sem(f"{tag}_taken")
    ready = sem(f"{tag}_ready") if lay.rope else taken
    s_mm = sem(f"{tag}_s_mm")
    s_rd = sem(f"{tag}_s_rd")
    expd = sem(f"{tag}_exp")
    inv = sem(f"{tag}_inv")
    p_ok = sem(f"{tag}_p_ok")
    t_mm = sem(f"{tag}_t_mm")
    t_sb = sem(f"{tag}_t_sb")
    o_mm = sem(f"{tag}_o_mm")
    o_sb = sem(f"{tag}_o_sb")
    o_lo = sem(f"{tag}_o_lo")
    w_hi = sem(f"{tag}_w_hi")
    w_lo = [sem(f"{tag}_w_lo{p}") for p in range(len(PIECES))]
    POOLS = (0,) if lay.rope else (0, 2, 3, 4)
    w_mm = sem(f"{tag}_w_mm")
    w_rd = sem(f"{tag}_w_rd")
    psQ, psS, psT, psO, psW = [bank[0], bank[7]], bank[1:3], bank[3:5], bank[5], bank[6]
    norm = Norm(nc, g, sem, f"n{lay.n}", "x", "ln+rms", 2 * lay.n, banks=(1, 2, 5, 6))
    landed = [g["stage"][0][:], g["stage"][1][:], y[:].rearrange("p t d -> p (t d)"), g["stage"][0][:], g["stage"][1][:]]

    def high_part(act, p):
        act.wait_ge(g["piece_loaded"][p], 16 * (lay.n + 1))
        nc.scalar.activation(wat[0][:, PIECES[p]:PIECES[p] + PIECE], landed[p], ACT.Copy).then_inc(w_hi, 1)

    def low_part(engine, p):
        at = slice(PIECES[p], PIECES[p] + PIECE)
        engine.wait_ge(g["piece_loaded"][p], 16 * (lay.n + 1))
        engine.wait_ge(w_hi, p + 1)
        engine.tensor_tensor(wat[1][:, at], landed[p], wat[0][:, at].bitcast(F32), ALU.subtract).then_inc(w_lo[p], 1)
    TK = 3 if lay.rope else 1
    parts = [(0, P, C_MASK + P), (P, 2 * P, C_MASK)]

    with nc.Block() as block:
        @block.sync
        def _(sp):
            for p in (3, 4):
                sp.wait_ge(w_lo[p - 3], 1)
                sp.dma_start(landed[p], g["wa_in"][lay.n][:, PIECES[p]:PIECES[p] + PIECE]
                             ).then_inc(g["piece_loaded"][p], 16)

        @block.tensor
        def _(pe):
            norm.tensor(pe)
            pe.wait_ge(w_lo[0], 1)

            def batch(b, first, last):
                def project(n, b=b):
                    if n >= 2:
                        pe.wait_ge(taken, b * (NPR * TK) + (n - 1) * TK)
                    elif n == 0:
                        pe.wait_ge(taken, b * (NPR * TK))
                    for i in range(2):
                        if hd < P and i == 1:
                            continue
                        for k in range(KB):
                            at = WK0 + k * KW + 2 * n * hd + i * P if n < KU else k * QW + 2 * (n - KU) * hd + i * P
                            for wp, xp in TERMS:
                                mm = nc.tensor.matmul(psQ[n % 2][:, i * S:(i + 1) * S], wat[wp][:, at:at + P], yb[xp][:, k, :],
                                                      start=(k == 0 and wp + xp == 0), stop=(k == KB - 1 and wp == 1))
                    mm.then_inc(proj, 1)

                def scores(u):
                    pe.wait_ge(ready, b * NPR + KU + u + 1)
                    if u >= 1:
                        pe.wait_ge(s_rd, b * (4 * U) + 4 * u)
                    for i in range(2):
                        kv = (2 * u + i) // group
                        for r, (c0, n, _) in enumerate(parts):
                            if hd == P:
                                lhs, rhs = qT[u % 3][:, i, r * P:(r + 1) * P], kT[:, kv, 0:n]
                            else:
                                half = slice(i * hd, (i + 1) * hd)
                                lhs, rhs = qT[u % 3][half, 0, r * P:(r + 1) * P], kT[half, kv, 0:n]
                            mm = nc.tensor.matmul(psS[i][:, c0:c0 + n], lhs, rhs, start=True, stop=True)
                        mm.then_inc(s_mm, 1)

                def turn(u):
                    pe.wait_ge(p_ok, b * (4 * U) + 4 * u + 4)
                    for i in range(2):
                        if u >= 1:
                            pe.wait_ge(t_sb, b * (2 * U) + 2 * u - 1 + i)
                        else:
                            pe.wait_ge(v_sb, b * TS + 1 + i)
                        for j in range(3):
                            mm = nc.tensor.transpose(psT[i][:, j * P:(j + 1) * P], pr[u % 3][:, i, j * P:(j + 1) * P], ident)
                        mm.then_inc(t_mm, 1)

                def values(u, first=first):
                    pe.wait_ge(t_sb, b * (2 * U) + 2 * u + 2)
                    if u >= 1:
                        pe.wait_ge(o_lo, b * U + u)
                    elif not first:
                        pe.wait_ge(o_lo, b * U)
                    for i in range(2):
                        kv = (2 * u + i) // group
                        o = psO[:, i * S:(i + 1) * S] if hd == P else psO[i * hd:(i + 1) * hd, 0:S]
                        nc.tensor.matmul(o, v[:, 0, kv * hd:(kv + 1) * hd], prT[u % 2][:, i, 0:2 * P],
                                         start=True, stop=False)
                        mm = nc.tensor.matmul(o[:, P:2 * P], v[:, 1, kv * hd:(kv + 1) * hd], prT[u % 2][:, i, 2 * P:3 * P],
                                              start=False, stop=True)
                    mm.then_inc(o_mm, 1)

                def all_values(b):
                    for t in range(TS):
                        pe.wait_ge(t_sb, b * (2 * U))
                        for k in range(KB):
                            for wp, xp in TERMS:
                                mm = nc.tensor.matmul(psT[t][:, 0:KW], yb[xp][:, k, t * P:(t + 1) * P],
                                                      wat[wp][:, WV0 + k * KW:WV0 + (k + 1) * KW],
                                                      start=(k == 0 and wp + xp == 0), stop=(k == KB - 1 and wp == 1))
                        mm.then_inc(v_mm, 1)

                if first:
                    pe.wait_ge(yb_ok, 2)
                    for n in range(KU):
                        project(n)
                    all_values(b)
                    pe.wait_ge(w_lo[1], 1)
                    pe.wait_ge(w_lo[2], 1)
                    project(KU)
                    project(KU + 1)
                    pe.wait_ge(norm.in_yt, 2 * KB)
                for u in range(U + 3):
                    if u < U:
                        scores(u)
                    if u + 2 < U:
                        project(KU + u + 2)
                    if u < TS and not first:
                        output(b - 1, u)
                    if 2 <= u < U + 2:
                        turn(u - 2)
                    if u > U and not last:
                        project(KU + u - U - 1, b + 1)
                    if u >= 3:
                        values(u - 3)
                    if u == U and not last:
                        pe.wait_ge(yb_ok, 2 * b + 4)
                        for n in range(KU):
                            project(n, b + 1)
                if not last:
                    all_values(b + 1)

            def output(b, t):
                if t == 0:
                    pe.wait_ge(w_rd, b)
                    pe.wait_ge(o_lo, b * U + U)
                    pe.wait_ge(w_lo[3], 1)
                    pe.wait_ge(w_lo[4], 1)
                for c in range(OB):
                    for wp, xp in TERMS:
                        mm = nc.tensor.matmul(psW[:, t * D:(t + 1) * D], oT[xp][:, c, t * P:(t + 1) * P],
                                              wat[wp][:, WO0 + c * D:WO0 + (c + 1) * D],
                                              start=(c == 0 and wp + xp == 0), stop=(c == OB - 1 and wp == 1))
                if t == TS - 1:
                    mm.then_inc(w_mm, 1)

            batch(0, True, False)
            with pe.Fori(1, NB - 1) as b:
                batch(b, False, False)
            batch(NB - 1, False, True)
            for t in range(TS):
                output(NB - 1, t)

        @block.scalar
        def _(act):
            for p in range(3):
                high_part(act, p)
            norm.scalar(act)
            norm.keep(act, w_lo[2], 1)

            def batch(b, first):
                for t in range(TS):
                    act.wait_ge(v_mm, b * TS + t + 1)
                    act.wait_ge(o_mm, b * U)
                    nc.scalar.activation(v[:, t, :], psT[t][:], ACT.Copy).then_inc(v_sb, 1)
                for u in range(U + 3):
                    if u < U:
                        for i in range(2):
                            for r, (c0, n, _) in enumerate(parts):
                                act.wait_ge(s_rd, b * (4 * U) + 4 * u + 2 * i + r + 1)
                                p = pr[u % 3][:, i, c0:c0 + n]
                                k = 2 * i + r
                                nc.scalar.activation(p, p, ACT.Exp, scale=-1.0, bias=nmax[u % 3][:, k:k + 1],
                                                     accum_out=total[u % 3][:, k:k + 1]).then_inc(expd, 1)
                    if 2 <= u < U + 2:
                        for i in range(2):
                            act.wait_ge(t_mm, b * (2 * U) + 2 * (u - 2) + i + 1)
                            if u >= 4:
                                act.wait_ge(o_mm, b * U + u - 3)
                            nc.scalar.activation(prT[u % 2][:, i, :], psT[i][:, 0:W], ACT.Copy).then_inc(t_sb, 1)
                    if u >= 3:
                        act.wait_ge(o_mm, b * U + u - 2)
                        if u == 3:
                            act.wait_ge(w_mm, b)
                        if hd == P:
                            nc.scalar.activation(oT[0][:, 2 * (u - 3):2 * (u - 2), :].rearrange("p h s -> p (h s)"), psO[:],
                                                 ACT.Copy).then_inc(o_sb, 1)
                        else:
                            nc.scalar.activation(oT[0][:, u - 3, :], psO[:, 0:S], ACT.Copy).then_inc(o_sb, 1)
                    if first and u in (3, 4):
                        high_part(act, u)

            batch(0, True)
            with act.Fori(1, NB) as b:
                batch(b, False)

        def dest(n):
            if n >= KU:
                return qT[(n - KU) % 3][:]
            return kT[:, 2 * n:2 * n + 2, :]

        @block.gpsimd
        def _(pool):
            norm.pool(pool)
            for p in POOLS:
                low_part(pool, p)

            def rope(b, n):
                if lay.rope:
                    pool.wait_ge(taken, b * (NPR * TK) + n * TK + TK)
                    nc.gpsimd.tensor_tensor(dest(n), dest(n), rot[n % 2][:], ALU.add).then_inc(ready, 1)

            def batch(b, first, last):
                if first:
                    for n in range(KU + 2):
                        rope(b, n)
                for u in range(U - 2):
                    rope(b, KU + u + 2)
                if not last:
                    for n in range(KU + 2):
                        rope(b + 1, n)

            batch(0, True, False)
            with pool.Fori(1, NB - 1) as b:
                batch(b, False, False)
            batch(NB - 1, False, True)

        @block.vector
        def _(dve):
            cos = con[:, C_COS:C_COS + S].rearrange("p (o s) -> p o s", o=1)
            sin = con[:, C_SIN:C_SIN + S].rearrange("p (o s) -> p o s", o=1)
            norm.vector(dve)

            def batch(b, first, last):
                def take(n, b=b):
                    dve.wait_ge(proj, b * NPR + n + 1)
                    ps = psQ[n % 2][:].rearrange("p (i s) -> p i s", i=2)
                    if n >= KU + 3:
                        dve.wait_ge(s_mm, b * (2 * U) + 2 * (n - KU - 2))
                    else:
                        dve.wait_ge(s_mm, b * (2 * U))
                    if not lay.rope:
                        if n >= KU:
                            nc.vector.tensor_copy(qT[(n - KU) % 3][:, 0, :], psQ[n % 2][:, 0:S]).then_inc(taken, 1)
                        else:
                            for i in range(2):
                                for half in range(2):
                                    cp = nc.vector.tensor_copy(kT[half * hd:(half + 1) * hd, 2 * n + i, :],
                                                               psQ[n % 2][i * hd:(i + 1) * hd, 0:S])
                            cp.then_inc(taken, 1)
                        return
                    if n >= 2:
                        dve.wait_ge(ready, b * NPR + n - 1)
                    h = P // 2
                    nc.vector.tensor_tensor(dest(n), ps, cos.to_broadcast([P, 2, S]), ALU.mult).then_inc(taken, 1)
                    nc.vector.tensor_tensor(rot[n % 2][0:h], ps[h:P], sin[h:P].to_broadcast([h, 2, S]),
                                            ALU.mult).then_inc(taken, 1)
                    nc.vector.tensor_tensor(rot[n % 2][h:P], ps[0:h], sin[0:h].to_broadcast([h, 2, S]),
                                            ALU.mult).then_inc(taken, 1)

                def features(b, first):
                    dve.wait_ge(norm.in_yt, (b // 2 + 1) * KB)
                    dve.wait_ge(v_mm, b * TS)
                    ybT = yT[:, :, bass.ds(b * S, S)] if not first else yT[:, :, 0:S]
                    nc.vector.tensor_copy(yb[0], ybT).then_inc(yb_ok, 1)
                    dve.wait_ge(yb_ok, 2 * b + 1)
                    nc.vector.tensor_tensor(yb[1], ybT, yb[0].bitcast(F32), ALU.subtract).then_inc(yb_ok, 1)

                def divide(u):
                    dve.wait_ge(expd, b * (4 * U) + 4 * u + 4)
                    nc.vector.reciprocal(rinv[u % 3][:], total[u % 3][:]).then_inc(inv, 1)
                    dve.wait_ge(inv, b * U + u + 1)
                    for i in range(2):
                        for r, (c0, n, _) in enumerate(parts):
                            k = 2 * i + r
                            p = pr[u % 3][:, i, c0:c0 + n]
                            nc.vector.tensor_scalar(p, p, rinv[u % 3][:, k:k + 1], None, ALU.mult).then_inc(p_ok, 1)

                def low_output(u):
                    dve.wait_ge(o_sb, b * U + u + 1)
                    o = oT[0][:, 2 * u:2 * u + 2, :].rearrange("p h s -> p (h s)") if hd == P else oT[0][:, u, :]
                    low = oT[1][:, 2 * u:2 * u + 2, :].rearrange("p h s -> p (h s)") if hd == P else oT[1][:, u, :]
                    ps = psO[:] if hd == P else psO[:, 0:S]
                    nc.vector.tensor_tensor(low, ps, o.bitcast(F32), ALU.subtract).then_inc(o_lo, 1)

                if first:
                    features(0, True)
                    for p in (1, 2):
                        if p not in POOLS:
                            low_part(dve, p)
                    for n in range(KU + 2):
                        take(n)
                for u in range(U):
                    if u == TS and not first:
                        add_output(b - 1)
                    if u >= 4:
                        low_output(u - 4)
                    if first and u in (4, 5) and u - 1 not in POOLS:
                        low_part(dve, u - 1)
                    for i in range(2):
                        dve.wait_ge(s_mm, b * (2 * U) + 2 * u + i + 1)
                        if u >= 3:
                            dve.wait_ge(t_mm, b * (2 * U) + 2 * (u - 2))
                        dve.wait_ge(waited, b * (2 * U) + 2 * u + i)
                        nc.vector.memset(idle, 0.0).then_inc(waited, 1)
                        for r, (c0, n, m) in enumerate(parts):
                            k = 2 * i + r
                            nc.vector.tensor_tensor_reduce(pr[u % 3][:, i, c0:c0 + n], psS[i][:, c0:c0 + n],
                                                           con[:, m:m + n], -lay.scale, 3.0e38, ALU.add, ALU.min,
                                                           nmax[u % 3][:, k:k + 1]).then_inc(s_rd, 1)
                    if u >= 1:
                        divide(u - 1)
                    if u + 2 < U:
                        take(KU + u + 2)
                    if u == U - 1 and not last:
                        features(b + 1, False)
                low_output(U - 4)
                divide(U - 1)
                low_output(U - 3)
                if not last:
                    for n in range(KU):
                        take(n, b + 1)
                low_output(U - 2)
                if not last:
                    for n in range(KU, KU + 2):
                        take(n, b + 1)
                low_output(U - 1)

            def add_output(b):
                dve.wait_ge(norm.kept, NT)
                dve.wait_ge(w_mm, b + 1)
                tiles = slice(b * TS, (b + 1) * TS) if isinstance(b, int) else bass.ds(b * TS, TS)
                yt = y[:, tiles, :].rearrange("p t d -> p (t d)")
                nc.vector.tensor_tensor(yt, yt, psW[:], ALU.add).then_inc(w_rd, 1)
                dve.wait_ge(w_rd, b + 1)
                for t in range(TS):
                    tile_stats(nc, g, "y", b * TS + t)

            batch(0, True, False)
            with dve.Fori(1, NB - 1) as b:
                batch(b, False, False)
            batch(NB - 1, False, True)
            add_output(NB - 1)


def key_rows(nc, g, sem, scratch):
    con = g["con"]
    rep = [scratch(f"k_rep{b}", [P, XKV * S]) for b in range(NB)]
    part = [scratch(f"k_part{b}", [P, XKV * S // 2]).bitcast(BF16) for b in range(NB)]
    loaded = [sem(f"k_loaded{b}") for b in range(NB)]
    rounded = sem("k_rounded")
    left = sem("k_left")
    stored = sem("k_stored")

    def fetch(sp):
        for b in range(NB):
            sp.dma_start(rep[b], g["ctx_rep_in"][b]).then_inc(loaded[b], 16)

    def store(sp):
        for b in range(NB):
            sp.wait_ge(left, NB + b + 1)
            sp.dma_start(g["keys_dram"][b].rearrange("p h t -> p (h t)"), part[b]).then_inc(stored, 16)
        sp.wait_ge(stored, NB * 16)

    def scalar(act, first, end):
        for n in range(first, end):
            b = n % NB
            act.wait_ge(loaded[b], 16)
            if n >= NB:
                act.wait_ge(left, b + 1)
            nc.scalar.activation(part[b], rep[b], ACT.Copy).then_inc(rounded, 1)

    def vector(dve, first, end):
        for n in range(first, end):
            b = n % NB
            mask = con[:, C_M1:C_M1 + 1] if n < NB else con[:, C_M2:C_M2 + 1]
            dve.wait_ge(loaded[b], 16)
            dve.wait_ge(rounded, n + 1)
            if n >= NB:
                dve.wait_ge(left, b + 1)
            nc.vector.scalar_tensor_tensor(out=rep[b] if n < NB else part[b], in0=part[b], scalar=mask, in1=rep[b],
                                           op0=ALU.mult, op1=ALU.add).then_inc(left, 1)

    return fetch, store, scalar, vector


def route_phase(nc, g, sem, scratch, lay):
    con, sm, bank, yT, xn, slot, wgt, offs = (g[k] for k in ("con", "sm", "bank", "yT", "xn", "slot", "wgt", "offs"))
    tag = f"r{lay.n}"
    logit = scratch(f"{tag}_logit", [P, NT, NE])
    best = scratch(f"{tag}_best", [P, NT, 8])
    arg = scratch(f"{tag}_arg", [P, NT, 8], U32)
    argf = scratch(f"{tag}_argf", [P, NT, 2])
    hot = [scratch(f"{tag}_hot{k}", [P, NT, NE]) for k in range(2)]
    both = scratch(f"{tag}_both", [P, NT, NE])
    before = scratch(f"{tag}_before", [P, NT + 1, NE])
    count = scratch(f"{tag}_count", [P, NE])
    fills = scratch(f"{tag}_fills", [P, NE, NT])
    tiles = scratch(f"{tag}_tiles", [P, NE])
    end = scratch(f"{tag}_end", [P, NE])
    start = scratch(f"{tag}_start", [P, NE])
    pos = scratch(f"{tag}_pos", [P, NT, NE])
    mine = scratch(f"{tag}_mine", [P, NT, NE])
    slotf = scratch(f"{tag}_slotf", [P, NT])
    passed = scratch(f"{tag}_passed", [1, NSLOT, NE])
    expert = scratch(f"{tag}_expert", [1, NSLOT])
    expert2 = scratch(f"{tag}_expert2", [1, NSLOT])
    gap = scratch(f"{tag}_gap", [P, NT])
    log_mm = sem(f"{tag}_log_mm")
    step = sem(f"{tag}_step")
    rank_mm = sem(f"{tag}_rank_mm")
    exp_ok = sem(f"{tag}_exp")
    slot_ok = sem(f"{tag}_slot_ok")
    sent = sem(f"{tag}_sent")
    BEFORE = {}

    def bc(ap, shape):
        return ap.to_broadcast(shape)

    norm = Norm(nc, g, sem, f"m{lay.n}", "y", "rms", 2 * lay.n + 1, banks=(2, 3, 4, 5))
    if lay.n == 0:
        fetch_keys, store_keys, round_keys, split_keys = key_rows(nc, g, sem, scratch)
    with nc.Block() as block:
        @block.sync
        def _(sp):
            if lay.n == 0:
                fetch_keys(sp)
            sp.dma_start(g["ring"][:, 0:CHUNK_W], g["wm_in"][lay.n][0]).then_inc(g["ring_loaded"][lay.n], 16)
            if lay.n == 0:
                store_keys(sp)

        @block.vector
        def _(dve):
            norm.vector(dve)
            if lay.n == 0:
                split_keys(dve, 0, 2)
            n = 0

            def then(ins):
                nonlocal n
                n += 1
                ins.then_inc(step, 1)
                dve.wait_ge(step, n)

            dve.wait_ge(log_mm, 1)
            then(nc.vector.tensor_copy(logit.rearrange("p t e -> p (t e)"), bank[0][:, 0:NT * NE]))
            for t in range(NT):
                n += 1
                nc.vector.max(best[:, t, :], logit[:, t, :]).then_inc(step, 1)
            first = n - NT
            for t in range(NT):
                dve.wait_ge(step, first + t + 1)
                n += 1
                nc.vector.max_index(arg[:, t, :], best[:, t, :], logit[:, t, :]).then_inc(step, 1)
            dve.wait_ge(step, n)
            then(nc.vector.tensor_tensor(gap, best[:, :, 1], best[:, :, 0], ALU.subtract))
            BEFORE["gap"] = n
            then(nc.vector.tensor_copy(argf, arg[:, :, 0:2]))
            iota = con[:, C_IOTA:C_IOTA + NE].rearrange("p (o e) -> p o e", o=1)
            for k in range(2):
                n += 1
                nc.vector.tensor_tensor(hot[k], bc(iota, [P, NT, NE]), bc(argf[:, :, k:k + 1], [P, NT, NE]),
                                        ALU.is_equal).then_inc(step, 1)
            dve.wait_ge(step, n)
            then(nc.vector.tensor_tensor(both, hot[0], hot[1], ALU.add))
            then(nc.vector.memset(before[:, 0, :], 0.0))
            for t in range(NT):
                then(nc.vector.tensor_tensor(before[:, t + 1, :], before[:, t, :], both[:, t, :], ALU.add))
            BEFORE["before"] = n
            dve.wait_ge(rank_mm, 1)
            then(nc.vector.tensor_copy(count, bank[1][:, NT * NE:(NT + 1) * NE]))
            thr = con[:, C_THR:C_THR + NT].rearrange("p (o k) -> p o k", o=1)
            then(nc.vector.tensor_tensor(fills, bc(count.rearrange("p (e o) -> p e o", o=1), [P, NE, NT]),
                                         bc(thr, [P, NE, NT]), ALU.is_gt))
            then(nc.vector.tensor_reduce(tiles, fills, AX_X, ALU.add))
            then(nc.vector.tensor_tensor_scan(end, con[:, C_ONE:C_ONE + NE], tiles, 0.0, ALU.mult, ALU.add))
            then(nc.vector.tensor_tensor(start, end, tiles, ALU.subtract))
            then(nc.vector.scalar_tensor_tensor(
                out=pos, in0=bc(start.rearrange("p (o e) -> p o e", o=1), [P, NT, NE]), scalar=float(P),
                in1=bank[1][:, 0:NT * NE].rearrange("p (t e) -> p t e", t=NT), op0=ALU.mult, op1=ALU.add))
            for k in range(2):
                then(nc.vector.tensor_tensor(mine, hot[k], pos, ALU.mult))
                then(nc.vector.tensor_reduce(slotf, mine, AX_X, ALU.add))
                nc.vector.tensor_copy(slot[k][:], slotf).then_inc(slot_ok, 1)
                dve.wait_ge(slot_ok, k + 1)
            then(nc.vector.tensor_tensor(
                passed, bc(end[0:1].rearrange("p (o e) -> p o e", o=1), [1, NSLOT, NE]),
                bc(con[0:1, C_TILE:C_TILE + NSLOT].rearrange("p (t o) -> p t o", o=1), [1, NSLOT, NE]), ALU.is_le))
            then(nc.vector.tensor_reduce(expert, passed, AX_X, ALU.add))
            then(nc.vector.tensor_scalar(expert2, expert, float(NE - 1), None, ALU.min))
            for c in range(lay.chunks):
                nc.vector.tensor_scalar(offs[:, c * NSLOT:(c + 1) * NSLOT], expert2, float(EW), float(c % 2 * CHUNK_W),
                                        ALU.mult, ALU.add).then_inc(step, 1)
            dve.wait_ge(exp_ok, 1)
            n += lay.chunks
            then(nc.vector.tensor_scalar(gap, wgt[:, 2, :], 1.0, None, ALU.add))
            then(nc.vector.reciprocal(wgt[:, 0, :], gap))
            then(nc.vector.tensor_tensor(wgt[:, 1, :], wgt[:, 2, :], wgt[:, 0, :], ALU.mult))
            if lay.n == 0:
                split_keys(dve, 2, 2 * NB)

        @block.scalar
        def _(act):
            norm.scalar(act)
            if lay.n == 0:
                round_keys(act, 0, 3)
            act.wait_ge(step, BEFORE["gap"])
            nc.scalar.activation(wgt[:, 2, :], gap, ACT.Exp).then_inc(exp_ok, 1)
            if lay.n == 0:
                round_keys(act, 3, 2 * NB)

        @block.tensor
        def _(pe):
            norm.tensor(pe)
            for t in range(NT):
                if t % 4 == 0:
                    pe.wait_ge(norm.in_yt, (t // 4 + 1) * KB)
                for k in range(KB):
                    w = W_G + (lay.n * KB + k) * NE
                    mm = nc.tensor.matmul(bank[0][:, t * NE:(t + 1) * NE], yT[:, k, t * P:(t + 1) * P], sm[:, w:w + NE],
                                          start=(k == 0), stop=(k == KB - 1))
            mm.then_inc(log_mm, 1)
            pe.wait_ge(step, BEFORE["before"])
            tri, ones = con[:, C_TRI:C_TRI + P], con[:, C_ONE:C_ONE + P]
            nc.tensor.matmul(bank[1][:, 0:NT * NE], tri, both.rearrange("p t e -> p (t e)"), start=True, stop=False)
            nc.tensor.matmul(bank[1][:, 0:NT * NE], ones, before[:, 0:NT, :].rearrange("p t e -> p (t e)"),
                             start=False, stop=True)
            nc.tensor.matmul(bank[1][:, NT * NE:(NT + 1) * NE], ones, before[:, NT, :],
                             start=True, stop=True).then_inc(rank_mm, 1)

        @block.gpsimd
        def _(pool):
            norm.pool(pool)
            pool.wait_ge(norm.steps, norm.end)
            for k in range(2):
                pool.wait_ge(slot_ok, k + 1)
                for t in range(NT):
                    nc.gpsimd.indirect_dma_start(
                        g["xs_dram"][lay.n], bass.IndirectOffsetOnAxis(ap=slot[k][:, t:t + 1], axis=0),
                        xn[:, t, :], None).then_inc(sent, 16)
            pool.wait_ge(sent, 2 * NT * 16)


def expert_phase(nc, g, sem, scratch, lay):
    con, sm, bank, ring, offs = (g[k] for k in ("con", "sm", "bank", "ring", "offs"))
    tag, NS, C = f"e{lay.n}", lay.steps, lay.chunks
    ident = con[:, C_ID:C_ID + P]
    acc = scratch(f"{tag}_acc", [P, NSLOT, D])
    xf = [scratch(f"{tag}_xf{i}", [P, KB, P]) for i in range(2)]
    up = [scratch(f"{tag}_up{i}", [P, CF]) for i in range(2)]
    hid = [scratch(f"{tag}_hid{i}", [P, CF]) for i in range(2)]
    hidT = [scratch(f"{tag}_hidT{i}", [P, CF // P, P]) for i in range(2)]
    xsT = scratch(f"{tag}_xsT", [P, NSLOT, KB, P])
    FB = CF // P
    UNROLL = 4
    PEELED = UNROLL + NS % UNROLL
    PARTS = [(0, 4), (4, 12), (12, NSLOT)]
    STORES = [(0, 12), (12, 20), (20, NSLOT)]
    GROUPS = [(a, min(a + 4, NSLOT)) for a in range(0, NSLOT, 4)]
    fetched = [sem(f"{tag}_fetched{i}") for i in range(len(PARTS))]
    turned = sem(f"{tag}_turned")
    in_xs0 = sem(f"{tag}_in_xs0")
    in_xs1 = sem(f"{tag}_in_xs1")
    cleared = sem(f"{tag}_cleared")
    xf_ok = sem(f"{tag}_xf")
    up_mm = sem(f"{tag}_up_mm")
    up_sb = sem(f"{tag}_up_sb")
    hid_ok = sem(f"{tag}_hid")
    hidt_mm = sem(f"{tag}_hidt_mm")
    hidt_sb = sem(f"{tag}_hidt_sb")
    dn_mm = sem(f"{tag}_dn_mm")
    added = sem(f"{tag}_added")
    stored = sem(f"{tag}_stored")
    loaded = g["ring_loaded"][lay.n]
    psH, psT, psD = bank[0:2], bank[2:4], bank[4:6]

    with nc.Block() as block:
        @block.sync
        def _(sp):
            xs = g["xs_dram"][lay.n].rearrange("(t p) d -> p t d", p=P)
            for i, (a, z) in enumerate(PARTS):
                sp.dma_start(acc[:, a:z, :], xs[:, a:z, :]).then_inc(fetched[i], 16)
            for c in range(1, C):
                if c == 1:
                    sp.wait_ge(fetched[-1], 16)
                if c >= 2:
                    sp.wait_ge(dn_mm, (c - 1) * NSLOT)
                sp.dma_start(ring[:, c % 2 * CHUNK_W:(c % 2 + 1) * CHUNK_W], g["wm_in"][lay.n][c]).then_inc(loaded, 16)
            ys = g["ys_dram"][lay.n].rearrange("(t p) d -> p t d", p=P)
            for a, z in STORES:
                sp.wait_ge(added, (C - 1) * NSLOT + z)
                sp.dma_start(ys[:, a:z, :], acc[:, a:z, :]).then_inc(stored, 16)
            sp.wait_ge(stored, 16 * len(STORES))

        @block.gpsimd
        def _(pool):
            pool.wait_ge(turned, KB * len(GROUPS))
            nc.gpsimd.memset(acc, 0.0).then_inc(cleared, 1)

        @block.tensor
        def _(pe):
            for q, (a, z) in enumerate(GROUPS):
                for i, (first, _) in enumerate(PARTS):
                    if a == first:
                        pe.wait_ge(fetched[i], 16)
                for k in range(KB):
                    if q >= 4:
                        pe.wait_ge((in_xs0, in_xs1)[k], q - 3)
                    for t in range(a, z):
                        mm = nc.tensor.transpose(bank[q % 4 * KB + k][:, (t - a) * P:(t - a + 1) * P],
                                                 acc[:, t, k * P:(k + 1) * P], ident)
                    mm.then_inc(turned, 1)

            def offset(s):
                return nc.tensor.value_load(offs[0:1, bass.ds(s, 1)], min_val=0, max_val=CHUNK_W + (NE - 1) * EW)

            def hidden(s, par):
                w = offset(s)
                pe.wait_ge(loaded, (s // NSLOT + 1) * 16)
                pe.wait_ge(xf_ok, s + 1)
                if not isinstance(s, int) or s >= 2:
                    pe.wait_ge(hid_ok, s - 1)
                for k in range(KB):
                    mm = nc.tensor.matmul(psH[par][:], xf[par][:, k, :], ring[:, bass.ds(w + k * 2 * CF, 2 * CF)],
                                          start=(k == 0), stop=(k == KB - 1))
                mm.then_inc(up_mm, 1)

            def turn(s, par):
                pe.wait_ge(hid_ok, s + 1)
                if not isinstance(s, int) or s >= 2:
                    pe.wait_ge(hidt_sb, s - 1)
                for k in range(FB):
                    mm = nc.tensor.transpose(psT[par][:, k * P:(k + 1) * P], hid[par][:, k * P:(k + 1) * P], ident)
                mm.then_inc(hidt_mm, 1)

            def down(s, par):
                w = offset(s)
                pe.wait_ge(hidt_sb, s + 1)
                if not isinstance(s, int) or s >= 2:
                    pe.wait_ge(added, s - 1)
                for k in range(FB):
                    mm = nc.tensor.matmul(psD[par][:, 0:D], hidT[par][:, k, :], ring[:, bass.ds(w + KB * 2 * CF + k * D, D)],
                                          start=(k == 0), stop=(k == FB - 1))
                mm.then_inc(dn_mm, 1)

            for s in range(PEELED):
                hidden(s, s % 2)
                if s >= 1:
                    turn(s - 1, (s - 1) % 2)
                if s >= 2:
                    down(s - 2, s % 2)
            with pe.Fori(0, (NS - PEELED) // UNROLL) as turns:
                s = turns * UNROLL + PEELED
                for i in range(UNROLL):
                    hidden(s + i, i % 2)
                    turn(s + (i - 1), (i - 1) % 2)
                    down(s + (i - 2), i % 2)
            turn(NS - 1, 1)
            down(NS - 2, 0)
            down(NS - 1, 1)

        @block.scalar
        def _(act):
            for q, (a, z) in enumerate(GROUPS):
                act.wait_ge(turned, KB * q + 1)
                w = W_N + (2 * lay.n + 1) * KB
                nc.scalar.activation(xsT[:, a:z, 0, :],
                                     bank[q % 4 * KB][:, 0:(z - a) * P].rearrange("p (t r) -> p t r", r=P),
                                     ACT.Copy, scale=sm[:, w:w + 1]).then_inc(in_xs0, 1)

            def activate(s, par):
                act.wait_ge(up_mm, s + 1)
                if not isinstance(s, int) or s >= 2:
                    act.wait_ge(hid_ok, s - 1)
                nc.scalar.activation(up[par], psH[par][:, 0:CF], lay.act).then_inc(up_sb, 1)

            def take(s, par):
                act.wait_ge(hidt_mm, s + 1)
                if not isinstance(s, int) or s >= 2:
                    act.wait_ge(dn_mm, s - 1)
                nc.scalar.activation(hidT[par].rearrange("p k t -> p (k t)"), psT[par][:, 0:CF], ACT.Copy).then_inc(hidt_sb, 1)

            for s in range(PEELED):
                activate(s, s % 2)
                if s >= 1:
                    take(s - 1, (s - 1) % 2)
            with act.Fori(0, (NS - PEELED) // UNROLL) as turns:
                s = turns * UNROLL + PEELED
                for i in range(UNROLL):
                    activate(s + i, i % 2)
                    take(s + (i - 1), (i - 1) % 2)
            take(NS - 1, 1)

        @block.vector
        def _(dve):
            for q, (a, z) in enumerate(GROUPS):
                dve.wait_ge(turned, KB * q + 2)
                w = W_N + (2 * lay.n + 1) * KB + 1
                nc.vector.tensor_scalar(xsT[:, a:z, 1, :],
                                        bank[q % 4 * KB + 1][:, 0:(z - a) * P].rearrange("p (t r) -> p t r", r=P),
                                        sm[:, w:w + 1], None, ALU.mult).then_inc(in_xs1, 1)
            dve.wait_ge(in_xs0, len(GROUPS))
            dve.wait_ge(in_xs1, len(GROUPS))

            def fixed(s, par):
                if not isinstance(s, int) or s >= 2:
                    dve.wait_ge(up_mm, s - 1)
                t = s % NSLOT
                nc.vector.tensor_copy(xf[par], xsT[:, bass.ds(t, 1), :, :].rearrange("p o k t -> p (o k) t")).then_inc(xf_ok, 1)

            def hide(s, par):
                dve.wait_ge(up_sb, s + 1)
                if not isinstance(s, int) or s >= 2:
                    dve.wait_ge(hidt_mm, s - 1)
                nc.vector.tensor_tensor(hid[par], up[par], psH[par][:, CF:2 * CF], ALU.mult).then_inc(hid_ok, 1)

            def gather(s, par):
                dve.wait_ge(dn_mm, s + 1)
                if not isinstance(s, int) or s >= NSLOT:
                    dve.wait_ge(added, (s - NSLOT + 1) if isinstance(s, int) else s - 1)
                t = acc[:, bass.ds(s % NSLOT, 1), :].rearrange("p o d -> p (o d)")
                nc.vector.tensor_tensor(t, t, psD[par][:, 0:D], ALU.add).then_inc(added, 1)

            fixed(0, 0)
            for s in range(PEELED):
                fixed(s + 1, (s + 1) % 2)
                hide(s, s % 2)
                if s == 2:
                    dve.wait_ge(cleared, 1)
                if s >= 2:
                    gather(s - 2, s % 2)
            with dve.Fori(0, (NS - PEELED) // UNROLL) as turns:
                s = turns * UNROLL + PEELED
                for i in range(UNROLL):
                    fixed(s + (i + 1), (i + 1) % 2)
                    hide(s + i, i % 2)
                    gather(s + (i - 2), i % 2)
            gather(NS - 2, 0)
            gather(NS - 1, 1)


def combine_phase(nc, g, sem, scratch, lay):
    x, y, slot, wgt = g["x"], g["y"], g["slot"], g["wgt"]
    tag = f"c{lay.n}"
    rows = [scratch(f"{tag}_rows{k}", [P, NT, D]) for k in range(2)]
    got = g["got"]
    add = sem(f"{tag}_add")
    stored = sem(f"{tag}_stored")
    with nc.Block() as block:
        @block.gpsimd
        def _(pool):
            for t in range(NT):
                for k in range(2):
                    nc.gpsimd.indirect_dma_start(
                        rows[k][:, t, :], None, g["ys_dram"][lay.n],
                        bass.IndirectOffsetOnAxis(ap=slot[k][:, t:t + 1], axis=0)).then_inc(got[k][t // 2], 16)

        @block.vector
        def _(dve):
            for t in range(NT):
                nc.vector.tensor_tensor(x[:, t, :], x[:, t, :], y[:, t, :], ALU.add).then_inc(add, 1)
            n = NT
            for q in range(NT // 2):
                for k in range(2):
                    dve.wait_ge(got[k][q], 32 * (lay.n + 1))
                    for t in (2 * q, 2 * q + 1):
                        dve.wait_ge(add, t + 1 if k == 0 else n - 1)
                        nc.vector.scalar_tensor_tensor(out=x[:, t, :], in0=rows[k][:, t, :], scalar=wgt[:, k, t:t + 1],
                                                       in1=x[:, t, :], op0=ALU.mult, op1=ALU.add).then_inc(add, 1)
                        n += 1
                if lay.n == 0:
                    for t in (2 * q, 2 * q + 1):
                        dve.wait_ge(add, n - 1 + t % 2)
                        tile_stats(nc, g, "x", t)

        if lay.n == 1:
            @block.sync
            def _(sp):
                for q in range(NT // 2):
                    sp.wait_ge(add, NT + 4 * (q + 1))
                    sp.dma_start(g["out"][:, 2 * q:2 * q + 2, :], x[:, 2 * q:2 * q + 2, :]).then_inc(stored, 16)
                sp.wait_ge(stored, 16 * (NT // 2))


def cross_phase(nc, g, sem, scratch):
    con, bank, x, xn, keys = (g[k] for k in ("con", "bank", "x", "xn", "keys_dram"))
    PAIRS = XKV // 2
    W2 = XG * XR
    pT = [scratch(f"x_pT{i}", [P, TS, 2, 2 * S]) for i in range(4)]
    xq = scratch("x_xq", [P, NT * XKV * W2 // 2]).bitcast(BF16).rearrange("p (t h c) -> p t h c", t=NT, c=XR)
    high = scratch("x_high", [P, NT * D // 2]).bitcast(BF16).rearrange("p (t d) -> p t d", t=NT)
    mid = scratch("x_mid", [P, NT * D // 2]).bitcast(BF16).rearrange("p (t d) -> p t d", t=NT)
    tok = scratch("x_tok", [P, NT, CD])
    vals = scratch("x_vals", [P, PAIRS, TS, 2, 32])
    osb = [scratch(f"x_osb{i}", [P, 2 * S]) for i in range(2)]
    add = [scratch(f"x_add{i}", [P, 8 * TS, XD]) for i in range(2)]
    rinv = [scratch(f"x_rinv{i}", [P, 8 * TS]) for i in range(2)]
    nmax = [scratch(f"x_nmax{i}", [P, TS, XG]) for i in range(2)]
    rest = [scratch(f"x_rest{i}", [P, 2, TS * XG]) for i in range(2)]
    ident = scratch("x_ident", [P, P], BF16)
    xslot = scratch("x_xslot", [P, PAIRS, TS, 2 * W2], BF16)
    kslot = scratch("x_kslot", [P, XKV, S], BF16)
    qt = [scratch(f"x_qt{i}", [P, 4 * S], BF16) for i in range(2)]

    loaded = sem("x_loaded")
    split = sem("x_split")
    spread = sem("x_spread")
    blank = sem("x_blank")
    vals_ok = sem("x_vals")
    slot_in = [sem(f"x_slot_in{w}") for w in range(PAIRS)]
    t_mm = sem("x_t_mm")
    t_sb = sem("x_t_sb")
    s_mm = sem("x_s_mm")
    m_ok = sem("x_m_ok")
    n_ok = sem("x_n_ok")
    p_mm = sem("x_p_mm")
    expd = sem("x_exp")
    o_mm = sem("x_o_mm")
    o_sb = sem("x_o_sb")
    u_mm = sem("x_u_mm")
    fin = sem("x_fin")
    psS, psP, psT, psO, psU = bank[0:2], bank[2:4], bank[4], bank[5], bank[6]
    psT = psT[:].bitcast(BF16)
    UNITS = NB * XKV
    norm = Norm(nc, g, sem, "nx", "x", "ln")
    FIN = 2 + TS

    def sweep(engine, step):
        for j in range(XKV):
            step(0, j)
        with engine.Fori(1, NB) as b:
            for j in range(XKV):
                step(b, j)
        for j in range(XKV):
            step(NB, j)

    def unit(b, j, lag):
        d = j - 1 - lag
        n = b * XKV + d
        if isinstance(b, int) and not 0 <= n < UNITS:
            return None
        return n, d % XKV, b + d // XKV

    def since(n, least):
        return not isinstance(n, int) or n >= least

    with nc.Block() as block:
        @block.sync
        def _(sp):
            sp.dma_start(tok, g["ctx_tok_in"]).then_inc(loaded, 16)

            def fill(w, tiles, keys):
                sp.dma_start(xslot[:, w], xq[:, tiles, 2 * XG * w:2 * XG * (w + 1), :].rearrange("p t h c -> p t (h c)")
                             ).then_inc(slot_in[w], 16)
                sp.dma_start(kslot[:, 2 * w:2 * w + 2, :], keys).then_inc(slot_in[w], 16)

            sp.wait_ge(blank, 1)
            for b in range(2):
                sp.wait_ge(split, 4 if b == 0 else 4 * NB)
                sp.wait_ge(spread, 2 if b == 0 else 2 * NB)
                if b == 0:
                    for w in range(PAIRS):
                        fill(w, slice(0, TS), keys[0, :, 2 * w:2 * w + 2, :])
                    load_pieces(sp, g, 1)
            with sp.Fori(1, NB) as b:
                for w in range(PAIRS):
                    sp.wait_ge(p_mm, b * (4 * XKV) + 4 * (2 * w + 2 - XKV))
                    fill(w, bass.ds(b * TS, TS), keys[bass.ds(b, 1), :, 2 * w:2 * w + 2, :].rearrange("o p h t -> (o p) h t"))

        @block.gpsimd
        def _(pool):
            norm.pool(pool)
            nc.gpsimd.memset(xq[:, :, :, 6 * XD:XR].rearrange("p t h c -> p (t h) c"), 0.0).then_inc(blank, 1)
            nc.gpsimd.memset(vals, 0.0).then_inc(blank, 1)
            pool.wait_ge(blank, 2)
            nc.gpsimd.memset(vals.rearrange("p w t h c -> p (w t h) c")[:, :, XD:XD + 1], 1.0).then_inc(blank, 1)
            one = con[:, C_ONE:C_ONE + TS * XG].rearrange("p (t g) -> p t g", t=TS)

            def step(b, j):
                at = unit(b, j, 0)
                if at:
                    n, u, _ = at
                    rows = xslot[:, u // 2].rearrange("p t (h g c) -> p t h g c", h=2, g=XG)[:, :, u % 2]
                    part = [rows[:, :, :, 6 * XD + i] for i in range(3)]
                    nm, r = nmax[u % 2], [rest[u % 2][:, i].rearrange("p (t g) -> p t g", t=TS) for i in range(2)]
                    pool.wait_ge(m_ok, n * 4 + 4)
                    nc.gpsimd.tensor_tensor(part[0], nm, one, ALU.mult).then_inc(n_ok, 1)
                    pool.wait_ge(n_ok, n * 5 + 1)
                    nc.gpsimd.tensor_tensor(r[0], nm, part[0], ALU.subtract).then_inc(n_ok, 1)
                    pool.wait_ge(n_ok, n * 5 + 2)
                    nc.gpsimd.tensor_tensor(part[1], r[0], one, ALU.mult).then_inc(n_ok, 1)
                    pool.wait_ge(n_ok, n * 5 + 3)
                    nc.gpsimd.tensor_tensor(r[1], r[0], part[1], ALU.subtract).then_inc(n_ok, 1)
                    pool.wait_ge(n_ok, n * 5 + 4)
                    nc.gpsimd.tensor_tensor(part[2], r[1], one, ALU.mult).then_inc(n_ok, 1)

            sweep(pool, step)

        @block.vector
        def _(dve):
            nc.vector.tensor_copy(ident, con[:, C_ID:C_ID + P]).then_inc(vals_ok, 1)
            norm.vector(dve)
            def split_queries(b):
                tiles = slice(b * TS, (b + 1) * TS)
                xb = xn[:, tiles, :]
                dve.wait_ge(norm.steps, norm.rows(b * TS + TS - 1))
                nc.vector.tensor_copy(high[:, tiles], xb).then_inc(split, 1)
                dve.wait_ge(split, 4 * b + 1)
                nc.vector.tensor_tensor(xb, xb, high[:, tiles], ALU.subtract).then_inc(split, 1)
                dve.wait_ge(split, 4 * b + 2)
                nc.vector.tensor_copy(mid[:, tiles], xb).then_inc(split, 1)
                dve.wait_ge(split, 4 * b + 3)
                nc.vector.tensor_tensor(xq[:, tiles, :, 5 * XD:6 * XD].rearrange("p t h c -> p (t h) c"),
                                        xb.rearrange("p t (h c) -> p (t h) c", c=XD),
                                        mid[:, tiles].rearrange("p t (h c) -> p (t h) c", c=XD),
                                        ALU.subtract).then_inc(split, 1)

            split_queries(0)
            dve.wait_ge(loaded, 16)
            dve.wait_ge(blank, 3)

            def step(b, j):
                at = unit(b, j, 0)
                if at:
                    n, u, c = at
                    for q in range(4):
                        t, e = divmod(q, 2)
                        if q == 0 and since(n, 2):
                            dve.wait_ge(n_ok, n * 5 - 5)
                        dve.wait_ge(s_mm, n * 4 + q + 1)
                        nc.vector.tensor_reduce(nmax[u % 2][:, t].rearrange("p (h e) -> p h e", e=2)[:, :, e],
                                                psS[e][:].rearrange("p (h s) -> p h s", h=2),
                                                AX_X, ALU.max, negate=True).then_inc(m_ok, 1)
                    if isinstance(b, int) and b == 0 and 2 <= j < 1 + NB:
                        split_queries(j - 1)
                    if u % 2 == 0:
                        w = u // 2
                        if since(n, XKV):
                            dve.wait_ge(o_mm, c * XKV + 2 * w + 2 - XKV)
                        tiles = slice(c * TS, (c + 1) * TS) if isinstance(c, int) else bass.ds(c * TS, TS)
                        nc.vector.tensor_copy(vals[:, w, :, :, 0:XD],
                                              tok[:, tiles, 2 * XD * w:2 * XD * (w + 1)].rearrange("p t (h c) -> p t h c", h=2)
                                              ).then_inc(vals_ok, 1)
                at = unit(b, j, 8)
                if at and at[1] % 2 == 0:
                    _, u, c = at
                    w = u // 2
                    p, o = c * PAIRS + w, psU[:].rearrange("p (q c) -> p q c", c=32)
                    r = rinv[w % 2].rearrange("p (q o) -> p q o", o=1)
                    dve.wait_ge(u_mm, p + 1)
                    nc.vector.reciprocal(r, o[:, :, XD:XV]).then_inc(fin, 1)
                    dve.wait_ge(fin, p * FIN + 1)
                    nc.vector.tensor_tensor(add[w % 2], o[:, :, 0:XD], r.to_broadcast([P, 8 * TS, XD]),
                                            ALU.mult).then_inc(fin, 1)
                    dve.wait_ge(fin, p * FIN + 2)
                    for t in range(TS):
                        tile = slice(c * TS + t, c * TS + t + 1) if isinstance(c, int) else bass.ds(c * TS + t, 1)
                        xt = x[:, tile, 8 * XD * w:8 * XD * (w + 1)].rearrange("p o (k h c) -> p (o h) k c", k=2, h=2)
                        nc.vector.tensor_tensor(xt, xt, add[w % 2][:, 8 * t:8 * t + 8].rearrange("p (h k e) d -> p h k (e d)", h=2, k=2),
                                                ALU.add).then_inc(fin, 1)
                    if w == PAIRS - 1:
                        dve.wait_ge(fin, p * FIN + FIN)
                        for t in range(TS):
                            tile_stats(nc, g, "x", c * TS + t)

            sweep(dve, step)

        @block.scalar
        def _(act):
            def spread_queries(b):
                tiles = slice(b * TS, (b + 1) * TS)
                for i, (part, lo, hi) in enumerate([(high, 0, 3), (mid, 3, 5)]):
                    act.wait_ge(split, 4 * b + 1 + 2 * i)
                    src = part[:, tiles].rearrange("p t (h o c) -> p (t h) o c", o=1, c=XD)
                    nc.scalar.activation(xq[:, tiles, :, lo * XD:hi * XD].rearrange("p t h (r c) -> p (t h) r c", c=XD),
                                         src.to_broadcast([P, TS * XKV * XG, hi - lo, XD]), ACT.Copy).then_inc(spread, 1)

            spread_queries(0)

            def step(b, j):
                k = b * XKV + j - 1
                plain, shifted = unit(b, j, -1), unit(b, j, 2)
                if plain or shifted:
                    act.wait_ge(t_mm, k + 2)
                    if unit(b, j, 1):
                        act.wait_ge(s_mm, k * 4)
                    if since(k, 4):
                        act.wait_ge(p_mm, k * 4 - 12)
                    cols = slice(0 if plain else 2 * S, 4 * S if shifted else 2 * S)
                    nc.scalar.activation(qt[(j - 1) % 2][:, cols], psT[:, cols], ACT.Copy).then_inc(t_sb, 1)
                at, out = unit(b, j, 3), unit(b, j, 7)
                for q in range(4):
                    if at:
                        n, u, c = at
                        if since(n, 4) and q % 2 == 0:
                            act.wait_ge(o_mm, (c * PAIRS + u // 2) * 2 - 3 + q // 2)
                        act.wait_ge(p_mm, n * 4 + q + 1)
                        nc.scalar.activation(pT[u % 4][:, q // 2, q % 2], psP[q % 2][:], ACT.Exp,
                                             scale=float(1.0 / np.sqrt(np.float32(XD)))).then_inc(expd, 1)
                    if q == 1 and out and out[1] % 2 == 0:
                        p = out[2] * PAIRS + out[1] // 2
                        act.wait_ge(o_mm, p * 2 + 2)
                        if since(p, 1):
                            act.wait_ge(u_mm, p)
                        nc.scalar.activation(osb[out[1] // 2 % 2], psO[:], ACT.Copy).then_inc(o_sb, 1)
                if isinstance(b, int) and b == 0 and 2 <= j < 1 + NB:
                    spread_queries(j - 1)

            sweep(act, step)

        @block.tensor
        def _(pe):
            def step(b, j):
                k, par = b * XKV + j - 1, (j - 1) % 2
                plain, shifted = unit(b, j, -1), unit(b, j, 2)
                if (plain or shifted) and since(k, 0):
                    pe.wait_ge(t_sb, k + 1)
                for at, base in ((plain, 0), (shifted, 2 * S)):
                    if not at:
                        continue
                    n, u, c = at
                    if at is plain and u % 2 == 0:
                        pe.wait_ge(slot_in[u // 2], c * 32 + 32)
                    if at is shifted:
                        pe.wait_ge(n_ok, n * 5 + 5)
                    for h in range(2):
                        for t in range(TS):
                            mm = nc.tensor.transpose(psT[:, base + h * S + t * P:base + h * S + (t + 1) * P],
                                                     xslot[:, u // 2, t, u % 2 * W2 + h * P:u % 2 * W2 + (h + 1) * P], ident)
                if plain or shifted:
                    mm.then_inc(t_mm, 1)
                seen, lessmax, back = unit(b, j, 0), unit(b, j, 3), unit(b, j, 8)
                for q in range(4):
                    t, e = divmod(q, 2)
                    half = slice(64 * e, 64 * e + 64)
                    if seen:
                        n, u, _ = seen
                        if q == 0:
                            pe.wait_ge(t_sb, k + 1)
                        if q >= 2 or since(n, 1):
                            pe.wait_ge(m_ok, n * 4 + q - 1)
                        for h in range(2):
                            mm = nc.tensor.matmul(psS[e][:, h * S:(h + 1) * S],
                                                  qt[1 - par][half, h * S + t * P:h * S + (t + 1) * P],
                                                  kslot[half, u, :], start=True, stop=True)
                        mm.then_inc(s_mm, 1)
                    if lessmax:
                        n, u, _ = lessmax
                        if q == 0:
                            pe.wait_ge(t_sb, k + 1)
                        if q >= 2 or since(n, 1):
                            pe.wait_ge(expd, n * 4 + q - 1)
                        nc.tensor.matmul(psP[e][:], kslot[half, u, t * P:(t + 1) * P], qt[1 - par][half, 2 * S:4 * S],
                                         start=True, stop=True).then_inc(p_mm, 1)
                    if q == 1:
                        output(b, j)
                if back and back[1] % 2 == 0:
                    w = back[1] // 2
                    p = back[2] * PAIRS + w
                    pe.wait_ge(o_sb, p + 1)
                    if since(p, 1):
                        pe.wait_ge(fin, p * FIN)
                    for t in range(TS):
                        for h in range(2):
                            mm = nc.tensor.transpose(psU[:, (2 * t + h) * P:(2 * t + h + 1) * P],
                                                     osb[w % 2][:, h * S + t * P:h * S + (t + 1) * P], con[:, C_ID:C_ID + P])
                    mm.then_inc(u_mm, 1)

            def output(b, j):
                for m, lag in ((0, 6), (1, 7)):
                    at = unit(b, j, lag)
                    if at and at[1] % 2 == 0:
                        w = at[1] // 2
                        p = at[2] * PAIRS + w
                        pe.wait_ge(expd, p * 8 + (6, 8)[m])
                        if m == 0:
                            pe.wait_ge(vals_ok, p + 2)
                            if since(p, 1):
                                pe.wait_ge(o_sb, p)
                        for i in range(4):
                            mm = nc.tensor.matmul(psO[32 * i:32 * i + 32, :], vals[:, w, m, i // 2, :],
                                                  pT[(2 * w + i // 2) % 4][:, m, i % 2], start=(m == 0), stop=(m == TS - 1))
                        mm.then_inc(o_mm, 1)

            pe.wait_ge(vals_ok, 1)
            sweep(pe, step)


def program(nc, x_in, ctx_t, ctx_tok, ctx_rep, wqk, small, const, wa0, wa1, wm0, wm1, out):
    ctx = ExitStack()
    with ctx:
        def sb(name, shape, dt=F32):
            return ctx.enter_context(nc.sbuf_tensor(name, shape, dt))

        def sem(name):
            return ctx.enter_context(nc.semaphore(name))

        g = {
            "bank": [ctx.enter_context(nc.psum_tensor(f"bank{i}", [P, 512], F32)) for i in range(8)],
            "x": sb("x", [P, NT, D]),
            "y": sb("y", [P, NT, D]),
            "yT": sb("yT", [P, KB, NT * P]),
            "con": sb("con", [P, C_END]),
            "sm": sb("sm", [P, W_END]),
            "xn": sb("xn", [P, NT, D]),
            "zero": sb("zero", [P, D]),
            "stat": sb("stat", [P, NT, 6]),
            "mv": sb("mv", [P, NT, 2]),
            "qd": sb("qd", [P, 8, NT]),
            "slot": [sb(f"slot{k}", [P, NT], U32) for k in range(2)],
            "wgt": sb("wgt", [P, 3, NT]),
            "offs": sb("offs", [1, LAYERS[1].steps], I32),
            "x_in": x_in, "ctx_t_in": ctx_t, "ctx_tok_in": ctx_tok, "ctx_rep_in": ctx_rep, "wqk_in": wqk,
            "small_in": small, "const_in": const, "wa_in": [wa0, wa1], "wm_in": [wm0, wm1], "out": out,
            "xs_dram": [nc.dram_tensor(f"xs{n}", (NSLOT * P, D), F32, kind="Internal").ap() for n in range(2)],
            "ys_dram": [nc.dram_tensor(f"ys{n}", (NSLOT * P, D), F32, kind="Internal").ap() for n in range(2)],
            "keys_dram": nc.dram_tensor("keys", (NB, P, XKV, S), BF16, kind="Internal").ap(),
            "piece_loaded": [sem(f"piece_loaded{p}") for p in range(len(PIECES))],
            "got": [[sem(f"got{k}_{t}") for t in range(NT // 2)] for k in range(2)],
            "ring_loaded": [sem(f"ring_loaded{n}") for n in range(2)],
        }

        def phase(f, *args, give_back=False):
            with ExitStack() as own:
                sems = []

                def own_sem(name):
                    sems.append(own.enter_context(nc.semaphore(name)))
                    return sems[-1]

                f(nc, g, own_sem if give_back else sem,
                  lambda name, shape, dt=F32: own.enter_context(nc.sbuf_tensor(name, shape, dt))[:], *args)
                if give_back:
                    with nc.Block() as block:
                        @block.gpsimd
                        def _(pool):
                            for s in sems:
                                pool.sem_clear(s)

        for n, lay in enumerate(LAYERS):
            with ExitStack() as shared:
                g["stage"] = [shared.enter_context(nc.sbuf_tensor(f"stage{n}_{i}", [P, PIECE], F32)) for i in range(2)]
                if n == 0:
                    phase(graph_phase)
                else:
                    phase(cross_phase)
                phase(attention_phase, lay, give_back=(n == 0))
            with ExitStack() as shared:
                g["ring"] = shared.enter_context(nc.sbuf_tensor(f"ring{n}", [P, 2 * CHUNK_W], F32))
                phase(route_phase, lay)
                phase(expert_phase, lay)
            phase(combine_phase, lay)


def kernel(**inputs):
    import concourse.bacc as _bacc
    from concourse.bass_utils import run_bass_kernel_spmd as _run

    def tiles(a):
        return a.reshape(-1, P, a.shape[-1]).transpose(1, 0, 2)

    def blocks(w):
        return w.reshape(-1, P, w.shape[-1]).transpose(1, 0, 2).reshape(P, -1)

    def attention(n):
        return np.concatenate([blocks(inputs[f"L{n}_ffn_{k}"]) for k in ("wq", "wk", "wv", "wo")], axis=1)

    def experts(n):
        w1, w3, w2 = (inputs[f"L{n}_ffn_{k}"] for k in ("w1", "w3", "w2"))
        f = w1.shape[2]
        up = np.stack([w1, w3], axis=2).reshape(NE, KB, P, 2, f // CF, CF).transpose(4, 2, 0, 1, 3, 5)
        down = w2.reshape(NE, f // CF, CF // P, P, D).transpose(1, 3, 0, 2, 4)
        return np.concatenate([up.reshape(f // CF, P, NE, -1), down.reshape(f // CF, P, NE, -1)], axis=3).reshape(f // CF, P, CHUNK_W)

    inputs = {k: np.asarray(v) for k, v in inputs.items()}
    ctx2 = inputs["ctx_512"].reshape(NB * S, CD)
    ctx_t = ctx2.T
    rep = np.zeros((NB, P // XR, XR, XKV, S), np.float32)
    by_head = ctx_t.reshape(XKV, XD, NB, S).transpose(2, 1, 0, 3)
    rep[:, :, :len(PARTS_K) * XD] = np.tile(by_head, (1, len(PARTS_K), 1, 1))[:, None]
    rep[:, :, len(PARTS_K) * XD:len(PARTS_K) * XD + 3] = 1.0
    rep = rep.reshape(NB, P, XKV * S)
    small = np.concatenate(
        [inputs[k].reshape(KB, P).T for k in ("L0_ffn_norm1_w", "L0_ffn_norm2_w", "L1_ffn_ln1_w", "L1_ffn_ln2_w")]
        + [blocks(inputs[f"L{n}_ffn_gate_w"]) for n in range(2)]
        + [np.broadcast_to(inputs["L0_xattn_gamma_raw"].reshape(1, 1), (P, 1))], axis=1)
    data = {
        "x_in": tiles(inputs["x"].reshape(NB * S, D)), "ctx_t": ctx_t, "ctx_tok": tiles(ctx2), "ctx_rep": rep,
        "wqk": np.concatenate([inputs["L0_xattn_Wq"].T, inputs["L0_xattn_Wk"].T], axis=1), "small": small,
        "const": constants(), "wa0": attention(0), "wa1": attention(1), "wm0": experts(0), "wm1": experts(1),
    }
    nc = _bacc.Bacc("TRN2", target_bir_lowering=False, num_devices=1)
    arrays, args = {}, []
    for name, a in data.items():
        arrays[name] = np.ascontiguousarray(a)
        args.append(nc.dram_tensor(name, a.shape, F32, kind="ExternalInput").ap())
    res = nc.dram_tensor("result", (P, NT, D), F32, kind="ExternalOutput").ap()
    program(nc, *args, res)
    r = _run(nc, [arrays], core_ids=[0])
    return r.results[0]["result"].transpose(1, 0, 2).reshape(NB, S, D)
```
